# Optimizing a Trainium2 kernel written in Bass

```python
import numpy as np
import jax
import jax.numpy as jnp

def _softmax(x, axis=-1):
    return jax.nn.softmax(x, axis=axis)

def _gelu(x):
    return jax.nn.gelu(x, approximate=True)

def _silu(x):
    return jax.nn.silu(x)

def _sigmoid(x):
    return jax.nn.sigmoid(x)

def _layernorm(x, axis=-1, eps=1e-05):
    m = jnp.mean(x, axis=axis, keepdims=True)
    v = jnp.var(x, axis=axis, keepdims=True)
    return (x - m) / jnp.sqrt(v + eps)

def _scatter_add(tgt, idx, src, axis=0):
    return tgt.at[idx].add(src)

def _segment_sum(src, seg, n):
    return jax.ops.segment_sum(src, seg, n)
kernel_name = 'mk_macaron_d1_jaxref_r8_cc437e'

def setup_inputs(seed: int=0):
    np.random.seed(seed)
    _w = jnp.asarray

    def _L0_attn_setup():
        import jax, jax.numpy as jnp
        import numpy as np
        B, S, HID, NH, BS = (1, 256, 128, 16, 64)
        D = HID // NH
        THRESH = 0.01
        SCALE = D ** (-0.5)
        key = jax.random.key(seed)
        ks = jax.random.split(key, 5)
        wscale = 1.0 / np.sqrt(HID)
        x = jax.random.normal(ks[0], (B, S, HID), dtype=jnp.float32)
        wq = jax.random.normal(ks[1], (HID, HID), dtype=jnp.float32) * wscale
        wk = jax.random.normal(ks[2], (HID, HID), dtype=jnp.float32) * wscale
        wv = jax.random.normal(ks[3], (HID, HID), dtype=jnp.float32) * wscale
        wo = jax.random.normal(ks[4], (HID, HID), dtype=jnp.float32) * wscale
        return {'x': x, 'wq': wq, 'wk': wk, 'wv': wv, 'wo': wo}
    _L0_attn_in = _L0_attn_setup()

    def _L0_ffn_setup():
        import jax, jax.numpy as jnp
        import numpy as np
        TOPK = 4
        key = jax.random.key(seed)
        ks = jax.random.split(key, 9)
        B, T, D = (4, 256, 128)
        E, H = (32, 128)
        HS = H * TOPK
        s = lambda k, shape, fan: jax.random.normal(k, shape, dtype=jnp.float32) / np.sqrt(fan)
        return {'x': jax.random.normal(ks[0], (B, T, D), dtype=jnp.float32), 'router_w': s(ks[1], (E, D), D), 'router_bias': jnp.zeros((E,), dtype=jnp.float32), 'gate_w': s(ks[2], (E, H, D), D), 'up_w': s(ks[3], (E, H, D), D), 'down_w': s(ks[4], (E, D, H), H), 'sgate_w': s(ks[5], (HS, D), D), 'sup_w': s(ks[6], (HS, D), D), 'sdown_w': s(ks[7], (D, HS), HS)}
    _L0_ffn_in = _L0_ffn_setup()
    _d = {'L0_attn_x': _L0_attn_in['x'], 'L0_attn_wq': _L0_attn_in['wq'], 'L0_attn_wk': _L0_attn_in['wk'], 'L0_attn_wv': _L0_attn_in['wv'], 'L0_attn_wo': _L0_attn_in['wo'], 'L0_ffn_router_w': _L0_ffn_in['router_w'], 'L0_ffn_router_bias': _L0_ffn_in['router_bias'], 'L0_ffn_gate_w': _L0_ffn_in['gate_w'], 'L0_ffn_up_w': _L0_ffn_in['up_w'], 'L0_ffn_down_w': _L0_ffn_in['down_w'], 'L0_ffn_sgate_w': _L0_ffn_in['sgate_w'], 'L0_ffn_sup_w': _L0_ffn_in['sup_w'], 'L0_ffn_sdown_w': _L0_ffn_in['sdown_w']}
    _x0 = _d['L0_attn_x']
    _d['L0_attn_x'] = jax.random.normal(jax.random.fold_in(jax.random.key(seed), 1), (8, 512, 128), dtype=_x0.dtype)
    del _x0
    return _d

def reference(L0_attn_x, L0_attn_wq, L0_attn_wk, L0_attn_wv, L0_attn_wo, L0_ffn_router_w, L0_ffn_router_bias, L0_ffn_gate_w, L0_ffn_up_w, L0_ffn_down_w, L0_ffn_sgate_w, L0_ffn_sup_w, L0_ffn_sdown_w):

    def _L0_attn_ref(x, wq, wk, wv, wo):
        import jax, jax.numpy as jnp
        import numpy as np
        B, S, HID, NH, BS = (1, 256, 128, 16, 64)
        D = HID // NH
        THRESH = 0.01
        SCALE = D ** (-0.5)
        b, s, _ = x.shape
        nb = s // BS

        def proj(w):
            return (x @ w.T).reshape(b, s, NH, D).transpose(0, 2, 1, 3)
        q, k, v = (proj(wq), proj(wk), proj(wv))
        q_mean = q.reshape(b, NH, nb, BS, D).mean(axis=3)
        k_mean = k.reshape(b, NH, nb, BS, D).mean(axis=3)
        block_scores = jnp.einsum('bhid,bhjd->bhij', q_mean, k_mean) / np.sqrt(D)
        block_mask = block_scores > THRESH
        full_mask = jnp.broadcast_to(block_mask[:, :, :, None, :, None], (b, NH, nb, BS, nb, BS)).reshape(b, NH, s, s)
        eye = jnp.eye(s, dtype=bool)
        full_mask = full_mask | eye
        scores = jnp.einsum('bhid,bhjd->bhij', q, k) * SCALE
        scores = jnp.where(full_mask, scores, -jnp.inf)
        attn = jax.nn.softmax(scores, axis=-1)
        block_max = attn.reshape(b, NH, nb, BS, nb, BS).max(axis=(3, 5))
        smask = block_max > THRESH
        sfull = jnp.broadcast_to(smask[:, :, :, None, :, None], (b, NH, nb, BS, nb, BS)).reshape(b, NH, s, s) | eye
        attn = jnp.where(sfull, attn, 0.0)
        out = jnp.einsum('bhij,bhjd->bhid', attn, v)
        out = out.transpose(0, 2, 1, 3).reshape(b, s, NH * D)
        return out @ wo.T

    def _L0_ffn_ref(x, router_w, router_bias, gate_w, up_w, down_w, sgate_w, sup_w, sdown_w):
        import jax, jax.numpy as jnp
        import numpy as np
        TOPK = 4
        B, T, D = x.shape
        flat = x.reshape(B * T, D)
        logits = flat.astype(jnp.float32) @ router_w.T + router_bias
        scores = jax.nn.softmax(logits, axis=-1)
        topk_scores, topk_idx = jax.lax.top_k(scores, TOPK)
        topk_scores = topk_scores / jnp.clip(topk_scores.sum(axis=-1, keepdims=True), 1e-12, None)
        h = jax.nn.silu(jnp.einsum('nd,ehd->neh', flat, gate_w)) * jnp.einsum('nd,ehd->neh', flat, up_w)
        expert_out = jnp.einsum('neh,edh->ned', h, down_w)
        sel = jnp.take_along_axis(expert_out, topk_idx[:, :, None], axis=1)
        out = (sel * topk_scores.astype(flat.dtype)[:, :, None]).sum(axis=1)
        out = out + jax.nn.silu(flat @ sgate_w.T) * (flat @ sup_w.T) @ sdown_w.T
        return out.reshape(B, T, D)
    x = L0_attn_x
    x = x + 0.5 * _L0_ffn_ref(_layernorm(x, axis=-1), L0_ffn_router_w, L0_ffn_router_bias, L0_ffn_gate_w, L0_ffn_up_w, L0_ffn_down_w, L0_ffn_sgate_w, L0_ffn_sup_w, L0_ffn_sdown_w)
    x = x + _L0_attn_ref(_layernorm(x, axis=-1), L0_attn_wq, L0_attn_wk, L0_attn_wv, L0_attn_wo)
    x = x + 0.5 * _L0_ffn_ref(_layernorm(x, axis=-1), L0_ffn_router_w, L0_ffn_router_bias, L0_ffn_gate_w, L0_ffn_up_w, L0_ffn_down_w, L0_ffn_sgate_w, L0_ffn_sup_w, L0_ffn_sdown_w)
    return x

_drawn_inputs = setup_inputs


def setup_inputs(seed=0):
    import zlib

    import numpy as np

    out = dict(_drawn_inputs(seed))
    spreads = {'L0_ffn_router_bias': (0.0, 0.1)}
    factors = {}
    for name, (base, spread) in spreads.items():
        noise = np.random.default_rng([zlib.crc32(name.encode()), seed]).standard_normal(out[name].shape)
        drawn = base * np.exp(spread * noise) if base else spread * noise
        out[name] = jnp.asarray(drawn.astype(out[name].dtype))
    for name, factor in factors.items():
        out[name] = (out[name] * factor).astype(out[name].dtype)
    return out
```

```python
import concourse.bass as bass
from concourse import mybir
from contextlib import ExitStack

FP32 = mybir.dt.float32
BF16 = mybir.dt.bfloat16
U32 = mybir.dt.uint32
I32 = mybir.dt.int32
ALU = mybir.AluOpType
ACT = mybir.ActivationFunctionType
AX = mybir.AxisListType.X

P = 128
D = 128
NH, HD = 16, 8
BS = 64
SCALE = float(HD) ** -0.5
THRESH = 0.01
BIG = 1.0e30
E, K, H, HS = 32, 4, 128, 512
EPS = 1e-5
ROUND = 12582912.0


class Chain:

    def __init__(self, engine, sem):
        self.engine, self.sem, self.n, self.off = engine, sem, 0, 0

    def mark(self, ins):
        ins.then_inc(self.sem, 1)
        self.n += 1

    def link(self, ins):
        self.mark(ins)
        self.engine.wait_ge(self.sem, self.n + self.off)

    def enter(self, i, per):
        self.start, self.per, self.off = self.n, per, i * per

    def leave(self, rounds):
        assert self.n - self.start == self.per, (self.n - self.start, self.per)
        self.n, self.off = self.start + rounds * self.per, 0


class Batch:

    def __init__(self, k, i=0):
        self.k, self.i = k, i
        self.index, self.slot, self.round = k + 2 * i, k % 2, k // 2 + i

    def plus(self, d):
        return Batch(self.k + d, self.i)


def build(nc, x, wqkv, wo, rw, rb, wgu, wd, sg, su, sd, out):
    T = x.shape[0]
    NB = T // 4
    CH = 2
    CT = T // CH
    TG = CT // 4
    BLK = (CT * P * K + E * (P - 1)) // P
    BLK += -BLK % 8
    GR = BLK // 4

    ctx = ExitStack()
    with ctx:
        def sb(name, shape, dt=FP32):
            return ctx.enter_context(nc.sbuf_tensor(name, shape, dt))

        def sem(name):
            return ctx.enter_context(nc.semaphore(name))

        XS = [nc.dram_tensor(f"rows_by_expert{c}", [BLK * P, D], FP32).ap() for c in range(CH)]
        YS = [nc.dram_tensor(f"results_by_expert{c}", [BLK * P, D], FP32).ap() for c in range(CH)]
        qk_parts = [nc.dram_tensor(f"qk_parts{s}", [6, NH * HD, 512], BF16).ap() for s in range(2)]
        mask_rows = [nc.dram_tensor(f"mask_rows{s}", [NH * 8, 512], BF16).ap() for s in range(2)]
        max_rows = [nc.dram_tensor(f"max_rows{s}", [3 * NH, 512], BF16).ap() for s in range(2)]

        X = sb("X", [P, T, D])
        wqkv_s = sb("wqkv_s", [P, 3 * D])
        wo_s = sb("wo_s", [P, D])
        rw_s = sb("rw_s", [P, E])
        rb_s = sb("rb_s", [P, E])
        wgu_s = sb("wgu_s", [P, E * 2 * H])
        wd_s = sb("wd_s", [P, E * D])
        sg_s = sb("sg_s", [P, HS])
        su_s = sb("su_s", [P, HS])
        sd_s = sb("sd_s", [P, 4, D])
        identf = sb("identf", [P, P])
        identb = sb("identb", [P, P], BF16)
        tri = sb("tri", [P, P], BF16)
        ones_b = sb("ones_b", [P, 512], BF16)
        iota_e = sb("iota_e", [P, E])
        iota_p = sb("iota_p", [P, 1])
        block_diag = sb("block_diag", [P, NH, 8])
        diag_sel = sb("diag_sel", [P, 4, 8])
        diag_bias = sb("diag_bias", [P, 4, 8])
        key_block = sb("key_block", [8, 512], BF16)
        eps_c = sb("eps_c", [P, 1])
        half_sel = sb("half_sel", [P, 2])
        ones_f = sb("ones_f", [P, 4 * NH])
        reset_e = sb("reset_e", [P, E * 16])

        arena_g = sb("arena_g", [P, CT * K * D])
        arena_n = sb("arena_n", [P, T * D])
        arena_o = sb("arena_o", [P, 2 * NH * 4 * 72])
        G = arena_g[:, :].rearrange("p (t k d) -> p t k d", t=CT, k=K)
        stacks = wgu_s[:, :].bitcast(BF16)
        QS = [stacks[:, 4096 * s:4096 * (s + 1)] for s in range(2)]
        KS = [stacks[:, 8192 + 4096 * s:8192 + 4096 * (s + 1)] for s in range(2)]
        PT = [wd_s[:, 2048 * s:2048 * (s + 1)] for s in range(2)]
        XNT = arena_n
        XN = arena_o[:, 0:T * D].rearrange("p (t d) -> p t d", t=T)
        O = [arena_o[:, 4608 * s:4608 * (s + 1)].rearrange("p (h i j c) -> p h i j c", h=NH, i=4, j=8)
             for s in range(2)]
        zero_t = XNT[:, 0:2048]

        class Carve:

            def __init__(self, arena, at):
                self.arena, self.at = arena, at

            def take(self, words, dt=FP32):
                piece = self.arena[:, self.at:self.at + words]
                self.at += words
                assert self.at <= self.arena.shape[1]
                return piece if dt == FP32 else piece.bitcast(dt)

        beside_xn = Carve(arena_o, T * D)
        in_g = Carve(arena_g, 0)
        in_n = Carve(arena_n, 0)

        stats = sb("stats", [P, CT, 6])
        mv = sb("mv", [P, CT, 2])
        rstd = sb("rstd", [P, CT])
        arena_r = sb("arena_r", [P, 5 * 512])
        L = arena_r[:, 0:512].rearrange("p (t e) -> p t e", t=CT)
        EX = arena_r[:, 512:1024].rearrange("p (t e) -> p t e", t=CT)
        tot = arena_r[:, 1024:1536]
        scan = arena_r[:, 1536:2048]
        place = arena_r[:, 2048:2560]
        OH = beside_xn.take(K * E * CT // 2, BF16).rearrange("p (k e t) -> p k e t", k=K, e=E)
        OHP = sb("OHP", [P, K, E, CT])
        top8 = sb("top8", [P, CT, 8])
        idx8 = sb("idx8", [P, CT, 8], U32)
        idxf = sb("idxf", [P, CT, 8])
        topw = sb("topw", [P, CT, K])
        zsum = sb("zsum", [P, CT])
        wsum = sb("wsum", [P, CT])
        GW = [sb(f"GW{c}", [P, CT, K]) for c in range(CH)]
        posf = sb("posf", [P, K, CT])
        pos = [sb(f"pos{c}", [P, K, CT], U32) for c in range(CH)]
        nblk = sb("nblk", [P, E])
        cumb = sb("cumb", [P, E])
        begin = sb("begin", [P, E])
        cmpb = sb("cmpb", [P, E])
        eblk = sb("eblk", [P, 1])
        ids = [sb(f"ids{c}", [1, P], I32) for c in range(CH)]
        XG = [sb("XG0", [P, 512])[:, :], beside_xn.take(512)]
        XG = [g.rearrange("p (b d) -> p b d", b=4) for g in XG]
        XT = [sb("XT0", [P, 512]), beside_xn.take(512)]
        SG = [sb("SG0", [P, 512]), beside_xn.take(512)]
        HG = [sb("HG0", [P, 512])[:, :], beside_xn.take(512)]
        HG = [g.rearrange("p (b d) -> p b d", b=4) for g in HG]
        HT = [sb(f"HT{s}", [P, 512]) for s in range(2)]
        YG = [sb(f"YG{s}", [P, 4, D]) for s in range(2)]
        SHT = [OHP[:, :, :, :].rearrange("p k e t -> p (k e t)"), beside_xn.take(2048)]
        SHT = [h.rearrange("p (j n) -> p j n", j=4) for h in SHT]

        xa = XG[0]
        xaT = XT[0]
        qk_hi, qk_mid, qk_lo = ([in_g.take(256, BF16) for n in range(2)] for _ in range(3))
        rest = [HT[0], HT[1]]
        bsum = sb("bsum", [P, 2, 8])
        kmd = in_g.take(128).rearrange("p (h j) -> p h j", h=NH)
        mbt = in_g.take(256, BF16)
        NAT = in_g.take(4 * 384).rearrange("p (i a h d) -> p i a h d", i=4, a=3, h=NH)
        prod = HG[0][:, :, :].rearrange("p a (h d) -> p a h d", h=NH)
        MN, MX, AL = ([in_n.take(512).rearrange("p (i h j) -> p i h j", i=4, h=NH) for s in range(2)] for _ in range(3))
        tmp = in_n.take(512).rearrange("p (i h j) -> p i h j", i=4, h=NH)
        sdiag = [sb(f"sdiag{s}", [P, 4, NH]) for s in range(2)]
        ediag = [sb(f"ediag{s}", [P, 4, NH]) for s in range(2)]
        adiag = [sb(f"adiag{s}", [P, 4, NH]) for s in range(2)]
        mrow = sb("mrow", [P, 4, NH])
        mres = sb("mres", [P, 4, NH])
        mparts = sb("mparts", [P, 4, 3, NH], BF16)
        mrows = sb("mrows", [3 * NH, 512], BF16)
        lsum = sb("lsum", [P, 4, NH])
        rinv = sb("rinv", [P, 4, NH])
        dcor = sb("dcor", [P, 4, NH])
        bmax = sb("bmax", [P, 8])
        keepx = in_g.take(256, BF16)
        KR = YG[0][:, :, :].rearrange("p i (h j) -> p i h j", h=NH)
        AO = YG[1][:, :, :].rearrange("p i (h d) -> p i h d", h=NH)
        AOT = SG[0]
        VA = [in_g.take(4 * NH * 18).rearrange("p (i h c) -> p i h c", i=4, h=NH) for s in range(2)]

        banks = ctx.enter_context(nc.psum_tensor("banks", [P, 8, 512], FP32))

        def bank(n):
            return banks[:, n, :]

        s_x = [sem(f"s_x{c}") for c in range(CH)]
        s_w = sem("s_w")
        s_we = sem("s_we")
        s_zero = sem("s_zero")
        s_cst = sem("s_cst")
        s_zt = sem("s_zt")
        dch = sem("dve_chain")
        ach = sem("act_chain")
        pch = sem("pool_chain")
        f_stat = sem("f_stat")
        f_sqrt = sem("f_sqrt")
        f_xn = sem("f_xn")
        f_tx = sem("f_tx")
        f_xnt = sem("f_xnt")
        f_log = sem("f_log")
        f_lm = sem("f_lm")
        f_ex = sem("f_ex")
        f_oh = sem("f_oh")
        f_cnt = sem("f_cnt")
        f_eb = sem("f_eb")
        f_ebt = sem("f_ebt")
        f_ids = sem("f_ids")
        f_pos = sem("f_pos")
        h_g = sem("h_g")
        h_s = sem("h_s")
        h_m = sem("h_m")
        h_y = sem("h_y")
        h_x = sem("h_x")
        e_scat = [sem(f"e_scat{c}") for c in range(CH)]
        e_xg = [sem(f"e_xg{s}") for s in range(2)]
        e_tx = sem("e_tx")
        e_xt = sem("e_xt")
        e_gu = sem("e_gu")
        e_s = sem("e_s")
        e_h = sem("e_h")
        e_th = sem("e_th")
        e_ht = sem("e_ht")
        e_y = sem("e_y")
        e_yc = sem("e_yc")
        e_st = [sem(f"e_st{s}") for s in range(2)]
        e_gat = [sem(f"e_gat{c}") for c in range(CH)]
        e_comb = sem("e_comb")
        a_va = sem("a_va")
        a_cdma = sem("a_cdma")
        a_stat = sem("a_stat")
        a_sqrt = sem("a_sqrt")
        a_xa = sem("a_xa")
        a_tx = sem("a_tx")
        a_xt = sem("a_xt")
        a_qk = sem("a_qk")
        a_hi = sem("a_hi")
        a_rest = sem("a_rest")
        a_sum = sem("a_sum")
        a_parts = sem("a_parts")
        a_nat = sem("a_nat")
        a_natc = sem("a_natc")
        a_sd = sem("a_sd")
        a_kmd = sem("a_kmd")
        a_mb = sem("a_mb")
        a_mbt = sem("a_mbt")
        a_mn = sem("a_mn")
        a_mnc = sem("a_mnc")
        a_dw = sem("a_dw")
        a_stk = [sem(f"a_stk{s}") for s in range(2)]
        a_a = sem("a_a")
        a_ar = sem("a_ar")
        a_mp = sem("a_mp")
        a_mt = sem("a_mt")
        a_mtc = sem("a_mtc")
        a_pd = sem("a_pd")
        a_pe = sem("a_pe")
        a_mw = sem("a_mw")
        a_mr = [sem(f"a_mr{s}") for s in range(2)]
        a_s = sem("a_s")
        a_e = sem("a_e")
        a_pv = sem("a_pv")
        a_oc = sem("a_oc")
        t_pm = sem("t_pm")
        t_pt = sem("t_pt")
        t_kx = sem("t_kx")
        t_kn = sem("t_kn")
        t_kr = sem("t_kr")
        t_w = sem("t_w")
        t_ao = sem("t_ao")
        t_at = sem("t_at")
        t_atc = sem("t_atc")
        t_op = sem("t_op")
        t_x = sem("t_x")
        s_out = sem("s_out")

        NW = 9
        NCST = 0
        STK = 26 * 16
        AH = 4
        LAST = 2

        def steps():
            yield None, 0, [(-2, "P"), (-1, "AP"), (0, "BAP")]
            yield 2, 1, [(1, "TBAP"), (2, "TBAP")]
            yield None, 0, [(5, "TBAP"), (6, "TBA"), (7, "TB"), (8, "T")]

        block = ctx.enter_context(nc.Block())

        @block.sync
        def _(sp):
            for c in range(CH):
                sp.dma_start(X[:, c * CT:(c + 1) * CT, :], x[c * CT:(c + 1) * CT].rearrange("t p d -> p t d")).then_inc(s_x[c], 16)
            for dst, src in ((rw_s, rw), (rb_s, rb.rearrange("(a e) -> a e", a=1).to_broadcast([P, E])),
                             (sg_s, sg), (su_s, su), (wqkv_s, wqkv), (wo_s, wo)):
                sp.dma_start(dst[:, :], src).then_inc(s_w, 16)
            sp.dma_start(sd_s[:, :, :], sd).then_inc(s_w, 16)
            sp.dma_start(wgu_s[:, :], wgu).then_inc(s_we, 16)
            sp.dma_start(wd_s[:, :], wd).then_inc(s_we, 16)
            sp.wait_ge(s_zt, 1)
            for c in range(CH):
                for n in range(BLK // 16):
                    sp.dma_start(XS[c][n * 16 * P:(n + 1) * 16 * P, :].rearrange("(b p) d -> p b d", p=P),
                                 zero_t.rearrange("p (b d) -> p b d", d=D)).then_inc(s_zero, 16)

            def load_group(c, q, g, s):
                src = XS[c][bass.ds(g * 512, 512), :].rearrange("(b p) d -> p b d", p=P)
                sp.dma_start(XG[s][:, :, :], src).then_inc(e_xg[s], 16)

            def store_group(c, q, g, s):
                sp.wait_ge(e_yc, q * GR + g + 1)
                dst = YS[c][bass.ds(g * 512, 512), :].rearrange("(b p) d -> p b d", p=P)
                sp.dma_start(dst, YG[s][:, :, :]).then_inc(e_st[s], 16)

            def ffn(f):
                for c in range(CH):
                    q = CH * f + c
                    sp.wait_ge(e_scat[c], (f + 1) * CT * K * 16)
                    for s in range(2):
                        if q:
                            sp.wait_ge(e_tx, q * GR)
                        load_group(c, q, s, s)
                    with sp.Fori(0, GR // 2 - 1) as i:
                        for s in range(2):
                            sp.wait_ge(e_tx, q * GR + 2 * i + s + 1)
                            load_group(c, q, 2 * i + s + 2, s)
                        for s in range(2):
                            store_group(c, q, 2 * i + s, s)
                    for s in range(2):
                        store_group(c, q, GR - 2 + s, s)

            ffn(0)

            sp.wait_ge(e_yc, CH * GR)
            for s in range(2):
                for par in range(2):
                    dst = KS[s][64 * par + 48:64 * par + 56, :].rearrange("p (a n) -> p a n", n=512)
                    for a in range(8):
                        sp.dma_start(dst[:, a, :], key_block[:, :]).then_inc(a_cdma, 16)
                    dst = KS[s][64 * par + 56:64 * par + 59, :].rearrange("p (a n) -> p a n", n=512)
                    for a in range(8):
                        sp.dma_start(dst[:, a, :], ones_b[0:3, :]).then_inc(a_cdma, 16)

            def step(b, what):
                c, a = b.plus(2), b.plus(1)
                if "A" in what:
                    sp.wait_ge(a_mtc, a.index + 1)
                    sp.dma_start(max_rows[a.slot], mrows[:, :]).then_inc(a_mw, 16)
                    sp.wait_ge(a_mw, 16 * (a.index + 1))
                    for par in range(2):
                        src = max_rows[a.slot].rearrange("(m h) n -> m h n", m=3)[:, par::2, :]
                        dst = QS[a.slot][64 * par + 56:64 * par + 59, :].rearrange("p (a n) -> p a n", n=512)
                        sp.dma_start(dst, src).then_inc(a_mr[a.slot], 16)
                if "P" in what:
                    sp.wait_ge(a_parts, 2 * (c.index + 1))
                    for n in range(2):
                        for m, part in enumerate((qk_hi[n], qk_mid[n], qk_lo[n])):
                            sp.dma_start(qk_parts[c.slot][3 * n + m], part[:, :]).then_inc(a_dw, 16)
                    sp.wait_ge(a_mbt, c.index + 1)
                    sp.dma_start(mask_rows[c.slot], mbt[:, :]).then_inc(a_dw, 16)
                    sp.wait_ge(a_dw, 7 * 16 * (c.index + 1))
                    if "B" in what:
                        sp.wait_ge(a_pv, NH * (b.index + 1))
                    for n, (stack, terms) in enumerate(((QS, (0, 0, 0, 1, 1, 2)), (KS, (0, 1, 2, 0, 1, 0)))):
                        for par in range(2):
                            for row, m in enumerate(terms):
                                src = qk_parts[c.slot][3 * n + m].rearrange("(h d) n -> d h n", d=HD)[:, par::2, :]
                                p0 = 64 * par + HD * row
                                dst = stack[c.slot][p0:p0 + HD, :].rearrange("p (a n) -> p a n", n=512)
                                sp.dma_start(dst, src).then_inc(a_stk[c.slot], 16)
                    for par in range(2):
                        src = mask_rows[c.slot].rearrange("(h j) n -> j h n", j=8)[:, par::2, :]
                        dst = QS[c.slot][64 * par + 48:64 * par + 56, :].rearrange("p (a n) -> p a n", n=512)
                        sp.dma_start(dst, src).then_inc(a_stk[c.slot], 16)

            for rounds, _, part in steps():
                if rounds is None:
                    for k, what in part:
                        step(Batch(k), what)
                else:
                    with sp.Fori(0, rounds) as i:
                        for k, what in part:
                            step(Batch(k, i), what)

            sp.wait_ge(a_pv, NH * NB)
            sp.dma_start(wgu_s[:, :], wgu).then_inc(s_we, 16)
            sp.dma_start(wd_s[:, :], wd).then_inc(s_we, 16)
            ffn(1)
            for c in range(CH):
                sp.wait_ge(e_comb, (CH + c + 1) * CT)
                sp.dma_start(out[c * CT:(c + 1) * CT].rearrange("t p d -> p t d"),
                             X[:, c * CT:(c + 1) * CT, :]).then_inc(s_out, 16)
            sp.wait_ge(s_out, 16 * CH)

        @block.gpsimd
        def _(pool):
            ch = Chain(pool, pch)
            g = nc.gpsimd
            g.memset(zero_t, 0.0).then_inc(s_zt, 1)
            g.memset(eps_c[:, :], EPS)
            g.memset(ones_b[:, :], 1.0)
            g.memset(ones_f[:, :], 1.0)
            g.memset(identf[:, :], 0.0)
            g.memset(identb[:, :], 0.0)
            g.memset(block_diag[:, :, :], 0.0)
            g.memset(diag_sel[:, :, :], 0.0)
            g.memset(reset_e[:, :], 1.0)
            ch.link(g.iota(iota_e[:, :], pattern=[[1, E]], base=0, channel_multiplier=0,
                           allow_small_or_imprecise_dtypes=True))
            g.iota(iota_p[:, :], pattern=[[0, 1]], base=0, channel_multiplier=1, allow_small_or_imprecise_dtypes=True)
            for half, op in enumerate((ALU.is_gt, ALU.is_ge)):
                sign = 1 if half else -1
                g.affine_select(out=half_sel[:, half:half + 1], in_=ones_f[:, 0:1], compare_op=op, fill=0.0,
                                base=-64 * sign, pattern=[[0, 1]], channel_multiplier=sign)
            for m in (identf, identb):
                g.affine_select(out=m[:, :], in_=m[:, :], compare_op=ALU.not_equal, fill=1.0, base=0,
                                pattern=[[-1, P]], channel_multiplier=1)
            g.affine_select(out=tri[:, :], in_=ones_b[:, 0:P], compare_op=ALU.is_gt, fill=0.0, base=0,
                            pattern=[[1, P]], channel_multiplier=-1)
            v = reset_e[:, :].rearrange("p (e t) -> p e t", e=E)
            g.affine_select(out=v, in_=v, compare_op=ALU.not_equal, fill=0.0, base=0,
                            pattern=[[0, E], [1, 16]], channel_multiplier=0)
            ch.link(g.affine_select(out=key_block[:, :], in_=ones_b[0:8, :], compare_op=ALU.is_ge, fill=0.0,
                                    base=0, pattern=[[1, 512]], channel_multiplier=-BS))
            g.memset(block_diag[:, :, :], 1.0).then_inc(pch, 1)
            ch.n += 1
            pool.wait_ge(pch, ch.n)
            ch.link(g.affine_select(out=block_diag[:, :, :], in_=block_diag[:, :, :], compare_op=ALU.is_ge,
                                    fill=0.0, base=0, pattern=[[-HD, NH], [0, 8]], channel_multiplier=1))
            ch.link(g.affine_select(out=block_diag[:, :, :], in_=block_diag[:, :, :], compare_op=ALU.is_ge,
                                    fill=0.0, base=HD - 1, pattern=[[HD, NH], [0, 8]], channel_multiplier=-1))
            ch.link(g.affine_select(out=key_block[:, :], in_=key_block[:, :], compare_op=ALU.is_ge, fill=0.0,
                                    base=BS - 1, pattern=[[-1, 512]], channel_multiplier=BS))
            for half in range(2):
                part = diag_sel[64 * half:64 * half + 64, :, :]
                ch.link(g.affine_select(out=part, in_=part, compare_op=ALU.not_equal, fill=1.0, base=-half,
                                        pattern=[[-2, 4], [1, 8]], channel_multiplier=0))
            g.tensor_scalar(diag_bias[:, :, :], diag_sel[:, :, :], -1.0, BIG, ALU.add, ALU.mult).then_inc(s_cst, 1)

            def scatter(f, c):
                q = CH * f + c
                pool.wait_ge(f_pos, q + 1)
                if f == 0 and c == 0:
                    pool.wait_ge(s_zero, 16 * CH * (BLK // 16))
                if f:
                    pool.wait_ge(e_tx, CH * GR)
                for t in range(CT):
                    for k in range(K):
                        pool.indirect_dma_start(
                            XS[c], bass.IndirectOffsetOnAxis(ap=pos[c][:, k, t:t + 1], axis=0),
                            XN[:, c * CT + t, :], None).then_inc(e_scat[c], 16)

            def gather(f, c):
                q = CH * f + c
                for s in range(2):
                    pool.wait_ge(e_st[s], 16 * (q + 1) * (GR // 2))
                if q:
                    pool.wait_ge(e_comb, q * CT)
                for t in range(CT):
                    for k in range(K):
                        pool.indirect_dma_start(
                            G[:, t, k, :], None, YS[c],
                            bass.IndirectOffsetOnAxis(ap=pos[c][:, k, t:t + 1], axis=0)).then_inc(e_gat[c], 16)

            for c in range(CH):
                scatter(0, c)
            for c in range(CH):
                gather(0, c)

            pool.wait_ge(e_comb, CH * CT)
            for s in range(2):
                for half in range(2):
                    o = VA[s][:, :, :, 9 * half + 8:9 * half + 9].rearrange("p i h c -> p (i h) c")
                    last = g.tensor_scalar(o, ones_f[:, 0:4 * NH].unsqueeze(2), half_sel[:, half:half + 1], None, ALU.mult)
            ch.link(last)

            def values(b):
                pool.wait_ge(a_natc, 4 * (b.index + 1))
                pool.nop(nofuse=True)
                for i in range(4):
                    for half in range(2):
                        last = g.tensor_scalar(VA[b.slot][:, i, :, 9 * half:9 * half + 8], NAT[:, i, 2, :, :],
                                               half_sel[:, half:half + 1], None, ALU.mult)
                last.then_inc(a_va, 1)

            def parts(c):
                for n in range(2):
                    pool.wait_ge(a_rest, 2 * c.index + n + 1)
                    if n == 0 and (c.k >= 1):
                        pool.wait_ge(a_dw, 7 * 16 * c.index)
                    pool.nop(nofuse=True)
                    ch.link(g.tensor_copy(qk_mid[n][:, :], rest[n][:, :]))
                    g.tensor_tensor(qk_lo[n][:, :], rest[n][:, :], qk_mid[n][:, :], ALU.subtract).then_inc(a_parts, 1)

            def step(b, what):
                a, c, t = b.plus(1), b.plus(2), b.plus(-1)
                if "T" in what:
                    pool.wait_ge(t_kr, t.index + 1)
                    for i in range(4):
                        o = O[t.slot][:, :, i, :, 0:8]
                        kr = KR[:, i, :, :].unsqueeze(3).to_broadcast([P, NH, 8, HD])
                        g.tensor_tensor(o, o, kr, ALU.mult).then_inc(t_w, 1)
                if "A" in what:
                    if "T" in what:
                        pool.wait_ge(t_ao, t.index + 1)
                    values(a)
                if "P" in what:
                    parts(c)

            per = 2 * 2
            for rounds, _, part in steps():
                if rounds is None:
                    for k, what in part:
                        step(Batch(k), what)
                else:
                    with pool.Fori(0, rounds) as i:
                        ch.enter(i, per)
                        for k, what in part:
                            step(Batch(k, i), what)
                        ch.leave(rounds)

            for c in range(CH):
                scatter(1, c)
            for c in range(CH):
                gather(1, c)

        @block.scalar
        def _(act):
            ch = Chain(act, ach)

            def copy(dst, src):
                return nc.scalar.activation(dst, src, ACT.Copy)

            def route(f, c):
                q = CH * f + c
                act.wait_ge(f_stat, q + 1)
                if q == 0:
                    act.wait_ge(s_cst, 1)
                nc.scalar.activation(rstd[:, :], mv[:, :, 1], ACT.Sqrt, bias=eps_c[:, :]).then_inc(f_sqrt, 1)
                for n in range(TG):
                    act.wait_ge(f_tx, q * TG + n + 1)
                    copy(XNT[:, (c * TG + n) * 512:(c * TG + n + 1) * 512], bank(4 + n % 2)).then_inc(f_xnt, 1)
                act.wait_ge(f_lm, q + 1)
                nc.scalar.activation(EX, L, ACT.Exp).then_inc(f_ex, 1)

            def shared(f):
                for g in range(CH * TG):
                    for j in range(4):
                        n = 4 * (CH * TG * f + g) + j
                        act.wait_ge(h_g, n + 1)
                        if n >= 2:
                            act.wait_ge(h_m, n - 1)
                        nc.scalar.activation(SG[j % 2][:, :], bank(j % 2), ACT.Silu).then_inc(h_s, 1)

            def experts(f, c):
                q = CH * f + c

                def xt(g, s):
                    act.wait_ge(e_tx, q * GR + g + 1)
                    copy(XT[s][:, :], bank(4)).then_inc(e_xt, 1)

                def silu(g, s):
                    act.wait_ge(e_gu, q * GR + g + 1)
                    v = banks[:, 2 * s:2 * s + 2, :].rearrange("p a (b c) -> p (a b) c", c=256)
                    o = SG[s][:, :].rearrange("p (b c) -> p b c", b=4)
                    nc.scalar.activation(o, v[:, :, 0:128], ACT.Silu).then_inc(e_s, 1)

                def y(g, s):
                    act.wait_ge(e_y, q * GR + g + 1)
                    yg = YG[s][:, :, :].rearrange("p b d -> p (b d)")
                    copy(yg, bank(6 + s)).then_inc(e_yc, 1)

                def pair(i):
                    silu(2 * i, 0)
                    silu(2 * i + 1, 1)
                    xt(2 * i + 2, 0)
                    xt(2 * i + 3, 1)
                    for s in range(2):
                        if q or not (isinstance(i, int) and i == 0):
                            act.wait_ge(e_st[s], 16 * (q * (GR // 2) + i))
                        y(2 * i + s, s)

                xt(0, 0)
                xt(1, 1)
                pair(0)
                with act.Fori(1, GR // 2 - 1) as i:
                    pair(i)
                silu(GR - 2, 0)
                silu(GR - 1, 1)
                for s in range(2):
                    act.wait_ge(e_st[s], 16 * ((q + 1) * (GR // 2) - 1))
                    y(GR - 2 + s, s)

            def tail_copy(t):
                act.wait_ge(t_at, t.index + 1)
                copy(AOT[:, :], bank(6)).then_inc(t_atc, 1)

            def probs(b, h, n):
                for j in range(AH):
                    act.wait_ge(a_s, AH * (n + h) + j + 1)
                    if j == 0 and (h >= 2 or b.k >= 1):
                        act.wait_ge(a_pv, n + h - 1)
                    nc.scalar.activation(PT[h % 2][:, 512 * j:512 * (j + 1)], bank(2 + (AH * h + j) % 3),
                                         ACT.Exp, scale=SCALE).then_inc(a_e, 1)

            def take_o(b, h, n):
                act.wait_ge(a_pv, n + h + 1)
                o = O[b.slot][:, h, :, :, :].rearrange("p i j c -> p (i j c)")
                copy(o, bank(5)[:, 0:288]).then_inc(a_oc, 1)

            def step(b, what):
                a, c, t = b.plus(1), b.plus(2), b.plus(-1)
                n = NH * b.index
                for h in range(NH + 1):
                    if "B" in what:
                        if h < NH:
                            probs(b, h, n)
                        if h > 0:
                            if h == 1 and "T" in what:
                                pass
                            take_o(b, h - 1, n)
                    if h == 9 and "T" in what:
                        tail_copy(t)
                    if h == 13 and "A" in what:
                        act.wait_ge(a_mt, a.index + 1)
                        nc.scalar.activation(mrows[:, :], bank(6).bitcast(BF16)[0:3 * NH, 0:512], ACT.Copy).then_inc(a_mtc, 1)
                        act.wait_ge(a_pd, a.index + 1)
                        mx = MX[a.slot].rearrange("p i h j -> p (i h j)")
                        nc.scalar.activation(mx, mx, ACT.Exp, scale=SCALE)
                        e = ediag[a.slot][:, :, :]
                        nc.scalar.activation(e, e, ACT.Exp, scale=SCALE).then_inc(a_pe, 1)
                    if h == 14 and "P" in what:
                        act.wait_ge(a_stat, c.index + 1)
                        nc.scalar.activation(rstd[:, 0:4], mv[:, 0:4, 1], ACT.Sqrt, bias=eps_c[:, :]).then_inc(a_sqrt, 1)
                        act.wait_ge(a_tx, c.index + 1)
                        copy(xaT[:, :], bank(7)).then_inc(a_xt, 1)
                        for m in range(2):
                            act.wait_ge(a_qk, 2 * c.index + m + 1)
                            if m == 0 and c.k >= 1:
                                act.wait_ge(a_dw, 7 * 16 * c.index)
                            copy(qk_hi[m][:, :], bank(6 + m)).then_inc(a_hi, 1)
                        for i in range(4):
                            act.wait_ge(a_nat, 4 * c.index + i + 1)
                            if i == 0 and c.k >= 1:
                                act.wait_ge(a_va, c.index)
                            nat = NAT[:, i, :, :, :].rearrange("p a h d -> p (a h d)")
                            copy(nat, bank(6 + i % 2)[:, 0:384]).then_inc(a_natc, 1)
                        act.wait_ge(a_mn, c.index + 1)
                        mn = MN[c.slot].rearrange("p i h j -> p (i h j)")
                        copy(mn, bank(7)).then_inc(a_mnc, 1)

            route(0, 0)
            route(0, 1)
            shared(0)
            experts(0, 0)
            experts(0, 1)
            for rounds, _, part in steps():
                if rounds is None:
                    for k, what in part:
                        step(Batch(k), what)
                else:
                    with act.Fori(0, rounds) as i:
                        for k, what in part:
                            step(Batch(k, i), what)
            route(1, 0)
            route(1, 1)
            shared(1)
            experts(1, 0)
            experts(1, 1)

        @block.vector
        def _(dve):
            v = nc.vector
            ch = Chain(dve, dch)

            def route(f, c):
                q = CH * f + c
                if f == 0:
                    dve.wait_ge(s_x[c], 16)
                    if c == 0:
                        dve.wait_ge(s_cst, 1)
                        dve.wait_ge(s_w, 7 * 16)
                for t in range(CT):
                    last = v.bn_stats(stats[:, t, :], X[:, c * CT + t, :])
                ch.link(last)
                for t in range(CT):
                    last = v.bn_aggr(mv[:, t, :], stats[:, t, :])
                last.then_inc(f_stat, 1)
                dve.wait_ge(f_sqrt, q + 1)
                if q == 0:
                    dve.wait_ge(s_zero, 16 * CH * (BLK // 16))
                ch.link(v.reciprocal(rstd[:, :], rstd[:, :]))
                for n in range(TG):
                    for t in range(4 * n, 4 * n + 4):
                        last = v.tensor_scalar(XN[:, c * CT + t, :], X[:, c * CT + t, :], mv[:, t, 0:1],
                                               rstd[:, t:t + 1], ALU.subtract, ALU.mult)
                    last.then_inc(f_xn, 1)
                dve.wait_ge(f_log, q + 1)
                ch.link(v.tensor_tensor(L, bank(6).rearrange("p (t e) -> p t e", t=CT),
                                        rb_s[:, :].unsqueeze(1).to_broadcast([P, CT, E]), ALU.add))
                for t in range(CT):
                    last = v.max(top8[:, t, :], L[:, t, :])
                ch.link(last)
                for t in range(CT):
                    last = v.max_index(idx8[:, t, :], top8[:, t, :], L[:, t, :])
                ch.link(last)
                ch.link(v.tensor_copy(idxf[:, :, :], idx8[:, :, :]))
                v.tensor_tensor(L, L, top8[:, :, 0:1].to_broadcast([P, CT, E]), ALU.subtract).then_inc(f_lm, 1)
                v.tensor_tensor(OH[:, :, :, :],
                                iota_e[:, :].unsqueeze(1).unsqueeze(3).to_broadcast([P, K, E, CT]),
                                idxf[:, :, 0:K].rearrange("p t k -> p k t").unsqueeze(2).to_broadcast([P, K, E, CT]),
                                ALU.is_equal).then_inc(f_oh, 1)
                dve.wait_ge(f_ex, q + 1)
                v.tensor_tensor(topw[:, :, :], top8[:, :, 0:K], top8[:, :, 0:1].to_broadcast([P, CT, K]), ALU.subtract)
                ch.link(v.tensor_reduce(zsum[:, :], EX, AX, ALU.add))
                dve.wait_ge(f_oh, q + 1)
                ch.link(v.reciprocal(zsum[:, :], zsum[:, :]))
                ch.link(v.tensor_tensor(EX, EX, zsum[:, :].unsqueeze(2).to_broadcast([P, CT, E]), ALU.mult))
                for k in range(K):
                    last = v.tensor_tensor(OHP[:, k, :, :], OH[:, k, :, :], EX.rearrange("p t e -> p e t"), ALU.mult)
                ch.link(last)
                ch.link(v.tensor_reduce(topw[:, :, :].rearrange("p t k -> p k t"),
                                        OHP[:, :, :, :].rearrange("p k e t -> p k t e"), AX, ALU.add))
                ch.link(v.tensor_reduce(wsum[:, :], topw[:, :, :], AX, ALU.add))
                ch.link(v.tensor_scalar_max(wsum[:, :], wsum[:, :], 1e-12))
                ch.link(v.reciprocal(wsum[:, :], wsum[:, :]))
                ch.link(v.tensor_tensor(topw[:, :, :], topw[:, :, :],
                                        wsum[:, :].unsqueeze(2).to_broadcast([P, CT, K]), ALU.mult))
                if f:
                    pass
                ch.link(v.tensor_scalar(GW[c][:, :, :], topw[:, :, :], 0.5, None, ALU.mult))
                dve.wait_ge(f_cnt, q + 1)
                ch.link(v.tensor_copy(tot, bank(3)))
                ch.link(v.tensor_tensor_scan(scan, reset_e[:, :], tot, 0.0, ALU.mult, ALU.add))
                sc3 = scan.rearrange("p (e t) -> p e t", e=E)
                ch.link(v.tensor_scalar(nblk[:, :], sc3[:, :, CT - 1], 1.0 / P, 0.5 - 1.0 / (2 * P), ALU.mult, ALU.add))
                ch.link(v.tensor_scalar(nblk[:, :], nblk[:, :], ROUND, -ROUND, ALU.add, ALU.add))
                ch.link(v.tensor_tensor_scan(cumb[:, :], ones_b[:, 0:E], nblk[:, :], 0.0, ALU.mult, ALU.add))
                v.tensor_scalar(cmpb[:, :], cumb[:, :], iota_p[:, :], None, ALU.is_le)
                ch.link(v.tensor_tensor(begin[:, :], cumb[:, :], nblk[:, :], ALU.subtract))
                ch.link(v.tensor_reduce(eblk[:, :], cmpb[:, :], AX, ALU.add))
                v.tensor_scalar(eblk[:, :], eblk[:, :], float(E - 1), None, ALU.min).then_inc(f_eb, 1)
                ch.link(v.tensor_scalar(begin[:, :], begin[:, :], float(P), None, ALU.mult))
                v.tensor_tensor(place, bank(7), scan, ALU.add).then_inc(dch, 1)
                ch.n += 1
                dve.wait_ge(dch, ch.n)
                ch.link(v.tensor_tensor(place, place, tot, ALU.subtract))
                pl3 = place.rearrange("p (e t) -> p e t", e=E)
                ch.link(v.tensor_tensor(pl3, pl3, begin[:, :].unsqueeze(2).to_broadcast([P, E, CT]), ALU.add))
                for k in range(K):
                    last = v.tensor_tensor(OHP[:, k, :, :], OH[:, k, :, :], pl3, ALU.mult)
                ch.link(last)
                ch.link(v.tensor_reduce(posf[:, :, :], OHP[:, :, :, :].rearrange("p k e t -> p k t e"), AX, ALU.add))
                v.tensor_copy(pos[c][:, :, :], posf[:, :, :]).then_inc(f_pos, 1)
                dve.wait_ge(f_ebt, q + 1)
                v.tensor_copy(ids[c][:, :], bank(6)[0:1, 0:P]).then_inc(f_ids, 1)

            def shared(f):
                base = CH * TG * f

                def finish(g):
                    dve.wait_ge(h_y, base + g + 1)
                    xg = X[:, 4 * g:4 * g + 4, :].rearrange("p t d -> p (t d)")
                    v.scalar_tensor_tensor(xg, bank(6 + g % 2), 0.5, xg, ALU.mult, ALU.add).then_inc(h_x, 1)

                for g in range(CH * TG):
                    for j in range(4):
                        n = 4 * (base + g) + j
                        dve.wait_ge(h_s, n + 1)
                        if j == 0 and g >= 2:
                            dve.wait_ge(h_y, base + g - 1)
                        v.tensor_tensor(SHT[g % 2][:, j, :], SG[j % 2][:, :], bank(2 + j % 2), ALU.mult).then_inc(h_m, 1)
                    if g:
                        finish(g - 1)
                finish(CH * TG - 1)

            def experts(f, c):
                q = CH * f + c

                def mul(g, s):
                    dve.wait_ge(e_s, q * GR + g + 1)
                    u = banks[:, 2 * s:2 * s + 2, :].rearrange("p a (b c) -> p (a b) c", c=256)
                    v.tensor_tensor(HG[s][:, :, :], SG[s][:, :].rearrange("p (b c) -> p b c", b=4), u[:, :, 128:256],
                                    ALU.mult).then_inc(e_h, 1)

                def ht(g, s):
                    dve.wait_ge(e_th, q * GR + g + 1)
                    v.tensor_copy(HT[s][:, :], bank(5)).then_inc(e_ht, 1)

                with dve.Fori(0, GR // 2) as i:
                    mul(2 * i, 0)
                    mul(2 * i + 1, 1)
                    ht(2 * i, 0)
                    ht(2 * i + 1, 1)

            def combine(f, c):
                q = CH * f + c
                dve.wait_ge(e_gat[c], (f + 1) * CT * K * 16)
                for t0 in range(0, CT, 4):
                    for k in range(K):
                        for t in range(t0, t0 + 4):
                            xt = X[:, c * CT + t, :]
                            last = v.scalar_tensor_tensor(xt, G[:, t, k, :], GW[c][:, t, k:k + 1], xt, ALU.mult, ALU.add)
                            if k == K - 1:
                                last.then_inc(e_comb, 1)
                        if k < K - 1:
                            ch.link(last)

            BJ = [P, 4, NH, 8]

            def tail1(t):
                o, s = O[t.slot], t.slot
                dve.wait_ge(a_oc, NH * (t.index + 1))
                dve.wait_ge(a_pe, t.index + 1)
                v.tensor_reduce(lsum[:, :, :], o[:, :, :, :, 8].rearrange("p h i j -> p i h j"), AX, ALU.add)
                ch.link(v.scalar_tensor_tensor(dcor[:, :, :], adiag[s][:, :, :], 1.0, ediag[s][:, :, :],
                                               ALU.subtract, ALU.mult))
                ch.link(v.tensor_tensor(lsum[:, :, :], lsum[:, :, :], dcor[:, :, :], ALU.subtract))
                ch.link(v.reciprocal(rinv[:, :, :], lsum[:, :, :]))
                v.tensor_tensor(MX[s], MX[s], rinv[:, :, :].unsqueeze(3).to_broadcast(BJ), ALU.mult).then_inc(t_pm, 1)

            def tail2(t):
                dve.wait_ge(t_pt, t.index + 1)
                ch.link(v.tensor_reduce(bmax[:, :], bank(6).rearrange("p (b n) -> p b n", n=BS), AX, ALU.max))
                v.tensor_scalar(keepx[:, :].rearrange("p (b n) -> p b n", n=BS),
                                bmax[:, :].unsqueeze(2).to_broadcast([P, 8, BS]), THRESH, None, ALU.is_gt).then_inc(t_kx, 1)

            def tail3(t):
                s = t.slot
                dve.wait_ge(t_kn, t.index + 1)
                v.tensor_tensor(KR, bank(7).rearrange("p (i h j) -> p i h j", i=4, h=NH),
                                rinv[:, :, :].unsqueeze(3).to_broadcast(BJ), ALU.mult).then_inc(t_kr, 1)
                dve.wait_ge(t_kr, t.index + 1)
                ch.link(v.tensor_tensor(tmp, KR, AL[s], ALU.mult))
                ch.link(v.tensor_tensor(tmp, tmp, diag_sel[:, :, :].unsqueeze(2).to_broadcast(BJ), ALU.mult))
                ch.link(v.tensor_reduce(dcor[:, :, :], tmp, AX, ALU.add))
                ch.link(v.tensor_tensor(dcor[:, :, :], rinv[:, :, :], dcor[:, :, :], ALU.subtract))
                ch.link(v.tensor_tensor(dcor[:, :, :], dcor[:, :, :], ediag[s][:, :, :], ALU.mult))
                for half in range(2):
                    ps = slice(64 * half, 64 * half + 64)
                    last = v.tensor_tensor(tmp[ps, :, :, :], VA[s][ps, :, :, 9 * half:9 * half + 8],
                                           dcor[ps, :, :].unsqueeze(3).to_broadcast([64, 4, NH, HD]), ALU.mult)
                ch.mark(last)

            def tail4(t):
                for i in range(4):
                    dve.wait_ge(t_w, 4 * t.index + i + 1)
                    last = v.tensor_reduce(AO[:, i, :, :], O[t.slot][:, :, i, :, 0:8].rearrange("p h j d -> p h d j"),
                                           AX, ALU.add)
                ch.link(last)
                v.tensor_tensor(AO, AO, tmp, ALU.add).then_inc(t_ao, 1)

            def tail5(t):
                dve.wait_ge(t_op, t.index + 1)
                xg = X[:, bass.ds(4 * t.index, 4), :].rearrange("p t d -> p (t d)")
                v.tensor_tensor(xg, xg, bank(7), ALU.add).then_inc(t_x, 1)

            def maxima(a, h):
                for i in range(4):
                    n = 4 * h + i
                    dve.wait_ge(a_a, 4 * NH * a.index + n + 1)
                    v.tensor_reduce(MX[a.slot][:, i, h, :], bank(n % 2).rearrange("p (b n) -> p b n", n=BS), AX,
                                    ALU.max).then_inc(a_ar, 1)

            def rows(a):
                s = a.slot
                dve.wait_ge(a_mnc, a.index + 1)
                dve.wait_ge(a_ar, 4 * NH * (a.index + 1))
                v.tensor_tensor(tmp, diag_bias[:, :, :].unsqueeze(2).to_broadcast(BJ),
                                sdiag[s][:, :, :].unsqueeze(3).to_broadcast(BJ), ALU.add)
                v.tensor_scalar(AL[s], MN[s], -1.0, None, ALU.is_ge)
                ch.link(v.tensor_tensor(MX[s], MX[s], MN[s], ALU.add))
                ch.link(v.tensor_tensor(MX[s], MX[s], tmp, ALU.max))
                ch.link(v.tensor_reduce(mrow[:, :, :], MX[s], AX, ALU.max))
                v.tensor_scalar(mparts[:, :, 0, :], mrow[:, :, :], -1.0, None, ALU.mult)
                v.tensor_tensor(ediag[s][:, :, :], sdiag[s][:, :, :], mrow[:, :, :], ALU.subtract)
                ch.link(v.tensor_tensor(MX[s], MX[s], mrow[:, :, :].unsqueeze(3).to_broadcast(BJ), ALU.subtract))
                ch.link(v.scalar_tensor_tensor(mres[:, :, :], mrow[:, :, :], -1.0, mparts[:, :, 0, :],
                                               ALU.mult, ALU.subtract))
                ch.link(v.tensor_copy(mparts[:, :, 1, :], mres[:, :, :]))
                v.tensor_tensor(mparts[:, :, 2, :], mres[:, :, :], mparts[:, :, 1, :], ALU.subtract).then_inc(a_mp, 1)
                ch.link(v.tensor_tensor(tmp, AL[s], diag_sel[:, :, :].unsqueeze(2).to_broadcast(BJ), ALU.mult))
                v.tensor_reduce(adiag[s][:, :, :], tmp, AX, ALU.add).then_inc(a_pd, 1)

            def prepare(c):
                s = c.slot
                for j in range(4):
                    last = v.bn_stats(stats[:, j, :], X[:, bass.ds(4 * c.index + j, 1), :].rearrange("p a d -> p (a d)"))
                ch.link(last)
                dve.nop(nofuse=True)
                for j in range(4):
                    last = v.bn_aggr(mv[:, j, :], stats[:, j, :])
                last.then_inc(a_stat, 1)
                dve.wait_ge(a_sqrt, c.index + 1)
                ch.link(v.reciprocal(rstd[:, 0:4], rstd[:, 0:4]))
                for j in range(4):
                    last = v.tensor_scalar(xa[:, j, :], X[:, bass.ds(4 * c.index + j, 1), :].rearrange("p a d -> p (a d)"),
                                           mv[:, j, 0:1], rstd[:, j:j + 1], ALU.subtract, ALU.mult)
                last.then_inc(a_xa, 1)
                for m in range(2):
                    dve.wait_ge(a_hi, 2 * c.index + m + 1)
                    if c.k >= 1 and m == 0:
                        dve.wait_ge(a_parts, 2 * c.index)
                    v.tensor_tensor(rest[m][:, :], bank(6 + m), qk_hi[m][:, :], ALU.subtract).then_inc(a_rest, 1)
                    v.tensor_reduce(bsum[:, m, :], bank(6 + m).rearrange("p (b n) -> p b n", n=BS), AX,
                                    ALU.add).then_inc(a_sum, 1)
                dve.wait_ge(a_sum, 2 * (c.index + 1))
                ch.link(v.tensor_scalar(bsum[:, :, :], bsum[:, :, :], 1.0 / BS, None, ALU.mult))
                v.tensor_tensor(kmd[:, :, :], block_diag[:, :, :], bsum[:, 1:2, :].to_broadcast([P, NH, 8]),
                                ALU.mult).then_inc(a_kmd, 1)
                dve.wait_ge(a_natc, 4 * (c.index + 1))
                for i in range(4):
                    last = v.tensor_tensor(prod[:, i, :, :], NAT[:, i, 0, :, :], NAT[:, i, 1, :, :], ALU.mult)
                ch.link(last)
                v.tensor_reduce(sdiag[s][:, :, :], prod, AX, ALU.add).then_inc(a_sd, 1)
                dve.wait_ge(a_mb, c.index + 1)
                if c.k >= 1:
                    dve.wait_ge(a_dw, 7 * 16 * c.index)
                v.tensor_scalar(mbt[:, :].rearrange("p (b n) -> p b n", n=BS),
                                bank(6)[:, 0:8].unsqueeze(2).to_broadcast([P, 8, BS]),
                                THRESH * float(HD) ** 0.5, -BIG, ALU.is_le, ALU.mult).then_inc(a_mbt, 1)
                dve.wait_ge(a_sd, c.index + 1)

            def step(b, what):
                a, c, t = b.plus(1), b.plus(2), b.plus(-1)
                if "T" in what:
                    tail1(t)
                    tail2(t)
                    tail3(t)
                if "A" in what:
                    for h in range(4):
                        maxima(a, h)
                if "T" in what:
                    tail4(t)
                if "A" in what:
                    for h in range(4, 12):
                        maxima(a, h)
                if "T" in what:
                    tail5(t)
                if "A" in what:
                    for h in range(12, NH):
                        maxima(a, h)
                    rows(a)
                if "P" in what:
                    prepare(c)

            route(0, 0)
            route(0, 1)
            shared(0)
            experts(0, 0)
            experts(0, 1)
            combine(0, 0)
            combine(0, 1)
            dve.wait_ge(e_comb, CH * CT)
            per = 2 * PER_DVE
            for rounds, _, part in steps():
                if rounds is None:
                    for k, what in part:
                        step(Batch(k), what)
                else:
                    with dve.Fori(0, rounds) as i:
                        ch.enter(i, per)
                        for k, what in part:
                            step(Batch(k, i), what)
                        ch.leave(rounds)
            dve.wait_ge(t_x, NB)
            route(1, 0)
            route(1, 1)
            shared(1)
            experts(1, 0)
            experts(1, 1)
            combine(1, 0)
            combine(1, 1)

        @block.tensor
        def _(pe):
            mm, tr = nc.tensor.matmul, nc.tensor.transpose

            def route(f, c):
                q = CH * f + c
                if q == 0:
                    pe.wait_ge(s_cst, 1)
                    pe.wait_ge(s_w, 7 * 16)
                if f == 1 and c == 0:
                    pe.wait_ge(t_x, NB)
                for n in range(TG):
                    pe.wait_ge(f_xn, q * TG + n + 1)
                    if n >= 2:
                        pe.wait_ge(f_xnt, q * TG + n - 1)
                    for j in range(4):
                        last = tr(bank(4 + n % 2)[:, j * P:(j + 1) * P], XN[:, c * CT + 4 * n + j, :], identf[:, :])
                    last.then_inc(f_tx, 1)
                    if n >= 1:
                        logits(q, c, n - 1)
                logits(q, c, TG - 1).then_inc(f_log, 1)
                pe.wait_ge(f_oh, q + 1)
                if c:
                    pe.wait_ge(f_pos, q)
                for k in range(K):
                    mm(bank(7), tri[:, :], OH[:, k, :, :].rearrange("p e t -> p (e t)"), start=k == 0, stop=k == K - 1)
                for k in range(K):
                    last = mm(bank(3), ones_b[:, 0:P], OH[:, k, :, :].rearrange("p e t -> p (e t)"),
                              start=k == 0, stop=k == K - 1)
                last.then_inc(f_cnt, 1)
                pe.wait_ge(f_eb, q + 1)
                mm(bank(6)[0:1, 0:P], eblk[:, :], identf[:, :], start=True, stop=True).then_inc(f_ebt, 1)

            def logits(q, c, n):
                pe.wait_ge(f_xnt, q * TG + n + 1)
                if n == 0 and c:
                    pe.wait_ge(f_ids, q)
                for j in range(4):
                    t = 4 * n + j
                    last = mm(bank(6)[:, t * E:(t + 1) * E], XNT[:, (c * CT + t) * P:(c * CT + t + 1) * P], rw_s[:, :],
                              start=True, stop=True)
                return last

            def shared(f):
                base = CH * TG * f
                pe.wait_ge(f_ids, CH * (f + 1))
                pe.wait_ge(f_pos, CH * (f + 1))

                def gate_up(g, j):
                    n = 4 * (base + g) + j
                    xn = XNT[:, g * 512:(g + 1) * 512]
                    if n >= 2:
                        pe.wait_ge(h_m, n - 1)
                    mm(bank(j % 2), sg_s[:, j * P:(j + 1) * P], xn, start=True, stop=True)
                    mm(bank(2 + j % 2), su_s[:, j * P:(j + 1) * P], xn, start=True, stop=True).then_inc(h_g, 1)

                def down(g):
                    pe.wait_ge(h_m, 4 * (base + g + 1))
                    if g >= 2:
                        pe.wait_ge(h_x, base + g - 1)
                    for t in range(4):
                        for j in range(4):
                            last = mm(bank(6 + g % 2)[:, t * P:(t + 1) * P], SHT[g % 2][:, j, t * P:(t + 1) * P],
                                      sd_s[:, j, :], start=j == 0, stop=j == 3)
                    last.then_inc(h_y, 1)

                for g in range(CH * TG):
                    gate_up(g, 0)
                    gate_up(g, 1)
                    if g:
                        down(g - 1)
                    gate_up(g, 2)
                    gate_up(g, 3)
                down(CH * TG - 1)

            def experts(f, c):
                q = CH * f + c
                if c == 0:
                    pe.wait_ge(s_we, 32 * (f + 1))
                if c == 0:
                    pe.wait_ge(h_x, CH * TG * (f + 1))

                def rows(g, i, s):
                    pe.wait_ge(e_xg[s], 16 * (q * (GR // 2) + i + 1))
                    if q or not (isinstance(g, int) and g == 0):
                        pe.wait_ge(e_xt, q * GR + g)
                    for j in range(4):
                        last = tr(bank(4)[:, j * P:(j + 1) * P], XG[s][:, j, :], identf[:, :])
                    last.then_inc(e_tx, 1)

                def gate_up(g, s, which):
                    pe.wait_ge(e_xt, q * GR + g + 1)
                    for j in range(4):
                        o = bank(2 * s + j // 2)[:, 256 * (j % 2):256 * (j % 2) + 256]
                        last = mm(o, XT[s][:, j * P:(j + 1) * P], wgu_s[:, bass.ds(which[j] * (2 * H), 2 * H)],
                                  start=True, stop=True)
                    last.then_inc(e_gu, 1)

                def turn(g, s):
                    pe.wait_ge(e_h, q * GR + g + 1)
                    if q or not (isinstance(g, int) and g == 0):
                        pe.wait_ge(e_ht, q * GR + g)
                    for j in range(4):
                        last = tr(bank(5)[:, j * P:(j + 1) * P], HG[s][:, j, :], identf[:, :])
                    last.then_inc(e_th, 1)

                def down(g, i, s, which):
                    pe.wait_ge(e_ht, q * GR + g + 1)
                    for j in range(4):
                        last = mm(bank(6 + s)[:, j * P:(j + 1) * P], HT[s][:, j * P:(j + 1) * P],
                                  wd_s[:, bass.ds(which[j] * D, D)], start=True, stop=True)
                    last.then_inc(e_y, 1)

                def pair(i, more):
                    which = [pe.value_load(ids[c][0:1, bass.ds(8 * i + j, 1)], min_val=0, max_val=E - 1) for j in range(8)]
                    if q or not (isinstance(i, int) and i == 0):
                        pe.wait_ge(e_yc, q * GR + 2 * i)
                    gate_up(2 * i, 0, which[0:4])
                    gate_up(2 * i + 1, 1, which[4:8])
                    turn(2 * i, 0)
                    if more:
                        rows(2 * i + 2, i + 1, 0)
                    turn(2 * i + 1, 1)
                    if more:
                        rows(2 * i + 3, i + 1, 1)
                    down(2 * i, i, 0, which[0:4])
                    down(2 * i + 1, i, 1, which[4:8])

                rows(0, 0, 0)
                rows(1, 0, 1)
                pair(0, True)
                with pe.Fori(1, GR // 2 - 1) as i:
                    pair(i, True)
                pair(GR // 2 - 1, False)

            def tail_p(t):
                pe.wait_ge(t_pm, t.index + 1)
                for i in range(4):
                    m = MX[t.slot][:, i, :, :].rearrange("p h j -> p (h j)")
                    last = tr(bank(6)[:, i * P:(i + 1) * P], m, identf[:, :])
                last.then_inc(t_pt, 1)

            def tail_k(t):
                pe.wait_ge(t_kx, t.index + 1)
                for i in range(4):
                    last = mm(bank(7)[:, i * P:(i + 1) * P], keepx[:, i * P:(i + 1) * P], identb[:, :], start=True, stop=True)
                last.then_inc(t_kn, 1)

            def tail_a(t):
                pe.wait_ge(t_ao, t.index + 1)
                for i in range(4):
                    o = AO[:, i, :, :].rearrange("p h d -> p (h d)")
                    last = tr(bank(6)[:, i * P:(i + 1) * P], o, identf[:, :])
                last.then_inc(t_at, 1)

            def tail_o(t):
                pe.wait_ge(t_atc, t.index + 1)
                for i in range(4):
                    last = mm(bank(7)[:, i * P:(i + 1) * P], AOT[:, i * P:(i + 1) * P], wo_s[:, :], start=True, stop=True)
                last.then_inc(t_op, 1)

            def max_scores(a, h):
                p0 = 64 * (h % 2)
                o = (h // 2) * 512
                for i in range(4):
                    n = 4 * h + i
                    if a.k >= 1 or n >= 2:
                        pe.wait_ge(a_ar, 4 * NH * a.index + n - 1)
                    mm(bank(n % 2), QS[a.slot][p0:p0 + 48, o + i * P:o + (i + 1) * P], KS[a.slot][p0:p0 + 48, o:o + 512],
                       start=True, stop=True).then_inc(a_a, 1)

            def scores(b, h):
                p0 = 64 * (h % 2)
                o = (h // 2) * 512
                for j in range(AH):
                    n = AH * h + j
                    if n >= 3:
                        pe.wait_ge(a_e, AH * NH * b.index + n - 2)
                    elif b.k >= 1:
                        pe.wait_ge(a_e, AH * NH * b.index)
                    mm(bank(2 + n % 3), KS[b.slot][p0:p0 + 59, o + j * P:o + (j + 1) * P], QS[b.slot][p0:p0 + 59, o:o + 512],
                       start=True, stop=True).then_inc(a_s, 1)

            def sums(b, h):
                pe.wait_ge(a_e, AH * (NH * b.index + h + 1))
                if b.k >= 1 or h >= 1:
                    pe.wait_ge(a_oc, NH * b.index + h)
                for i in range(4):
                    for j in range(AH):
                        last = mm(bank(5)[:, 72 * i + 18 * j:72 * i + 18 * j + 18],
                                  PT[h % 2][:, 512 * j + i * P:512 * j + (i + 1) * P], VA[b.slot][:, j, h, :],
                                  start=True, stop=True)
                last.then_inc(a_pv, 1)

            def max_turn(a):
                pe.wait_ge(a_mp, a.index + 1)
                pe.nop(nofuse=True)
                for i in range(4):
                    m = mparts[:, i, :, :].rearrange("p m h -> p (m h)")
                    last = tr(bank(6).bitcast(BF16)[0:3 * NH, i * P:(i + 1) * P], m, identb[:, :])
                last.then_inc(a_mt, 1)

            def prepare(c, after_max):
                pe.wait_ge(a_xa, c.index + 1)
                for j in range(4):
                    last = tr(bank(7)[:, j * P:(j + 1) * P], xa[:, j, :], identf[:, :])
                last.then_inc(a_tx, 1)
                pe.wait_ge(a_xt, c.index + 1)
                if after_max is not None:
                    pe.wait_ge(a_mtc, after_max.index + 1)
                for m in range(2):
                    mm(bank(6 + m), wqkv_s[:, m * D:(m + 1) * D], xaT[:, :], start=True, stop=True).then_inc(a_qk, 1)
                for i in range(4):
                    if i < 2:
                        pe.wait_ge(a_sum, 2 * c.index + i + 1)
                    else:
                        pe.wait_ge(a_natc, 4 * c.index + i - 1)
                    mm(bank(6 + i % 2)[:, 0:384], xaT[:, i * P:(i + 1) * P], wqkv_s[:, :], start=True, stop=True).then_inc(a_nat, 1)
                pe.wait_ge(a_natc, 4 * (c.index + 1))
                pe.wait_ge(a_kmd, c.index + 1)
                mm(bank(6)[:, 0:8], kmd[:, :, :].rearrange("p h j -> p (h j)"), bsum[:, 0, :], start=True,
                   stop=True).then_inc(a_mb, 1)
                pe.wait_ge(a_mbt, c.index + 1)
                for i in range(4):
                    last = mm(bank(7)[:, i * P:(i + 1) * P], mbt[:, i * P:(i + 1) * P], identb[:, :], start=True, stop=True)
                last.then_inc(a_mn, 1)

            def step(b, what):
                a, c, t = b.plus(1), b.plus(2), b.plus(-1)
                if "B" in what:
                    pe.wait_ge(a_mr[b.slot], 32 * (b.round + 1))
                    pe.wait_ge(a_va, b.index + 1)
                for h in range(NH + 1):
                    if "B" in what and h < NH:
                        scores(b, h)
                    if "A" in what and 4 <= h < 12:
                        if h == 4:
                            pe.wait_ge(a_stk[a.slot], STK * (a.round + 1))
                            if a.k == 0:
                                pe.wait_ge(a_cdma, 64 * 16)
                        max_scores(a, 2 * (h - 4))
                        max_scores(a, 2 * (h - 4) + 1)
                    if "B" in what and h > 0:
                        sums(b, h - 1)
                    if "T" in what:
                        {2: tail_p, 3: tail_k, 7: tail_a, 9: tail_o}.get(h, lambda t: None)(t)
                    if h == 13 and "A" in what:
                        max_turn(a)
                    if h == 14 and "P" in what:
                        if "T" in what:
                            pe.wait_ge(t_x, t.index + 1)
                        prepare(c, a if "A" in what else None)

            route(0, 0)
            route(0, 1)
            shared(0)
            experts(0, 0)
            experts(0, 1)
            pe.wait_ge(e_yc, CH * GR)
            for rounds, _, part in steps():
                if rounds is None:
                    for k, what in part:
                        step(Batch(k), what)
                else:
                    with pe.Fori(0, rounds) as i:
                        for k, what in part:
                            step(Batch(k, i), what)
            route(1, 0)
            route(1, 1)
            shared(1)
            experts(1, 0)
            experts(1, 1)


PER_DVE = 22


def kernel(**inputs):
    import numpy as np
    import concourse.bacc as bacc
    from concourse.bass_utils import run_bass_kernel_spmd

    def lay(a):
        return np.ascontiguousarray(a)

    g = {k.replace("L0_", ""): np.asarray(v) for k, v in inputs.items()}
    arrays = {
        "x": lay(g["attn_x"].reshape(-1, P, D)),
        "wqkv": lay(np.concatenate([g["attn_wq"].T, g["attn_wk"].T, g["attn_wv"].T], axis=1)),
        "wo": lay(g["attn_wo"].T),
        "rw": lay(g["ffn_router_w"].T),
        "rb": lay(g["ffn_router_bias"]),
        "wgu": lay(np.concatenate([g["ffn_gate_w"].transpose(2, 0, 1), g["ffn_up_w"].transpose(2, 0, 1)],
                                  axis=2).reshape(D, E * 2 * H)),
        "wd": lay(g["ffn_down_w"].transpose(2, 0, 1).reshape(H, E * D)),
        "sg": lay(g["ffn_sgate_w"].T),
        "su": lay(g["ffn_sup_w"].T),
        "sd": lay(g["ffn_sdown_w"].T.reshape(4, P, D).transpose(1, 0, 2)),
    }
    nc = bacc.Bacc("TRN2", target_bir_lowering=False, num_devices=1)
    aps = [nc.dram_tensor(n, a.shape, FP32, kind="ExternalInput").ap() for n, a in arrays.items()]
    out = nc.dram_tensor("out", arrays["x"].shape, FP32, kind="ExternalOutput").ap()
    nc.disable_value_cache = True
    build(nc, *aps, out)
    r = run_bass_kernel_spmd(nc, [arrays], core_ids=[0])
    return r.results[0]["out"].reshape(g["attn_x"].shape)
```

```python
import concourse.bass as bass
from concourse import mybir
from contextlib import ExitStack

FP32 = mybir.dt.float32
BF16 = mybir.dt.bfloat16
U32 = mybir.dt.uint32
I32 = mybir.dt.int32
ALU = mybir.AluOpType
ACT = mybir.ActivationFunctionType
AX = mybir.AxisListType.X

P = 128
D = 128
NH, HD = 16, 8
BS = 64
SCALE = float(HD) ** -0.5
THRESH = 0.01
PIECES = 10
BIG = 1.0e30
E, K, H, HS = 32, 4, 128, 512
EPS = 1e-5
ROUND = 12582912.0


class Chain:

    def __init__(self, engine, sem):
        self.engine, self.sem, self.n, self.off = engine, sem, 0, 0

    def mark(self, ins):
        ins.then_inc(self.sem, 1)
        self.n += 1

    def link(self, ins):
        self.mark(ins)
        self.engine.wait_ge(self.sem, self.n + self.off)

    def enter(self, i, per):
        self.start, self.per, self.off = self.n, per, i * per

    def leave(self, rounds):
        assert self.n - self.start == self.per, (self.n - self.start, self.per)
        self.n, self.off = self.start + rounds * self.per, 0


class Batch:

    def __init__(self, k, i=0):
        self.k, self.i = k, i
        self.index, self.slot, self.round = k + 2 * i, k % 2, k // 2 + i

    def plus(self, d):
        return Batch(self.k + d, self.i)


def build(nc, x, wqkv, wo, rw, rb, wgu, wd, sg, su, sd, out):
    T = x.shape[0]
    NB = T // 4
    CH = 2
    CT = T // CH
    TG = CT // 4
    BLK = (CT * P * K + E * (P - 1)) // P
    BLK += -BLK % 8
    GR = BLK // 4

    ctx = ExitStack()
    with ctx:
        def sb(name, shape, dt=FP32):
            return ctx.enter_context(nc.sbuf_tensor(name, shape, dt))

        def sem(name):
            return ctx.enter_context(nc.semaphore(name))

        XS = [nc.dram_tensor(f"rows_by_expert{c}", [BLK * P, D], FP32).ap() for c in range(CH)]
        YS = [nc.dram_tensor(f"results_by_expert{c}", [BLK * P, D], FP32).ap() for c in range(CH)]
        qk_parts = [nc.dram_tensor(f"qk_parts{s}", [6, NH * HD, 512], BF16).ap() for s in range(2)]
        mask_rows = [nc.dram_tensor(f"mask_rows{s}", [NH * 8, 512], BF16).ap() for s in range(2)]
        max_rows = [nc.dram_tensor(f"max_rows{s}", [3 * NH, 512], BF16).ap() for s in range(2)]

        X = sb("X", [P, T, D])
        wqkv_s = sb("wqkv_s", [P, 3 * D])
        wo_s = sb("wo_s", [P, D])
        rw_s = sb("rw_s", [P, E])
        rb_s = sb("rb_s", [P, E])
        wgu_s = sb("wgu_s", [P, E * 2 * H])
        wd_s = sb("wd_s", [P, E * D])
        sg_s = sb("sg_s", [P, HS])
        su_s = sb("su_s", [P, HS])
        sd_s = sb("sd_s", [P, 4, D])
        identf = sb("identf", [P, P])
        identb = sb("identb", [P, P], BF16)
        tri = sb("tri", [P, P], BF16)
        ones_b = sb("ones_b", [P, 512], BF16)
        iota_e = sb("iota_e", [P, E])
        iota_p = sb("iota_p", [P, 1])
        block_diag = sb("block_diag", [P, NH, 8])
        diag_sel = sb("diag_sel", [P, 4, 8])
        diag_bias = sb("diag_bias", [P, 4, 8])
        key_block = sb("key_block", [8, 512], BF16)
        eps_c = sb("eps_c", [P, 1])
        half_sel = sb("half_sel", [P, 2])
        ones_f = sb("ones_f", [P, 4 * NH])
        reset_e = sb("reset_e", [P, E * 16])

        arena_g = sb("arena_g", [P, CT * K * D])
        arena_n = sb("arena_n", [P, T * D])
        arena_o = sb("arena_o", [P, 2 * NH * 4 * 72])
        HC = CT // 2
        G0 = arena_g[:, :].rearrange("p (t k d) -> p t k d", t=CT, k=K)
        G1 = [m[:, 0:HC * K * D].rearrange("p (t k d) -> p t k d", t=HC, k=K) for m in (wd_s, arena_o)]
        G = [[G0[:, t] for t in range(CT)], [G1[t // HC][:, t % HC] for t in range(CT)]]
        stacks = wgu_s[:, :].bitcast(BF16)
        QS = [stacks[:, 4096 * s:4096 * (s + 1)] for s in range(2)]
        KS = [stacks[:, 8192 + 4096 * s:8192 + 4096 * (s + 1)] for s in range(2)]
        PT = [wd_s[:, 2048 * s:2048 * (s + 1)] for s in range(2)]
        XNT = arena_n
        XN = arena_o[:, 0:T * D].rearrange("p (t d) -> p t d", t=T)
        O = [arena_o[:, 4608 * s:4608 * (s + 1)].rearrange("p (h i j c) -> p h i j c", h=NH, i=4, j=8)
             for s in range(2)]

        class Carve:

            def __init__(self, arena, at):
                self.arena, self.at = arena, at

            def take(self, words, dt=FP32):
                piece = self.arena[:, self.at:self.at + words]
                self.at += words
                assert self.at <= self.arena.shape[1]
                return piece if dt == FP32 else piece.bitcast(dt)

        beside_xn = Carve(arena_o, T * D)
        in_g = Carve(arena_g, 0)
        work_g = Carve(arena_g, 0)
        zero_t = work_g.take(2048)
        in_n = Carve(arena_n, 0)

        stats = sb("stats", [P, CT, 6])
        mv = sb("mv", [P, CT, 2])
        rstd = sb("rstd", [P, CT])
        arena_r = sb("arena_r", [P, 5 * 512])
        L = arena_r[:, 0:512].rearrange("p (t e) -> p t e", t=CT)
        EX = arena_r[:, 512:1024].rearrange("p (t e) -> p t e", t=CT)
        tot = arena_r[:, 1024:1536]
        scan = arena_r[:, 1536:2048]
        place = arena_r[:, 2048:2560]
        OH = beside_xn.take(K * E * CT // 2, BF16).rearrange("p (k e t) -> p k e t", k=K, e=E)
        OHP = work_g.take(K * E * CT).rearrange("p (k e t) -> p k e t", k=K, e=E)
        top8 = sb("top8", [P, CT, 8])
        idx8 = sb("idx8", [P, CT, 8], U32)
        idxf = sb("idxf", [P, CT, 8])
        topw = sb("topw", [P, CT, K])
        zsum = sb("zsum", [P, CT])
        wsum = sb("wsum", [P, CT])
        GW = [sb(f"GW{c}", [P, CT, K]) for c in range(CH)]
        posf = sb("posf", [P, K, CT])
        pack = sb("pack", [P, GR])
        pos = [sb(f"pos{c}", [P, K, CT], U32) for c in range(CH)]
        nblk = sb("nblk", [P, E])
        cumb = sb("cumb", [P, E])
        begin = sb("begin", [P, E])
        cmpb = sb("cmpb", [P, E])
        eblk = sb("eblk", [P, 1])
        ids = [sb(f"ids{c}", [1, GR], I32) for c in range(CH)]
        XG = [sb("XG0", [P, 512])[:, :], beside_xn.take(512)]
        XG = [g.rearrange("p (b d) -> p b d", b=4) for g in XG]
        XT = [sb("XT0", [P, 512]), beside_xn.take(512)]
        SG = [sb("SG0", [P, 512]), beside_xn.take(512)]
        HG = [sb("HG0", [P, 512])[:, :], beside_xn.take(512)]
        HG = [g.rearrange("p (b d) -> p b d", b=4) for g in HG]
        HT = [sb(f"HT{s}", [P, 512]) for s in range(2)]
        YG = [sb(f"YG{s}", [P, 4, D]) for s in range(2)]
        SHT = [work_g.take(2048).rearrange("p (j n) -> p j n", j=4) for s in range(2)]

        xa = XG[0]
        xaT = XT[0]
        qk_hi, qk_mid, qk_lo = ([in_g.take(256, BF16) for n in range(2)] for _ in range(3))
        rest = [HT[0], HT[1]]
        bsum = sb("bsum", [P, 2, 8])
        kmd = in_g.take(128).rearrange("p (h j) -> p h j", h=NH)
        mbt = in_g.take(256, BF16)
        NAT = in_g.take(4 * 384).rearrange("p (i a h d) -> p i a h d", i=4, a=3, h=NH)
        prod = HG[0][:, :, :].rearrange("p a (h d) -> p a h d", h=NH)
        MN, MX, AL = ([in_n.take(512).rearrange("p (i h j) -> p i h j", i=4, h=NH) for s in range(2)] for _ in range(3))
        tmp = in_n.take(512).rearrange("p (i h j) -> p i h j", i=4, h=NH)
        sdiag = [sb(f"sdiag{s}", [P, 4, NH]) for s in range(2)]
        ediag = [sb(f"ediag{s}", [P, 4, NH]) for s in range(2)]
        adiag = [sb(f"adiag{s}", [P, 4, NH]) for s in range(2)]
        mrow = sb("mrow", [P, 4, NH])
        mres = sb("mres", [P, 4, NH])
        mparts = sb("mparts", [P, 4, 3, NH], BF16)
        mrows = sb("mrows", [3 * NH, 512], BF16)
        lsum = sb("lsum", [P, 4, NH])
        rinv = sb("rinv", [P, 4, NH])
        dcor = sb("dcor", [P, 4, NH])
        bmax = sb("bmax", [P, 8])
        keepx = in_g.take(256, BF16)
        KR = YG[0][:, :, :].rearrange("p i (h j) -> p i h j", h=NH)
        AO = YG[1][:, :, :].rearrange("p i (h d) -> p i h d", h=NH)
        AOT = SG[0]
        OT = arena_r[:, 0:512]
        VA = [in_g.take(4 * NH * 32).rearrange("p (i h c) -> p i h c", i=4, h=NH) for s in range(2)]

        banks = ctx.enter_context(nc.psum_tensor("banks", [P, 8, 512], FP32))

        def bank(n):
            return banks[:, n, :]

        s_x = [sem(f"s_x{c}") for c in range(CH)]
        s_w = sem("s_w")
        s_we = sem("s_we")
        s_zero = sem("s_zero")
        s_cst = sem("s_cst")
        s_zt = sem("s_zt")
        dch = sem("dve_chain")
        ach = sem("act_chain")
        pch = sem("pool_chain")
        f_stat = sem("f_stat")
        f_sqrt = sem("f_sqrt")
        f_xn = sem("f_xn")
        f_tx = sem("f_tx")
        f_xnt = sem("f_xnt")
        f_log = sem("f_log")
        f_lm = sem("f_lm")
        f_ex = sem("f_ex")
        f_oh = sem("f_oh")
        f_cnt = sem("f_cnt")
        f_eb = sem("f_eb")
        f_ebt = sem("f_ebt")
        f_ids = sem("f_ids")
        f_pos = sem("f_pos")
        h_g = sem("h_g")
        h_s = sem("h_s")
        h_m = sem("h_m")
        h_y = sem("h_y")
        h_x = sem("h_x")
        e_scat = [sem(f"e_scat{c}") for c in range(CH)]
        e_xg = [sem(f"e_xg{s}") for s in range(2)]
        e_tx = sem("e_tx")
        e_xt = sem("e_xt")
        e_gu = sem("e_gu")
        e_s = sem("e_s")
        e_h = sem("e_h")
        e_th = sem("e_th")
        e_ht = sem("e_ht")
        e_y = sem("e_y")
        e_yc = sem("e_yc")
        e_st = [sem(f"e_st{s}") for s in range(2)]
        e_gat = [sem(f"e_gat{c}") for c in range(CH)]
        e_comb = sem("e_comb")
        a_va = sem("a_va")
        a_cdma = sem("a_cdma")
        a_stat = sem("a_stat")
        a_sqrt = sem("a_sqrt")
        a_xa = sem("a_xa")
        a_tx = sem("a_tx")
        a_xt = sem("a_xt")
        a_qk = sem("a_qk")
        a_hi = sem("a_hi")
        a_rest = sem("a_rest")
        a_sum = sem("a_sum")
        a_parts = sem("a_parts")
        a_nat = sem("a_nat")
        a_natc = sem("a_natc")
        a_sd = sem("a_sd")
        a_kmd = sem("a_kmd")
        a_mb = sem("a_mb")
        a_mbt = sem("a_mbt")
        a_mn = sem("a_mn")
        a_mnc = sem("a_mnc")
        a_dw = sem("a_dw")
        a_stk = [sem(f"a_stk{s}") for s in range(2)]
        a_a = sem("a_a")
        a_ar = sem("a_ar")
        a_mp = sem("a_mp")
        a_mt = sem("a_mt")
        a_mtc = sem("a_mtc")
        a_pd = sem("a_pd")
        a_pe = sem("a_pe")
        a_mw = sem("a_mw")
        a_mr = [sem(f"a_mr{s}") for s in range(2)]
        a_s = sem("a_s")
        a_e = sem("a_e")
        a_pv = sem("a_pv")
        a_otc = sem("a_otc")
        a_ot = sem("a_ot")
        a_oc = sem("a_oc")
        t_pm = sem("t_pm")
        t_pt = sem("t_pt")
        t_kx = sem("t_kx")
        t_kn = sem("t_kn")
        t_kr = sem("t_kr")
        t_w = sem("t_w")
        t_ao = sem("t_ao")
        t_at = sem("t_at")
        t_atc = sem("t_atc")
        t_op = sem("t_op")
        t_x = sem("t_x")
        s_out = sem("s_out")

        STK = 26 * 16
        AH = 4

        def steps():
            yield None, 0, [(-2, "P"), (-1, "AP"), (0, "BAP")]
            yield 2, 1, [(1, "TBAP"), (2, "TBAP")]
            yield None, 0, [(5, "TBAP"), (6, "TBA"), (7, "TB"), (8, "T")]

        block = ctx.enter_context(nc.Block())

        @block.sync
        def _(sp):
            for c in range(CH):
                sp.dma_start(X[:, c * CT:(c + 1) * CT, :], x[c * CT:(c + 1) * CT].rearrange("t p d -> p t d")).then_inc(s_x[c], 16)
            for dst, src in ((rw_s, rw), (rb_s, rb.rearrange("(a e) -> a e", a=1).to_broadcast([P, E])),
                             (sg_s, sg), (su_s, su), (wqkv_s, wqkv), (wo_s, wo)):
                sp.dma_start(dst[:, :], src).then_inc(s_w, 16)
            sp.dma_start(sd_s[:, :, :], sd).then_inc(s_w, 16)
            sp.wait_ge(s_zt, 1)
            for c in range(CH):
                for n in range(BLK // 16):
                    sp.dma_start(XS[c][n * 16 * P:(n + 1) * 16 * P, :].rearrange("(b p) d -> p b d", p=P),
                                 zero_t.rearrange("p (b d) -> p b d", d=D)).then_inc(s_zero, 16)
            sp.dma_start(wgu_s[:, :], wgu).then_inc(s_we, 16)
            sp.dma_start(wd_s[:, :], wd).then_inc(s_we, 16)

            def load_group(c, q, g, s):
                src = XS[c][bass.ds(g * 512, 512), :].rearrange("(b p) d -> p b d", p=P)
                sp.dma_start(XG[s][:, :, :], src).then_inc(e_xg[s], 16)

            def store_group(c, q, g, s):
                sp.wait_ge(e_yc, q * GR + g + 1)
                dst = YS[c][bass.ds(g * 512, 512), :].rearrange("(b p) d -> p b d", p=P)
                sp.dma_start(dst, YG[s][:, :, :]).then_inc(e_st[s], 16)

            def ffn(f):
                for c in range(CH):
                    q = CH * f + c
                    sp.wait_ge(e_scat[c], (f + 1) * CT * K * 16)
                    for s in range(2):
                        if q:
                            sp.wait_ge(e_tx, q * GR)
                        load_group(c, q, s, s)
                    with sp.Fori(0, GR // 2 - 1) as i:
                        for s in range(2):
                            sp.wait_ge(e_tx, q * GR + 2 * i + s + 1)
                            load_group(c, q, 2 * i + s + 2, s)
                        for s in range(2):
                            store_group(c, q, 2 * i + s, s)
                    for s in range(2):
                        store_group(c, q, GR - 2 + s, s)

            ffn(0)

            sp.wait_ge(e_yc, CH * GR)
            for s in range(2):
                for par in range(2):
                    dst = KS[s][64 * par + 48:64 * par + 56, :].rearrange("p (a n) -> p a n", n=512)
                    sp.dma_start(dst, key_block[:, :].unsqueeze(1).to_broadcast([8, 8, 512])).then_inc(a_cdma, 16)
                    dst = KS[s][64 * par + 56:64 * par + 59, :].rearrange("p (a n) -> p a n", n=512)
                    sp.dma_start(dst, ones_b[0:3, :].unsqueeze(1).to_broadcast([3, 8, 512])).then_inc(a_cdma, 16)

            def step(b, what):
                c, a = b.plus(2), b.plus(1)
                if "A" in what:
                    sp.wait_ge(a_mtc, a.index + 1)
                    sp.dma_start(max_rows[a.slot], mrows[:, :]).then_inc(a_mw, 16)
                    sp.wait_ge(a_mw, 16 * (a.index + 1))
                    for par in range(2):
                        src = max_rows[a.slot].rearrange("(m h) n -> m h n", m=3)[:, par::2, :]
                        dst = QS[a.slot][64 * par + 56:64 * par + 59, :].rearrange("p (a n) -> p a n", n=512)
                        sp.dma_start(dst, src).then_inc(a_mr[a.slot], 16)
                if "P" in what:
                    sp.wait_ge(a_parts, 2 * (c.index + 1))
                    for n in range(2):
                        for m, part in enumerate((qk_hi[n], qk_mid[n], qk_lo[n])):
                            sp.dma_start(qk_parts[c.slot][3 * n + m], part[:, :]).then_inc(a_dw, 16)
                    sp.wait_ge(a_mbt, c.index + 1)
                    sp.dma_start(mask_rows[c.slot], mbt[:, :]).then_inc(a_dw, 16)
                    sp.wait_ge(a_dw, 7 * 16 * (c.index + 1))
                    if "B" in what:
                        sp.wait_ge(a_pv, NH * (b.index + 1))
                    for n, (stack, terms) in enumerate(((QS, (0, 0, 0, 1, 1, 2)), (KS, (0, 1, 2, 0, 1, 0)))):
                        for par in range(2):
                            for row, m in enumerate(terms):
                                src = qk_parts[c.slot][3 * n + m].rearrange("(h d) n -> d h n", d=HD)[:, par::2, :]
                                p0 = 64 * par + HD * row
                                dst = stack[c.slot][p0:p0 + HD, :].rearrange("p (a n) -> p a n", n=512)
                                sp.dma_start(dst, src).then_inc(a_stk[c.slot], 16)
                    for par in range(2):
                        src = mask_rows[c.slot].rearrange("(h j) n -> j h n", j=8)[:, par::2, :]
                        dst = QS[c.slot][64 * par + 48:64 * par + 56, :].rearrange("p (a n) -> p a n", n=512)
                        sp.dma_start(dst, src).then_inc(a_stk[c.slot], 16)

            for rounds, _, part in steps():
                if rounds is None:
                    for k, what in part:
                        step(Batch(k), what)
                else:
                    with sp.Fori(0, rounds) as i:
                        for k, what in part:
                            step(Batch(k, i), what)

            sp.wait_ge(a_pv, NH * NB)
            sp.dma_start(wgu_s[:, :], wgu).then_inc(s_we, 16)
            sp.dma_start(wd_s[:, :], wd).then_inc(s_we, 16)
            ffn(1)
            for c in range(CH):
                sp.wait_ge(e_comb, (CH + c + 1) * CT)
                sp.dma_start(out[c * CT:(c + 1) * CT].rearrange("t p d -> p t d"),
                             X[:, c * CT:(c + 1) * CT, :]).then_inc(s_out, 16)
            sp.wait_ge(s_out, 16 * CH)

        @block.gpsimd
        def _(pool):
            ch = Chain(pool, pch)
            g = nc.gpsimd
            g.memset(zero_t, 0.0).then_inc(s_zt, 1)
            g.memset(eps_c[:, :], EPS)
            g.memset(ones_b[:, :], 1.0)
            g.memset(ones_f[:, :], 1.0)
            g.memset(identf[:, :], 0.0)
            g.memset(identb[:, :], 0.0)
            g.memset(block_diag[:, :, :], 0.0)
            g.memset(diag_sel[:, :, :], 0.0)
            g.memset(reset_e[:, :], 1.0)
            g.memset(pack[:, :], 0.0)
            ch.link(g.iota(iota_e[:, :], pattern=[[1, E]], base=0, channel_multiplier=0,
                           allow_small_or_imprecise_dtypes=True))
            g.iota(iota_p[:, :], pattern=[[0, 1]], base=0, channel_multiplier=1, allow_small_or_imprecise_dtypes=True)
            for r in range(4):
                ch.link(g.affine_select(out=pack[:, :], in_=pack[:, :], compare_op=ALU.not_equal, fill=float(32 ** r),
                                        base=-r, pattern=[[-4, GR]], channel_multiplier=1))
            for half, op in enumerate((ALU.is_gt, ALU.is_ge)):
                sign = 1 if half else -1
                g.affine_select(out=half_sel[:, half:half + 1], in_=ones_f[:, 0:1], compare_op=op, fill=0.0,
                                base=-64 * sign, pattern=[[0, 1]], channel_multiplier=sign)
            for m in (identf, identb):
                g.affine_select(out=m[:, :], in_=m[:, :], compare_op=ALU.not_equal, fill=1.0, base=0,
                                pattern=[[-1, P]], channel_multiplier=1)
            g.affine_select(out=tri[:, :], in_=ones_b[:, 0:P], compare_op=ALU.is_gt, fill=0.0, base=0,
                            pattern=[[1, P]], channel_multiplier=-1)
            v = reset_e[:, :].rearrange("p (e t) -> p e t", e=E)
            g.affine_select(out=v, in_=v, compare_op=ALU.not_equal, fill=0.0, base=0,
                            pattern=[[0, E], [1, 16]], channel_multiplier=0)
            ch.link(g.affine_select(out=key_block[:, :], in_=ones_b[0:8, :], compare_op=ALU.is_ge, fill=0.0,
                                    base=0, pattern=[[1, 512]], channel_multiplier=-BS))
            g.memset(block_diag[:, :, :], 1.0).then_inc(pch, 1)
            ch.n += 1
            pool.wait_ge(pch, ch.n)
            ch.link(g.affine_select(out=block_diag[:, :, :], in_=block_diag[:, :, :], compare_op=ALU.is_ge,
                                    fill=0.0, base=0, pattern=[[-HD, NH], [0, 8]], channel_multiplier=1))
            ch.link(g.affine_select(out=block_diag[:, :, :], in_=block_diag[:, :, :], compare_op=ALU.is_ge,
                                    fill=0.0, base=HD - 1, pattern=[[HD, NH], [0, 8]], channel_multiplier=-1))
            ch.link(g.affine_select(out=key_block[:, :], in_=key_block[:, :], compare_op=ALU.is_ge, fill=0.0,
                                    base=BS - 1, pattern=[[-1, 512]], channel_multiplier=BS))
            for half in range(2):
                part = diag_sel[64 * half:64 * half + 64, :, :]
                ch.link(g.affine_select(out=part, in_=part, compare_op=ALU.not_equal, fill=1.0, base=-half,
                                        pattern=[[-2, 4], [1, 8]], channel_multiplier=0))
            g.tensor_scalar(diag_bias[:, :, :], diag_sel[:, :, :], -1.0, BIG, ALU.add, ALU.mult).then_inc(s_cst, 1)

            def scatter(f, c):
                q = CH * f + c
                pool.wait_ge(f_pos, q + 1)
                if f == 0 and c == 0:
                    pool.wait_ge(s_zero, 16 * CH * (BLK // 16))
                if f:
                    pool.wait_ge(e_tx, CH * GR)
                for t in range(CT):
                    for k in range(K):
                        pool.indirect_dma_start(
                            XS[c], bass.IndirectOffsetOnAxis(ap=pos[c][:, k, t:t + 1], axis=0),
                            XN[:, c * CT + t, :], None).then_inc(e_scat[c], 16)

            def gather(f, c, tiles=range(CT)):
                q = CH * f + c
                if 0 in tiles:
                    for s in range(2):
                        pool.wait_ge(e_st[s], 16 * (q + 1) * (GR // 2))
                for t in tiles:
                    for k in range(K):
                        pool.indirect_dma_start(
                            G[c][t][:, k, :], None, YS[c],
                            bass.IndirectOffsetOnAxis(ap=pos[c][:, k, t:t + 1], axis=0)).then_inc(e_gat[c], 16)

            scatter(0, 0)
            scatter(0, 1)
            gather(0, 0)
            gather(0, 1, range(0, 4))

            pool.wait_ge(e_comb, CT)
            for s in range(2):
                last = g.memset(VA[s], 0.0)
            ch.link(last)
            for s in range(2):
                for half in range(2):
                    o = VA[s][:, :, :, 9 * half + 8:9 * half + 9].rearrange("p i h c -> p (i h) c")
                    last = g.tensor_scalar(o, ones_f[:, 0:4 * NH].unsqueeze(2), half_sel[:, half:half + 1], None, ALU.mult)
            ch.link(last)

            def values(b):
                pool.wait_ge(a_natc, 4 * (b.index + 1))
                pool.nop(nofuse=True)
                for i in range(4):
                    for half in range(2):
                        last = g.tensor_scalar(VA[b.slot][:, i, :, 9 * half:9 * half + 8], NAT[:, i, 2, :, :],
                                               half_sel[:, half:half + 1], None, ALU.mult)
                last.then_inc(a_va, 1)

            def parts(c):
                for n in range(2):
                    pool.wait_ge(a_rest, 2 * c.index + n + 1)
                    if n == 0 and (c.k >= 1):
                        pool.wait_ge(a_dw, 7 * 16 * c.index)
                    pool.nop(nofuse=True)
                    ch.link(g.tensor_copy(qk_mid[n][:, :], rest[n][:, :]))
                    g.tensor_tensor(qk_lo[n][:, :], rest[n][:, :], qk_mid[n][:, :], ALU.subtract).then_inc(a_parts, 1)

            def step(b, what):
                a, c, t = b.plus(1), b.plus(2), b.plus(-1)
                if "T" in what:
                    pool.wait_ge(t_kr, t.index + 1)
                    for i in range(4):
                        o = O[t.slot][:, :, i, :, 0:8]
                        kr = KR[:, i, :, :].unsqueeze(3).to_broadcast([P, NH, 8, HD])
                        g.tensor_tensor(o, o, kr, ALU.mult).then_inc(t_w, 1)
                if "A" in what:
                    if "T" in what:
                        pool.wait_ge(t_ao, t.index + 1)
                    values(a)
                if "P" in what:
                    parts(c)

            per = 2 * 2
            for rounds, _, part in steps():
                if rounds is None:
                    for k, what in part:
                        step(Batch(k), what)
                        if k < 0:
                            gather(0, 1, range(4, 8) if k == -2 else range(8, CT))
                else:
                    with pool.Fori(0, rounds) as i:
                        ch.enter(i, per)
                        for k, what in part:
                            step(Batch(k, i), what)
                        ch.leave(rounds)

            for c in range(CH):
                scatter(1, c)
            for c in range(CH):
                gather(1, c)

        @block.scalar
        def _(act):
            ch = Chain(act, ach)

            def copy(dst, src):
                return nc.scalar.activation(dst, src, ACT.Copy)

            def normalise(f, c):
                q = CH * f + c
                act.wait_ge(f_stat, q + 1)
                if q == 0:
                    act.wait_ge(s_cst, 1)
                nc.scalar.activation(rstd[:, :], mv[:, :, 1], ACT.Sqrt, bias=eps_c[:, :]).then_inc(f_sqrt, 1)
                for n in range(TG):
                    act.wait_ge(f_tx, q * TG + n + 1)
                    copy(XNT[:, (c * TG + n) * 512:(c * TG + n + 1) * 512], bank(4 + n % 2)).then_inc(f_xnt, 1)

            def shared(f):
                for g in range(CH * TG):
                    for j in range(4):
                        n = 4 * (CH * TG * f + g) + j
                        act.wait_ge(h_g, n + 1)
                        if n >= 2:
                            act.wait_ge(h_m, n - 1)
                        nc.scalar.activation(SG[j % 2][:, :], bank(j % 2), ACT.Silu).then_inc(h_s, 1)
                        if 4 * g + j in (3, 3 + PIECES):
                            act.wait_ge(f_lm, CH * f + (4 * g + j) // PIECES + 1)
                            nc.scalar.activation(EX, L, ACT.Exp).then_inc(f_ex, 1)

            def experts(f, c):
                q = CH * f + c

                def xt(g, s):
                    act.wait_ge(e_tx, q * GR + g + 1)
                    copy(XT[s][:, :], bank(4)).then_inc(e_xt, 1)

                def silu(g, s):
                    act.wait_ge(e_gu, q * GR + g + 1)
                    v = banks[:, 2 * s:2 * s + 2, :].rearrange("p a (b c) -> p (a b) c", c=256)
                    o = SG[s][:, :].rearrange("p (b c) -> p b c", b=4)
                    nc.scalar.activation(o, v[:, :, 0:128], ACT.Silu).then_inc(e_s, 1)

                def y(g, s):
                    act.wait_ge(e_y, q * GR + g + 1)
                    yg = YG[s][:, :, :].rearrange("p b d -> p (b d)")
                    copy(yg, bank(6 + s)).then_inc(e_yc, 1)

                def pair(i):
                    silu(2 * i, 0)
                    silu(2 * i + 1, 1)
                    xt(2 * i + 2, 0)
                    xt(2 * i + 3, 1)
                    for s in range(2):
                        if q or not (isinstance(i, int) and i == 0):
                            act.wait_ge(e_st[s], 16 * (q * (GR // 2) + i))
                        y(2 * i + s, s)

                xt(0, 0)
                xt(1, 1)
                pair(0)
                with act.Fori(1, GR // 2 - 1) as i:
                    pair(i)
                silu(GR - 2, 0)
                silu(GR - 1, 1)
                for s in range(2):
                    act.wait_ge(e_st[s], 16 * ((q + 1) * (GR // 2) - 1))
                    y(GR - 2 + s, s)

            def tail_copy(t):
                act.wait_ge(t_at, t.index + 1)
                copy(AOT[:, :], bank(6)).then_inc(t_atc, 1)

            def probs(b, h, n):
                for j in range(AH):
                    act.wait_ge(a_s, AH * (n + h) + j + 1)
                    if j == 0 and (h >= 2 or b.k >= 1):
                        act.wait_ge(a_pv, n + h - 1)
                    nc.scalar.activation(PT[h % 2][:, 512 * j:512 * (j + 1)], bank(2 + j % 2),
                                         ACT.Exp, scale=SCALE).then_inc(a_e, 1)

            def take_ot(b, h, n):
                act.wait_ge(a_pv, n + h + 1)
                if b.k >= 1 or h >= 1:
                    act.wait_ge(a_ot, n + h)
                copy(OT, bank(5)).then_inc(a_otc, 1)

            def take_o(b, h, n):
                act.wait_ge(a_ot, n + h + 1)
                o = O[b.slot][:, h, :, :, :].rearrange("p i (j a) c -> p (i j) (a c)", a=2)
                copy(o, bank(4).rearrange("p (m c) -> p m c", c=32)[:, :, 0:18]).then_inc(a_oc, 1)

            def step(b, what):
                a, c, t = b.plus(1), b.plus(2), b.plus(-1)
                n = NH * b.index
                if b.k == 0:
                    act.wait_ge(e_comb, CH * CT)
                for h in range(NH + 2):
                    if "B" in what:
                        if h >= 2:
                            take_ot(b, h - 2, n)
                        if h < NH:
                            probs(b, h, n)
                        if h >= 2:
                            take_o(b, h - 2, n)
                    if h == 9 and "T" in what:
                        tail_copy(t)
                    if h == 13 and "A" in what:
                        act.wait_ge(a_mt, a.index + 1)
                        nc.scalar.activation(mrows[:, :], bank(6).bitcast(BF16)[0:3 * NH, 0:512], ACT.Copy).then_inc(a_mtc, 1)
                        act.wait_ge(a_pd, a.index + 1)
                        mx = MX[a.slot].rearrange("p i h j -> p (i h j)")
                        nc.scalar.activation(mx, mx, ACT.Exp, scale=SCALE)
                        e = ediag[a.slot][:, :, :]
                        nc.scalar.activation(e, e, ACT.Exp, scale=SCALE).then_inc(a_pe, 1)
                    if h == 14 and "P" in what:
                        act.wait_ge(a_stat, c.index + 1)
                        nc.scalar.activation(rstd[:, 0:4], mv[:, 0:4, 1], ACT.Sqrt, bias=eps_c[:, :]).then_inc(a_sqrt, 1)
                        act.wait_ge(a_tx, c.index + 1)
                        copy(xaT[:, :], bank(7)).then_inc(a_xt, 1)
                        for m in range(2):
                            act.wait_ge(a_qk, 2 * c.index + m + 1)
                            if m == 0 and c.k >= 1:
                                act.wait_ge(a_dw, 7 * 16 * c.index)
                            copy(qk_hi[m][:, :], bank(6 + m)).then_inc(a_hi, 1)
                        for i in range(4):
                            act.wait_ge(a_nat, 4 * c.index + i + 1)
                            if i == 0 and c.k >= 1:
                                act.wait_ge(a_va, c.index)
                            nat = NAT[:, i, :, :, :].rearrange("p a h d -> p (a h d)")
                            copy(nat, bank(6 + i % 2)[:, 0:384]).then_inc(a_natc, 1)
                        act.wait_ge(a_mn, c.index + 1)
                        mn = MN[c.slot].rearrange("p i h j -> p (i h j)")
                        copy(mn, bank(7)).then_inc(a_mnc, 1)

            normalise(0, 0)
            normalise(0, 1)
            shared(0)
            experts(0, 0)
            experts(0, 1)
            for rounds, _, part in steps():
                if rounds is None:
                    for k, what in part:
                        step(Batch(k), what)
                else:
                    with act.Fori(0, rounds) as i:
                        for k, what in part:
                            step(Batch(k, i), what)
            normalise(1, 0)
            normalise(1, 1)
            shared(1)
            experts(1, 0)
            experts(1, 1)

        @block.vector
        def _(dve):
            v = nc.vector
            ch = Chain(dve, dch)

            def normalise(f, c):
                q = CH * f + c
                if f == 0:
                    dve.wait_ge(s_x[c], 16)
                    if c == 0:
                        dve.wait_ge(s_cst, 1)
                        dve.wait_ge(s_w, 7 * 16)
                for t in range(CT):
                    last = v.bn_stats(stats[:, t, :], X[:, c * CT + t, :])
                ch.link(last)
                for t in range(CT):
                    last = v.bn_aggr(mv[:, t, :], stats[:, t, :])
                last.then_inc(f_stat, 1)
                dve.wait_ge(f_sqrt, q + 1)
                ch.link(v.reciprocal(rstd[:, :], rstd[:, :]))
                for n in range(TG):
                    for t in range(4 * n, 4 * n + 4):
                        last = v.tensor_scalar(XN[:, c * CT + t, :], X[:, c * CT + t, :], mv[:, t, 0:1],
                                               rstd[:, t:t + 1], ALU.subtract, ALU.mult)
                    last.then_inc(f_xn, 1)

            def route(f, c):
                q = CH * f + c
                dve.wait_ge(f_log, q + 1)
                ch.link(v.tensor_tensor(L, bank(6 + c).rearrange("p (t e) -> p t e", t=CT),
                                        rb_s[:, :].unsqueeze(1).to_broadcast([P, CT, E]), ALU.add))
                for t in range(CT):
                    last = v.max(top8[:, t, :], L[:, t, :])
                ch.link(last)
                yield
                for t in range(CT):
                    last = v.max_index(idx8[:, t, :], top8[:, t, :], L[:, t, :])
                ch.link(last)
                ch.link(v.tensor_copy(idxf[:, :, :], idx8[:, :, :]))
                yield
                v.tensor_tensor(L, L, top8[:, :, 0:1].to_broadcast([P, CT, E]), ALU.subtract).then_inc(f_lm, 1)
                v.tensor_tensor(OH[:, :, :, :],
                                iota_e[:, :].unsqueeze(1).unsqueeze(3).to_broadcast([P, K, E, CT]),
                                idxf[:, :, 0:K].rearrange("p t k -> p k t").unsqueeze(2).to_broadcast([P, K, E, CT]),
                                ALU.is_equal).then_inc(f_oh, 1)
                yield
                dve.wait_ge(f_ex, q + 1)
                ch.link(v.tensor_reduce(zsum[:, :], EX, AX, ALU.add))
                dve.wait_ge(f_oh, q + 1)
                ch.link(v.reciprocal(zsum[:, :], zsum[:, :]))
                ch.link(v.tensor_tensor(EX, EX, zsum[:, :].unsqueeze(2).to_broadcast([P, CT, E]), ALU.mult))
                yield
                for k in range(K):
                    last = v.tensor_tensor(OHP[:, k, :, :], OH[:, k, :, :], EX.rearrange("p t e -> p e t"), ALU.mult)
                ch.link(last)
                yield
                ch.link(v.tensor_reduce(topw[:, :, :].rearrange("p t k -> p k t"),
                                        OHP[:, :, :, :].rearrange("p k e t -> p k t e"), AX, ALU.add))
                ch.link(v.tensor_reduce(wsum[:, :], topw[:, :, :], AX, ALU.add))
                ch.link(v.tensor_scalar_max(wsum[:, :], wsum[:, :], 1e-12))
                ch.link(v.reciprocal(wsum[:, :], wsum[:, :]))
                ch.link(v.tensor_tensor(topw[:, :, :], topw[:, :, :],
                                        wsum[:, :].unsqueeze(2).to_broadcast([P, CT, K]), ALU.mult))
                ch.link(v.tensor_scalar(GW[c][:, :, :], topw[:, :, :], 0.5, None, ALU.mult))
                yield
                dve.wait_ge(f_cnt, q + 1)
                ch.link(v.tensor_copy(tot, bank(4)))
                ch.link(v.tensor_tensor_scan(scan, reset_e[:, :], tot, 0.0, ALU.mult, ALU.add))
                sc3 = scan.rearrange("p (e t) -> p e t", e=E)
                ch.link(v.tensor_scalar(nblk[:, :], sc3[:, :, CT - 1], 1.0 / P, 0.5 - 1.0 / (2 * P), ALU.mult, ALU.add))
                ch.link(v.tensor_scalar(nblk[:, :], nblk[:, :], ROUND, -ROUND, ALU.add, ALU.add))
                ch.link(v.tensor_tensor_scan(cumb[:, :], ones_b[:, 0:E], nblk[:, :], 0.0, ALU.mult, ALU.add))
                v.tensor_scalar(cmpb[:, :], cumb[:, :], iota_p[:, :], None, ALU.is_le)
                ch.link(v.tensor_tensor(begin[:, :], cumb[:, :], nblk[:, :], ALU.subtract))
                ch.link(v.tensor_reduce(eblk[:, :], cmpb[:, :], AX, ALU.add))
                v.tensor_scalar(eblk[:, :], eblk[:, :], float(E - 1), None, ALU.min).then_inc(f_eb, 1)
                ch.link(v.tensor_scalar(begin[:, :], begin[:, :], float(P), None, ALU.mult))
                yield
                v.tensor_tensor(place, bank(5), scan, ALU.add).then_inc(dch, 1)
                ch.n += 1
                dve.wait_ge(dch, ch.n)
                ch.link(v.tensor_tensor(place, place, tot, ALU.subtract))
                pl3 = place.rearrange("p (e t) -> p e t", e=E)
                ch.link(v.tensor_tensor(pl3, pl3, begin[:, :].unsqueeze(2).to_broadcast([P, E, CT]), ALU.add))
                for k in range(K):
                    last = v.tensor_tensor(OHP[:, k, :, :], OH[:, k, :, :], pl3, ALU.mult)
                ch.link(last)
                yield
                ch.link(v.tensor_reduce(posf[:, :, :], OHP[:, :, :, :].rearrange("p k e t -> p k t e"), AX, ALU.add))
                v.tensor_copy(pos[c][:, :, :], posf[:, :, :]).then_inc(f_pos, 1)
                yield
                dve.wait_ge(f_ebt, q + 1)
                v.tensor_copy(ids[c][:, :], bank(4)[0:1, 0:GR]).then_inc(f_ids, 1)
                yield

            def shared(f):
                base = CH * TG * f
                pieces = (None for c in range(CH) for _ in route(f, c))

                def finish(g):
                    dve.wait_ge(h_y, base + g + 1)
                    xg = X[:, 4 * g:4 * g + 4, :].rearrange("p t d -> p (t d)")
                    v.scalar_tensor_tensor(xg, bank(6), 0.5, xg, ALU.mult, ALU.add).then_inc(h_x, 1)

                for g in range(CH * TG):
                    for j in range(4):
                        n = 4 * (base + g) + j
                        dve.wait_ge(h_s, n + 1)
                        if j == 0 and g >= 2:
                            dve.wait_ge(h_y, base + g - 1)
                        v.tensor_tensor(SHT[g % 2][:, j, :], SG[j % 2][:, :], bank(2 + j % 2), ALU.mult).then_inc(h_m, 1)
                        next(pieces, None)
                    if g:
                        finish(g - 1)
                finish(CH * TG - 1)

            def experts(f, c):
                q = CH * f + c

                def mul(g, s):
                    dve.wait_ge(e_s, q * GR + g + 1)
                    u = banks[:, 2 * s:2 * s + 2, :].rearrange("p a (b c) -> p (a b) c", c=256)
                    v.tensor_tensor(HG[s][:, :, :], SG[s][:, :].rearrange("p (b c) -> p b c", b=4), u[:, :, 128:256],
                                    ALU.mult).then_inc(e_h, 1)

                def ht(g, s):
                    dve.wait_ge(e_th, q * GR + g + 1)
                    v.tensor_copy(HT[s][:, :], bank(5)).then_inc(e_ht, 1)

                with dve.Fori(0, GR // 2) as i:
                    mul(2 * i, 0)
                    mul(2 * i + 1, 1)
                    ht(2 * i, 0)
                    ht(2 * i + 1, 1)

            def combine(f, c):
                q = CH * f + c
                dve.wait_ge(e_gat[c], (f + 1) * CT * K * 16)
                for t0 in range(0, CT, 4):
                    for k in range(K):
                        for t in range(t0, t0 + 4):
                            xt = X[:, c * CT + t, :]
                            last = v.scalar_tensor_tensor(xt, G[c][t][:, k, :], GW[c][:, t, k:k + 1], xt, ALU.mult, ALU.add)
                            if k == K - 1:
                                last.then_inc(e_comb, 1)
                        if k < K - 1:
                            ch.link(last)

            BJ = [P, 4, NH, 8]

            def tail1(t):
                o, s = O[t.slot], t.slot
                dve.wait_ge(a_oc, NH * (t.index + 1))
                dve.wait_ge(a_pe, t.index + 1)
                v.tensor_reduce(lsum[:, :, :], o[:, :, :, :, 8].rearrange("p h i j -> p i h j"), AX, ALU.add)
                ch.link(v.scalar_tensor_tensor(dcor[:, :, :], adiag[s][:, :, :], 1.0, ediag[s][:, :, :],
                                               ALU.subtract, ALU.mult))
                ch.link(v.tensor_tensor(lsum[:, :, :], lsum[:, :, :], dcor[:, :, :], ALU.subtract))
                ch.link(v.reciprocal(rinv[:, :, :], lsum[:, :, :]))
                v.tensor_tensor(MX[s], MX[s], rinv[:, :, :].unsqueeze(3).to_broadcast(BJ), ALU.mult).then_inc(t_pm, 1)

            def tail2(t):
                dve.wait_ge(t_pt, t.index + 1)
                ch.link(v.tensor_reduce(bmax[:, :], bank(6).rearrange("p (b n) -> p b n", n=BS), AX, ALU.max))
                v.tensor_scalar(keepx[:, :].rearrange("p (b n) -> p b n", n=BS),
                                bmax[:, :].unsqueeze(2).to_broadcast([P, 8, BS]), THRESH, None, ALU.is_gt).then_inc(t_kx, 1)

            def tail3(t):
                s = t.slot
                dve.wait_ge(t_kn, t.index + 1)
                v.tensor_tensor(KR, bank(7).rearrange("p (i h j) -> p i h j", i=4, h=NH),
                                rinv[:, :, :].unsqueeze(3).to_broadcast(BJ), ALU.mult).then_inc(t_kr, 1)
                dve.wait_ge(t_kr, t.index + 1)
                ch.link(v.tensor_tensor(tmp, KR, AL[s], ALU.mult))
                ch.link(v.tensor_tensor(tmp, tmp, diag_sel[:, :, :].unsqueeze(2).to_broadcast(BJ), ALU.mult))
                ch.link(v.tensor_reduce(dcor[:, :, :], tmp, AX, ALU.add))
                ch.link(v.tensor_tensor(dcor[:, :, :], rinv[:, :, :], dcor[:, :, :], ALU.subtract))
                ch.link(v.tensor_tensor(dcor[:, :, :], dcor[:, :, :], ediag[s][:, :, :], ALU.mult))
                for half in range(2):
                    ps = slice(64 * half, 64 * half + 64)
                    last = v.tensor_tensor(tmp[ps, :, :, :], VA[s][ps, :, :, 9 * half:9 * half + 8],
                                           dcor[ps, :, :].unsqueeze(3).to_broadcast([64, 4, NH, HD]), ALU.mult)
                ch.mark(last)

            def tail4(t):
                for i in range(4):
                    dve.wait_ge(t_w, 4 * t.index + i + 1)
                    last = v.tensor_reduce(AO[:, i, :, :], O[t.slot][:, :, i, :, 0:8].rearrange("p h j d -> p h d j"),
                                           AX, ALU.add)
                ch.link(last)
                v.tensor_tensor(AO, AO, tmp, ALU.add).then_inc(t_ao, 1)

            def tail5(t):
                dve.wait_ge(t_op, t.index + 1)
                xg = X[:, bass.ds(4 * t.index, 4), :].rearrange("p t d -> p (t d)")
                v.tensor_tensor(xg, xg, bank(7), ALU.add).then_inc(t_x, 1)

            def maxima(a, h):
                for i in range(4):
                    n = 4 * h + i
                    dve.wait_ge(a_a, 4 * NH * a.index + n + 1)
                    v.tensor_reduce(MX[a.slot][:, i, h, :], bank(n % 2).rearrange("p (b n) -> p b n", n=BS), AX,
                                    ALU.max).then_inc(a_ar, 1)

            def rows(a):
                s = a.slot
                dve.wait_ge(a_mnc, a.index + 1)
                dve.wait_ge(a_ar, 4 * NH * (a.index + 1))
                v.tensor_tensor(tmp, diag_bias[:, :, :].unsqueeze(2).to_broadcast(BJ),
                                sdiag[s][:, :, :].unsqueeze(3).to_broadcast(BJ), ALU.add)
                v.tensor_scalar(AL[s], MN[s], -1.0, None, ALU.is_ge)
                ch.link(v.tensor_tensor(MX[s], MX[s], MN[s], ALU.add))
                ch.link(v.tensor_tensor(MX[s], MX[s], tmp, ALU.max))
                ch.link(v.tensor_reduce(mrow[:, :, :], MX[s], AX, ALU.max))
                v.tensor_scalar(mparts[:, :, 0, :], mrow[:, :, :], -1.0, None, ALU.mult)
                v.tensor_tensor(ediag[s][:, :, :], sdiag[s][:, :, :], mrow[:, :, :], ALU.subtract)
                ch.link(v.tensor_tensor(MX[s], MX[s], mrow[:, :, :].unsqueeze(3).to_broadcast(BJ), ALU.subtract))
                ch.link(v.scalar_tensor_tensor(mres[:, :, :], mrow[:, :, :], -1.0, mparts[:, :, 0, :],
                                               ALU.mult, ALU.subtract))
                ch.link(v.tensor_copy(mparts[:, :, 1, :], mres[:, :, :]))
                v.tensor_tensor(mparts[:, :, 2, :], mres[:, :, :], mparts[:, :, 1, :], ALU.subtract).then_inc(a_mp, 1)
                ch.link(v.tensor_tensor(tmp, AL[s], diag_sel[:, :, :].unsqueeze(2).to_broadcast(BJ), ALU.mult))
                v.tensor_reduce(adiag[s][:, :, :], tmp, AX, ALU.add).then_inc(a_pd, 1)

            def prepare(c):
                s = c.slot
                for j in range(4):
                    last = v.bn_stats(stats[:, j, :], X[:, bass.ds(4 * c.index + j, 1), :].rearrange("p a d -> p (a d)"))
                ch.link(last)
                dve.nop(nofuse=True)
                for j in range(4):
                    last = v.bn_aggr(mv[:, j, :], stats[:, j, :])
                last.then_inc(a_stat, 1)
                dve.wait_ge(a_sqrt, c.index + 1)
                ch.link(v.reciprocal(rstd[:, 0:4], rstd[:, 0:4]))
                for j in range(4):
                    last = v.tensor_scalar(xa[:, j, :], X[:, bass.ds(4 * c.index + j, 1), :].rearrange("p a d -> p (a d)"),
                                           mv[:, j, 0:1], rstd[:, j:j + 1], ALU.subtract, ALU.mult)
                last.then_inc(a_xa, 1)
                for m in range(2):
                    dve.wait_ge(a_hi, 2 * c.index + m + 1)
                    if c.k >= 1 and m == 0:
                        dve.wait_ge(a_parts, 2 * c.index)
                    v.tensor_tensor(rest[m][:, :], bank(6 + m), qk_hi[m][:, :], ALU.subtract).then_inc(a_rest, 1)
                    v.tensor_reduce(bsum[:, m, :], bank(6 + m).rearrange("p (b n) -> p b n", n=BS), AX,
                                    ALU.add).then_inc(a_sum, 1)
                dve.wait_ge(a_sum, 2 * (c.index + 1))
                ch.link(v.tensor_scalar(bsum[:, :, :], bsum[:, :, :], 1.0 / BS, None, ALU.mult))
                v.tensor_tensor(kmd[:, :, :], block_diag[:, :, :], bsum[:, 1:2, :].to_broadcast([P, NH, 8]),
                                ALU.mult).then_inc(a_kmd, 1)
                dve.wait_ge(a_natc, 4 * (c.index + 1))
                for i in range(4):
                    last = v.tensor_tensor(prod[:, i, :, :], NAT[:, i, 0, :, :], NAT[:, i, 1, :, :], ALU.mult)
                ch.link(last)
                v.tensor_reduce(sdiag[s][:, :, :], prod, AX, ALU.add).then_inc(a_sd, 1)
                dve.wait_ge(a_mb, c.index + 1)
                if c.k >= 1:
                    dve.wait_ge(a_dw, 7 * 16 * c.index)
                v.tensor_scalar(mbt[:, :].rearrange("p (b n) -> p b n", n=BS),
                                bank(6)[:, 0:8].unsqueeze(2).to_broadcast([P, 8, BS]),
                                THRESH * float(HD) ** 0.5, -BIG, ALU.is_le, ALU.mult).then_inc(a_mbt, 1)
                dve.wait_ge(a_sd, c.index + 1)

            def step(b, what):
                a, c, t = b.plus(1), b.plus(2), b.plus(-1)
                if "T" in what:
                    tail1(t)
                    tail2(t)
                    tail3(t)
                if "A" in what:
                    for h in range(4):
                        maxima(a, h)
                if "T" in what:
                    tail4(t)
                if "A" in what:
                    for h in range(4, 12):
                        maxima(a, h)
                if "T" in what:
                    tail5(t)
                if "A" in what:
                    for h in range(12, NH):
                        maxima(a, h)
                    rows(a)
                if "P" in what:
                    prepare(c)

            normalise(0, 0)
            normalise(0, 1)
            shared(0)
            experts(0, 0)
            experts(0, 1)
            combine(0, 0)
            dve.wait_ge(e_comb, CT)
            per = 2 * PER_DVE
            for rounds, _, part in steps():
                if rounds is None:
                    for k, what in part:
                        if k == 0:
                            combine(0, 1)
                            dve.wait_ge(e_comb, CH * CT)
                        step(Batch(k), what)
                else:
                    with dve.Fori(0, rounds) as i:
                        ch.enter(i, per)
                        for k, what in part:
                            step(Batch(k, i), what)
                        ch.leave(rounds)
            dve.wait_ge(t_x, NB)
            normalise(1, 0)
            normalise(1, 1)
            shared(1)
            experts(1, 0)
            experts(1, 1)
            combine(1, 0)
            combine(1, 1)

        @block.tensor
        def _(pe):
            mm, tr = nc.tensor.matmul, nc.tensor.transpose
            packed = [pe.alloc_register(f"packed{s}") for s in range(2)]

            def normalise(f, c):
                q = CH * f + c
                if q == 0:
                    pe.wait_ge(s_cst, 1)
                    pe.wait_ge(s_w, 7 * 16)
                if f == 1 and c == 0:
                    pe.wait_ge(t_x, NB)
                for n in range(TG):
                    pe.wait_ge(f_xn, q * TG + n + 1)
                    if n >= 2 or c:
                        pe.wait_ge(f_xnt, q * TG + n - 1)
                    for j in range(4):
                        last = tr(bank(4 + n % 2)[:, j * P:(j + 1) * P], XN[:, c * CT + 4 * n + j, :], identf[:, :])
                    last.then_inc(f_tx, 1)
                    if n >= 1:
                        logits(q, c, n - 1)
                logits(q, c, TG - 1).then_inc(f_log, 1)

            def logits(q, c, n):
                pe.wait_ge(f_xnt, q * TG + n + 1)
                for j in range(4):
                    t = 4 * n + j
                    last = mm(bank(6 + c)[:, t * E:(t + 1) * E], XNT[:, (c * CT + t) * P:(c * CT + t + 1) * P],
                              rw_s[:, :], start=True, stop=True)
                return last

            def counts(f, c):
                q = CH * f + c
                pe.wait_ge(f_oh, q + 1)
                if c:
                    pe.wait_ge(f_pos, q)
                    pe.wait_ge(f_ids, q)
                for k in range(K):
                    mm(bank(5), tri[:, :], OH[:, k, :, :].rearrange("p e t -> p (e t)"), start=k == 0, stop=k == K - 1)
                for k in range(K):
                    last = mm(bank(4), ones_b[:, 0:P], OH[:, k, :, :].rearrange("p e t -> p (e t)"),
                              start=k == 0, stop=k == K - 1)
                last.then_inc(f_cnt, 1)

            def block_experts(f, c):
                pe.wait_ge(f_eb, CH * f + c + 1)
                mm(bank(4)[0:1, 0:GR], eblk[:, :], pack[:, :], start=True, stop=True).then_inc(f_ebt, 1)

            def shared(f):
                base = CH * TG * f

                def gate_up(g, j):
                    n = 4 * (base + g) + j
                    xn = XNT[:, g * 512:(g + 1) * 512]
                    if n >= 2:
                        pe.wait_ge(h_m, n - 1)
                    mm(bank(j % 2), sg_s[:, j * P:(j + 1) * P], xn, start=True, stop=True)
                    mm(bank(2 + j % 2), su_s[:, j * P:(j + 1) * P], xn, start=True, stop=True).then_inc(h_g, 1)
                    m = 4 * g + j
                    if m % PIECES == 4 and m // PIECES < CH:
                        counts(f, m // PIECES)
                    if m % PIECES == 8 and m // PIECES < CH:
                        block_experts(f, m // PIECES)

                def down(g):
                    pe.wait_ge(h_m, 4 * (base + g + 1))
                    if g:
                        pe.wait_ge(h_x, base + g)
                    for t in range(4):
                        for j in range(4):
                            last = mm(bank(6)[:, t * P:(t + 1) * P], SHT[g % 2][:, j, t * P:(t + 1) * P],
                                      sd_s[:, j, :], start=j == 0, stop=j == 3)
                    last.then_inc(h_y, 1)

                for g in range(CH * TG):
                    gate_up(g, 0)
                    gate_up(g, 1)
                    if g:
                        down(g - 1)
                    gate_up(g, 2)
                    gate_up(g, 3)
                down(CH * TG - 1)

            def experts(f, c):
                q = CH * f + c
                if c == 0:
                    pe.wait_ge(s_we, 32 * (f + 1))
                    pe.wait_ge(f_ids, CH * (f + 1))
                if c == 0:
                    pe.wait_ge(h_x, CH * TG * (f + 1))

                def rows(g, i, s):
                    pe.wait_ge(e_xg[s], 16 * (q * (GR // 2) + i + 1))
                    if q or not (isinstance(g, int) and g == 0):
                        pe.wait_ge(e_xt, q * GR + g)
                    for j in range(4):
                        last = tr(bank(4)[:, j * P:(j + 1) * P], XG[s][:, j, :], identf[:, :])
                    last.then_inc(e_tx, 1)

                def gate_up(g, s, which):
                    pe.wait_ge(e_xt, q * GR + g + 1)
                    for j in range(4):
                        o = bank(2 * s + j // 2)[:, 256 * (j % 2):256 * (j % 2) + 256]
                        last = mm(o, XT[s][:, j * P:(j + 1) * P], wgu_s[:, bass.ds(which[j] * (2 * H), 2 * H)],
                                  start=True, stop=True)
                    last.then_inc(e_gu, 1)

                def turn(g, s):
                    pe.wait_ge(e_h, q * GR + g + 1)
                    if q or not (isinstance(g, int) and g == 0):
                        pe.wait_ge(e_ht, q * GR + g)
                    for j in range(4):
                        last = tr(bank(5)[:, j * P:(j + 1) * P], HG[s][:, j, :], identf[:, :])
                    last.then_inc(e_th, 1)

                def down(g, i, s, which):
                    pe.wait_ge(e_ht, q * GR + g + 1)
                    for j in range(4):
                        last = mm(bank(6 + s)[:, j * P:(j + 1) * P], HT[s][:, j * P:(j + 1) * P],
                                  wd_s[:, bass.ds(which[j] * D, D)], start=True, stop=True)
                    last.then_inc(e_y, 1)

                def fetch(i):
                    for s in range(2):
                        pe.reg_load(packed[s], ids[c][0:1, bass.ds(2 * i + s, 1)])

                def pair(i, more):
                    four = [pe.snap(packed[s], min_val=0, max_val=E ** 4 - 1) for s in range(2)]
                    which = [(four[s] >> (5 * j)) & (E - 1) for s in range(2) for j in range(4)]
                    if q or not (isinstance(i, int) and i == 0):
                        pe.wait_ge(e_yc, q * GR + 2 * i)
                    gate_up(2 * i, 0, which[0:4])
                    gate_up(2 * i + 1, 1, which[4:8])
                    if more:
                        fetch(i + 1)
                    turn(2 * i, 0)
                    if more:
                        rows(2 * i + 2, i + 1, 0)
                    turn(2 * i + 1, 1)
                    if more:
                        rows(2 * i + 3, i + 1, 1)
                    down(2 * i, i, 0, which[0:4])
                    down(2 * i + 1, i, 1, which[4:8])

                fetch(0)
                rows(0, 0, 0)
                rows(1, 0, 1)
                pair(0, True)
                with pe.Fori(1, GR // 2 - 1) as i:
                    pair(i, True)
                pair(GR // 2 - 1, False)

            def tail_p(t):
                pe.wait_ge(t_pm, t.index + 1)
                for i in range(4):
                    m = MX[t.slot][:, i, :, :].rearrange("p h j -> p (h j)")
                    last = tr(bank(6)[:, i * P:(i + 1) * P], m, identf[:, :])
                last.then_inc(t_pt, 1)

            def tail_k(t):
                pe.wait_ge(t_kx, t.index + 1)
                for i in range(4):
                    last = mm(bank(7)[:, i * P:(i + 1) * P], keepx[:, i * P:(i + 1) * P], identb[:, :], start=True, stop=True)
                last.then_inc(t_kn, 1)

            def tail_a(t):
                pe.wait_ge(t_ao, t.index + 1)
                for i in range(4):
                    o = AO[:, i, :, :].rearrange("p h d -> p (h d)")
                    last = tr(bank(6)[:, i * P:(i + 1) * P], o, identf[:, :])
                last.then_inc(t_at, 1)

            def tail_o(t):
                pe.wait_ge(t_atc, t.index + 1)
                for i in range(4):
                    last = mm(bank(7)[:, i * P:(i + 1) * P], AOT[:, i * P:(i + 1) * P], wo_s[:, :], start=True, stop=True)
                last.then_inc(t_op, 1)

            def max_scores(a, n):
                h, i = n // 4, n % 4
                p0 = 64 * (h % 2)
                o = (h // 2) * 512
                if a.k >= 1 or n >= 2:
                    pe.wait_ge(a_ar, 4 * NH * a.index + n - 1)
                mm(bank(n % 2), QS[a.slot][p0:p0 + 48, o + i * P:o + (i + 1) * P], KS[a.slot][p0:p0 + 48, o:o + 512],
                   start=True, stop=True).then_inc(a_a, 1)

            def scores(b, h, j):
                p0 = 64 * (h % 2)
                o = (h // 2) * 512
                n = AH * h + j
                if b.k >= 1 or n >= 2:
                    pe.wait_ge(a_e, AH * NH * b.index + n - 1)
                mm(bank(2 + n % 2), KS[b.slot][p0:p0 + 59, o + j * P:o + (j + 1) * P], QS[b.slot][p0:p0 + 59, o:o + 512],
                   start=True, stop=True).then_inc(a_s, 1)

            def sums(b, h, j):
                pe.wait_ge(a_e, AH * (NH * b.index + h) + j + 1)
                if j == 0 and (b.k >= 1 or h >= 1):
                    pe.wait_ge(a_otc, NH * b.index + h)
                last = mm(bank(5)[32 * j:32 * j + 32, :], VA[b.slot][:, j, h, :], PT[h % 2][:, 512 * j:512 * (j + 1)],
                          start=True, stop=True)
                if j == AH - 1:
                    last.then_inc(a_pv, 1)

            def turn_sums(b, h):
                pe.wait_ge(a_otc, NH * b.index + h + 1)
                if b.k >= 1 or h >= 1:
                    pe.wait_ge(a_oc, NH * b.index + h)
                for i in range(4):
                    last = tr(bank(4)[:, i * P:(i + 1) * P], OT[:, i * P:(i + 1) * P], identf[:, :])
                last.then_inc(a_ot, 1)

            def max_turn(a):
                pe.wait_ge(a_mp, a.index + 1)
                pe.nop(nofuse=True)
                for i in range(4):
                    m = mparts[:, i, :, :].rearrange("p m h -> p (m h)")
                    last = tr(bank(6).bitcast(BF16)[0:3 * NH, i * P:(i + 1) * P], m, identb[:, :])
                last.then_inc(a_mt, 1)

            def prepare(c, after_max):
                pe.wait_ge(a_xa, c.index + 1)
                for j in range(4):
                    last = tr(bank(7)[:, j * P:(j + 1) * P], xa[:, j, :], identf[:, :])
                last.then_inc(a_tx, 1)
                pe.wait_ge(a_xt, c.index + 1)
                if after_max is not None:
                    pe.wait_ge(a_mtc, after_max.index + 1)
                for m in range(2):
                    mm(bank(6 + m), wqkv_s[:, m * D:(m + 1) * D], xaT[:, :], start=True, stop=True).then_inc(a_qk, 1)
                for i in range(4):
                    if i < 2:
                        pe.wait_ge(a_sum, 2 * c.index + i + 1)
                    else:
                        pe.wait_ge(a_natc, 4 * c.index + i - 1)
                    mm(bank(6 + i % 2)[:, 0:384], xaT[:, i * P:(i + 1) * P], wqkv_s[:, :], start=True, stop=True).then_inc(a_nat, 1)
                pe.wait_ge(a_natc, 4 * (c.index + 1))
                pe.wait_ge(a_kmd, c.index + 1)
                mm(bank(6)[:, 0:8], kmd[:, :, :].rearrange("p h j -> p (h j)"), bsum[:, 0, :], start=True,
                   stop=True).then_inc(a_mb, 1)
                pe.wait_ge(a_mbt, c.index + 1)
                for i in range(4):
                    last = mm(bank(7)[:, i * P:(i + 1) * P], mbt[:, i * P:(i + 1) * P], identb[:, :], start=True, stop=True)
                last.then_inc(a_mn, 1)

            def step(b, what):
                a, c, t = b.plus(1), b.plus(2), b.plus(-1)
                if "B" in what:
                    pe.wait_ge(a_mr[b.slot], 32 * (b.round + 1))
                    pe.wait_ge(a_va, b.index + 1)
                for h in range(NH + 2):
                    B, A = "B" in what, "A" in what and 4 <= h < 12
                    if A and h == 4:
                        pe.wait_ge(a_stk[a.slot], STK * (a.round + 1))
                        if a.k == 0:
                            pe.wait_ge(a_cdma, 8 * 16)
                    for m in range(AH + 1):
                        if B and h < NH and m < AH:
                            scores(b, h, m)
                        if A and m < AH:
                            max_scores(a, 8 * (h - 4) + 2 * m)
                        if B and 1 <= h <= NH and m >= 1:
                            sums(b, h - 1, m - 1)
                        if B and h >= 2 and m == AH - 1:
                            turn_sums(b, h - 2)
                        if A and m < AH:
                            max_scores(a, 8 * (h - 4) + 2 * m + 1)
                    if "T" in what:
                        {2: tail_p, 3: tail_k, 7: tail_a, 9: tail_o}.get(h, lambda t: None)(t)
                    if h == 13 and "A" in what:
                        max_turn(a)
                    if h == 14 and "P" in what:
                        if "T" in what:
                            pe.wait_ge(t_x, t.index + 1)
                        prepare(c, a if "A" in what else None)

            normalise(0, 0)
            normalise(0, 1)
            shared(0)
            experts(0, 0)
            experts(0, 1)
            pe.wait_ge(e_yc, CH * GR)
            for rounds, _, part in steps():
                if rounds is None:
                    for k, what in part:
                        step(Batch(k), what)
                else:
                    with pe.Fori(0, rounds) as i:
                        for k, what in part:
                            step(Batch(k, i), what)
            normalise(1, 0)
            normalise(1, 1)
            shared(1)
            experts(1, 0)
            experts(1, 1)


PER_DVE = 22


def kernel(**inputs):
    import numpy as np
    import concourse.bacc as bacc
    from concourse.bass_utils import run_bass_kernel_spmd

    def lay(a):
        return np.ascontiguousarray(a)

    g = {k.replace("L0_", ""): np.asarray(v) for k, v in inputs.items()}
    arrays = {
        "x": lay(g["attn_x"].reshape(-1, P, D)),
        "wqkv": lay(np.concatenate([g["attn_wq"].T, g["attn_wk"].T, g["attn_wv"].T], axis=1)),
        "wo": lay(g["attn_wo"].T),
        "rw": lay(g["ffn_router_w"].T),
        "rb": lay(g["ffn_router_bias"]),
        "wgu": lay(np.concatenate([g["ffn_gate_w"].transpose(2, 0, 1), g["ffn_up_w"].transpose(2, 0, 1)],
                                  axis=2).reshape(D, E * 2 * H)),
        "wd": lay(g["ffn_down_w"].transpose(2, 0, 1).reshape(H, E * D)),
        "sg": lay(g["ffn_sgate_w"].T),
        "su": lay(g["ffn_sup_w"].T),
        "sd": lay(g["ffn_sdown_w"].T.reshape(4, P, D).transpose(1, 0, 2)),
    }
    nc = bacc.Bacc("TRN2", target_bir_lowering=False, num_devices=1)
    aps = [nc.dram_tensor(n, a.shape, FP32, kind="ExternalInput").ap() for n, a in arrays.items()]
    out = nc.dram_tensor("out", arrays["x"].shape, FP32, kind="ExternalOutput").ap()
    nc.disable_value_cache = True
    build(nc, *aps, out)
    r = run_bass_kernel_spmd(nc, [arrays], core_ids=[0])
    return r.results[0]["out"].reshape(g["attn_x"].shape)
```

```python
import concourse.bass as bass
from concourse import mybir
from contextlib import ExitStack

FP32 = mybir.dt.float32
BF16 = mybir.dt.bfloat16
U32 = mybir.dt.uint32
I32 = mybir.dt.int32
ALU = mybir.AluOpType
ACT = mybir.ActivationFunctionType
AX = mybir.AxisListType.X

P = 128
D = 128
NH, HD = 16, 8
BS = 64
SCALE = float(HD) ** -0.5
THRESH = 0.01
PIECES = 10
BIG = 1.0e30
E, K, H, HS = 32, 4, 128, 512
EPS = 1e-5
ROUND = 12582912.0


class Chain:

    def __init__(self, engine, sem):
        self.engine, self.sem, self.n, self.off = engine, sem, 0, 0

    def mark(self, ins):
        ins.then_inc(self.sem, 1)
        self.n += 1

    def link(self, ins):
        self.mark(ins)
        self.engine.wait_ge(self.sem, self.n + self.off)

    def enter(self, i, per):
        self.start, self.per, self.off = self.n, per, i * per

    def leave(self, rounds):
        assert self.n - self.start == self.per, (self.n - self.start, self.per)
        self.n, self.off = self.start + rounds * self.per, 0


class Batch:

    def __init__(self, k, i=0):
        self.k, self.i = k, i
        self.index, self.slot, self.round = k + 2 * i, k % 2, k // 2 + i

    def plus(self, d):
        return Batch(self.k + d, self.i)


def build(nc, x, wqkv, wo, rw, rb, wgu, wd, sg, su, sd, out):
    T = x.shape[0]
    NB = T // 4
    CH = 2
    CT = T // CH
    TG = CT // 4
    BLK = (CT * P * K + E * (P - 1)) // P
    BLK += -BLK % 8
    GR = BLK // 4

    ctx = ExitStack()
    with ctx:
        def sb(name, shape, dt=FP32):
            return ctx.enter_context(nc.sbuf_tensor(name, shape, dt))

        def sem(name):
            return ctx.enter_context(nc.semaphore(name))

        XS = [nc.dram_tensor(f"rows_by_expert{c}", [BLK * P, D], FP32).ap() for c in range(CH)]
        YS = [nc.dram_tensor(f"results_by_expert{c}", [BLK * P, D], FP32).ap() for c in range(CH)]
        qk_parts = [nc.dram_tensor(f"qk_parts{s}", [6, NH * HD, 512], BF16).ap() for s in range(2)]
        mask_rows = [nc.dram_tensor(f"mask_rows{s}", [NH * 8, 512], BF16).ap() for s in range(2)]
        max_rows = [nc.dram_tensor(f"max_rows{s}", [3 * NH, 512], BF16).ap() for s in range(2)]

        X = sb("X", [P, T, D])
        wqkv_s = sb("wqkv_s", [P, 3 * D])
        wo_s = sb("wo_s", [P, D])
        rw_s = sb("rw_s", [P, E])
        rb_s = sb("rb_s", [P, E])
        wgu_s = sb("wgu_s", [P, E * 2 * H])
        wd_s = sb("wd_s", [P, E * D])
        sg_s = sb("sg_s", [P, HS])
        su_s = sb("su_s", [P, HS])
        sd_s = sb("sd_s", [P, 4, D])
        identf = sb("identf", [P, P])
        identb = sb("identb", [P, P], BF16)
        tri = sb("tri", [P, P], BF16)
        ones_b = sb("ones_b", [P, 512], BF16)
        iota_e = sb("iota_e", [P, E])
        iota_p = sb("iota_p", [P, 1])
        block_diag = sb("block_diag", [P, NH, 8])
        diag_sel = sb("diag_sel", [P, 4, 8])
        diag_bias = sb("diag_bias", [P, 4, 8])
        key_block = sb("key_block", [8, 512], BF16)
        eps_c = sb("eps_c", [P, 1])
        half_sel = sb("half_sel", [P, 2])
        ones_f = sb("ones_f", [P, 4 * NH])
        reset_e = sb("reset_e", [P, E * 16])

        arena_g = sb("arena_g", [P, CT * K * D])
        arena_n = sb("arena_n", [P, T * D])
        arena_o = sb("arena_o", [P, 2 * NH * 4 * 72])
        HC = CT // 2
        G0 = arena_g[:, :].rearrange("p (t k d) -> p t k d", t=CT, k=K)
        G1 = [m[:, 0:HC * K * D].rearrange("p (t k d) -> p t k d", t=HC, k=K) for m in (wd_s, arena_o)]
        G = [[G0[:, t] for t in range(CT)], [G1[t // HC][:, t % HC] for t in range(CT)]]
        stacks = wgu_s[:, :].bitcast(BF16)
        QS = [stacks[:, 4096 * s:4096 * (s + 1)] for s in range(2)]
        KS = [stacks[:, 8192 + 4096 * s:8192 + 4096 * (s + 1)] for s in range(2)]
        PT = [wd_s[:, 2048 * s:2048 * (s + 1)] for s in range(2)]
        XNT = arena_n
        XN = arena_o[:, 0:T * D].rearrange("p (t d) -> p t d", t=T)
        O = [arena_o[:, 4608 * s:4608 * (s + 1)].rearrange("p (h i j c) -> p h i j c", h=NH, i=4, j=8)
             for s in range(2)]

        class Carve:

            def __init__(self, arena, at):
                self.arena, self.at = arena, at

            def take(self, words, dt=FP32):
                piece = self.arena[:, self.at:self.at + words]
                self.at += words
                assert self.at <= self.arena.shape[1]
                return piece if dt == FP32 else piece.bitcast(dt)

        beside_xn = Carve(arena_o, T * D)
        in_g = Carve(arena_g, 0)
        work_g = Carve(arena_g, 0)
        zero_t = work_g.take(2048)
        in_n = Carve(arena_n, 0)

        stats = sb("stats", [P, CT, 6])
        mv = sb("mv", [P, CT, 2])
        rstd = sb("rstd", [P, CT])
        arena_r = sb("arena_r", [P, 5 * 512])
        L = arena_r[:, 0:512].rearrange("p (t e) -> p t e", t=CT)
        EX = arena_r[:, 512:1024].rearrange("p (t e) -> p t e", t=CT)
        tot = arena_r[:, 1024:1536]
        scan = arena_r[:, 1536:2048]
        place = arena_r[:, 2048:2560]
        OH = beside_xn.take(K * E * CT // 2, BF16).rearrange("p (k e t) -> p k e t", k=K, e=E)
        OHP = work_g.take(K * E * CT).rearrange("p (k e t) -> p k e t", k=K, e=E)
        top8 = sb("top8", [P, CT, 8])
        idx8 = sb("idx8", [P, CT, 8], U32)
        idxf = sb("idxf", [P, CT, 8])
        topw = sb("topw", [P, CT, K])
        zsum = sb("zsum", [P, CT])
        wsum = sb("wsum", [P, CT])
        GW = [sb(f"GW{c}", [P, CT, K]) for c in range(CH)]
        posf = sb("posf", [P, K, CT])
        pack = sb("pack", [P, GR])
        pos = [sb(f"pos{c}", [P, K, CT], U32) for c in range(CH)]
        nblk = sb("nblk", [P, E])
        cumb = sb("cumb", [P, E])
        begin = sb("begin", [P, E])
        cmpb = sb("cmpb", [P, E])
        eblk = sb("eblk", [P, 1])
        ids = [sb(f"ids{c}", [1, GR], I32) for c in range(CH)]
        XG = [sb("XG0", [P, 512])[:, :], beside_xn.take(512)]
        XG = [g.rearrange("p (b d) -> p b d", b=4) for g in XG]
        XT = [sb("XT0", [P, 512]), beside_xn.take(512)]
        SG = [sb("SG0", [P, 512]), beside_xn.take(512)]
        HG = [sb("HG0", [P, 512])[:, :], beside_xn.take(512)]
        HG = [g.rearrange("p (b d) -> p b d", b=4) for g in HG]
        HT = [sb(f"HT{s}", [P, 512]) for s in range(2)]
        YG = [sb(f"YG{s}", [P, 4, D]) for s in range(2)]
        SHT = [work_g.take(2048).rearrange("p (j n) -> p j n", j=4) for s in range(2)]

        xa = XG[0]
        xaT = XT[0]
        qk_hi, qk_mid, qk_lo = ([in_g.take(256, BF16) for n in range(2)] for _ in range(3))
        rest = [HT[0], HT[1]]
        bsum = sb("bsum", [P, 2, 8])
        kmd = in_g.take(128).rearrange("p (h j) -> p h j", h=NH)
        mbt = in_g.take(256, BF16)
        NAT = in_g.take(4 * 384).rearrange("p (i a h d) -> p i a h d", i=4, a=3, h=NH)
        prod = HG[0][:, :, :].rearrange("p a (h d) -> p a h d", h=NH)
        MN, MX, AL = ([in_n.take(512).rearrange("p (i h j) -> p i h j", i=4, h=NH) for s in range(2)] for _ in range(3))
        tmp = in_n.take(512).rearrange("p (i h j) -> p i h j", i=4, h=NH)
        sdiag = [sb(f"sdiag{s}", [P, 4, NH]) for s in range(2)]
        ediag = [sb(f"ediag{s}", [P, 4, NH]) for s in range(2)]
        adiag = [sb(f"adiag{s}", [P, 4, NH]) for s in range(2)]
        mrow = sb("mrow", [P, 4, NH])
        mres = sb("mres", [P, 4, NH])
        mparts = sb("mparts", [P, 4, 3, NH], BF16)
        mrows = sb("mrows", [3 * NH, 512], BF16)
        lsum = sb("lsum", [P, 4, NH])
        rinv = sb("rinv", [P, 4, NH])
        dcor = sb("dcor", [P, 4, NH])
        bmax = sb("bmax", [P, 8])
        keepx = in_g.take(256, BF16)
        KR = YG[0][:, :, :].rearrange("p i (h j) -> p i h j", h=NH)
        AO = YG[1][:, :, :].rearrange("p i (h d) -> p i h d", h=NH)
        AOT = SG[0]
        OT = arena_r[:, 0:512]
        VA = [in_g.take(4 * NH * 32).rearrange("p (i h c) -> p i h c", i=4, h=NH) for s in range(2)]

        banks = ctx.enter_context(nc.psum_tensor("banks", [P, 8, 512], FP32))

        def bank(n):
            return banks[:, n, :]

        s_x = [sem(f"s_x{c}") for c in range(CH)]
        s_w = sem("s_w")
        s_we = sem("s_we")
        s_zero = sem("s_zero")
        s_cst = sem("s_cst")
        s_zt = sem("s_zt")
        dch = sem("dve_chain")
        ach = sem("act_chain")
        pch = sem("pool_chain")
        f_stat = sem("f_stat")
        f_sqrt = sem("f_sqrt")
        f_xn = sem("f_xn")
        f_tx = sem("f_tx")
        f_xnt = sem("f_xnt")
        f_log = sem("f_log")
        f_lm = sem("f_lm")
        f_ex = sem("f_ex")
        f_oh = sem("f_oh")
        f_cnt = sem("f_cnt")
        f_eb = sem("f_eb")
        f_ebt = sem("f_ebt")
        f_ids = sem("f_ids")
        f_pos = sem("f_pos")
        h_g = sem("h_g")
        h_s = sem("h_s")
        h_m = sem("h_m")
        h_y = sem("h_y")
        h_x = sem("h_x")
        e_scat = [sem(f"e_scat{c}") for c in range(CH)]
        e_xg = [sem(f"e_xg{s}") for s in range(2)]
        e_tx = sem("e_tx")
        e_xt = sem("e_xt")
        e_gu = sem("e_gu")
        e_s = sem("e_s")
        e_h = sem("e_h")
        e_th = sem("e_th")
        e_ht = sem("e_ht")
        e_y = sem("e_y")
        e_yc = sem("e_yc")
        e_st = [sem(f"e_st{s}") for s in range(2)]
        e_gat = [[sem(f"e_gat{c}_{n}") for n in range(TG)] for c in range(CH)]
        e_comb = sem("e_comb")
        a_va = sem("a_va")
        a_cdma = sem("a_cdma")
        a_stat = sem("a_stat")
        a_sqrt = sem("a_sqrt")
        a_xa = sem("a_xa")
        a_tx = sem("a_tx")
        a_xt = sem("a_xt")
        a_qk = sem("a_qk")
        a_hi = sem("a_hi")
        a_rest = sem("a_rest")
        a_sum = sem("a_sum")
        a_parts = sem("a_parts")
        a_nat = sem("a_nat")
        a_natc = sem("a_natc")
        a_sd = sem("a_sd")
        a_kmd = sem("a_kmd")
        a_mb = sem("a_mb")
        a_mbt = sem("a_mbt")
        a_mn = sem("a_mn")
        a_mnc = sem("a_mnc")
        a_dw = sem("a_dw")
        a_stk = [sem(f"a_stk{s}") for s in range(2)]
        a_a = sem("a_a")
        a_ar = sem("a_ar")
        a_mp = sem("a_mp")
        a_mt = sem("a_mt")
        a_mtc = sem("a_mtc")
        a_pd = sem("a_pd")
        a_pe = sem("a_pe")
        a_mw = sem("a_mw")
        a_mr = [sem(f"a_mr{s}") for s in range(2)]
        a_s = sem("a_s")
        a_e = sem("a_e")
        a_pv = sem("a_pv")
        a_otc = sem("a_otc")
        a_ot = sem("a_ot")
        a_oc = sem("a_oc")
        t_pm = sem("t_pm")
        t_pt = sem("t_pt")
        t_kx = sem("t_kx")
        t_kn = sem("t_kn")
        t_kr = sem("t_kr")
        t_w = sem("t_w")
        t_ao = sem("t_ao")
        t_at = sem("t_at")
        t_atc = sem("t_atc")
        t_op = sem("t_op")
        t_x = sem("t_x")
        s_out = sem("s_out")

        STK = 26 * 16
        AH = 4

        def steps():
            yield None, 0, [(-2, "P"), (-1, "AP"), (0, "BAP")]
            yield 2, 1, [(1, "TBAP"), (2, "TBAP")]
            yield None, 0, [(5, "TBAP"), (6, "TBA"), (7, "TB"), (8, "T")]

        EARLY = [range(CH * TG), range(TG)]
        LATE = range(TG, CH * TG)

        def piece_slot(f, c, k):
            if f == 0:
                return PIECES * c + k
            return k // 2 if c == 0 else PIECES // 2 + k

        block = ctx.enter_context(nc.Block())

        @block.sync
        def _(sp):
            for c in range(CH):
                sp.dma_start(X[:, c * CT:(c + 1) * CT, :], x[c * CT:(c + 1) * CT].rearrange("t p d -> p t d")).then_inc(s_x[c], 16)
            for dst, src in ((rw_s, rw), (rb_s, rb.rearrange("(a e) -> a e", a=1).to_broadcast([P, E])),
                             (sg_s, sg), (su_s, su), (wqkv_s, wqkv), (wo_s, wo)):
                sp.dma_start(dst[:, :], src).then_inc(s_w, 16)
            sp.dma_start(sd_s[:, :, :], sd).then_inc(s_w, 16)
            sp.wait_ge(s_zt, 1)
            for c in range(CH):
                for n in range(BLK // 16):
                    sp.dma_start(XS[c][n * 16 * P:(n + 1) * 16 * P, :].rearrange("(b p) d -> p b d", p=P),
                                 zero_t.rearrange("p (b d) -> p b d", d=D)).then_inc(s_zero, 16)
            sp.dma_start(wgu_s[:, :], wgu).then_inc(s_we, 16)
            sp.dma_start(wd_s[:, :], wd).then_inc(s_we, 16)

            def load_group(c, q, g, s):
                src = XS[c][bass.ds(g * 512, 512), :].rearrange("(b p) d -> p b d", p=P)
                sp.dma_start(XG[s][:, :, :], src).then_inc(e_xg[s], 16)

            def store_group(c, q, g, s):
                sp.wait_ge(e_yc, q * GR + g + 1)
                dst = YS[c][bass.ds(g * 512, 512), :].rearrange("(b p) d -> p b d", p=P)
                sp.dma_start(dst, YG[s][:, :, :]).then_inc(e_st[s], 16)

            def ffn(f):
                for c in range(CH):
                    q = CH * f + c
                    sp.wait_ge(e_scat[c], (f + 1) * CT * K * 16)
                    for s in range(2):
                        if q:
                            sp.wait_ge(e_tx, q * GR)
                        load_group(c, q, s, s)
                    def reload(i, s):
                        sp.wait_ge(e_tx, q * GR + 2 * i + s + 1)
                        load_group(c, q, 2 * i + s + 2, s)

                    for i in range(2):
                        for s in range(2):
                            reload(i, s)
                    with sp.Fori(2, GR // 2 - 1) as i:
                        for s in range(2):
                            reload(i, s)
                            store_group(c, q, 2 * i - 4 + s, s)
                    for g in range(GR - 6, GR):
                        store_group(c, q, g, g % 2)

            ffn(0)

            sp.wait_ge(e_yc, CH * GR)
            for s in range(2):
                for par in range(2):
                    dst = KS[s][64 * par + 48:64 * par + 56, :].rearrange("p (a n) -> p a n", n=512)
                    sp.dma_start(dst, key_block[:, :].unsqueeze(1).to_broadcast([8, 8, 512])).then_inc(a_cdma, 16)
                    dst = KS[s][64 * par + 56:64 * par + 59, :].rearrange("p (a n) -> p a n", n=512)
                    sp.dma_start(dst, ones_b[0:3, :].unsqueeze(1).to_broadcast([3, 8, 512])).then_inc(a_cdma, 16)

            def step(b, what):
                c, a = b.plus(2), b.plus(1)
                if "P" in what:
                    sp.wait_ge(a_parts, 2 * (c.index + 1))
                    for n in range(2):
                        for m, part in enumerate((qk_hi[n], qk_mid[n], qk_lo[n])):
                            sp.dma_start(qk_parts[c.slot][3 * n + m], part[:, :]).then_inc(a_dw, 16)
                if "A" in what:
                    sp.wait_ge(a_mtc, a.index + 1)
                    sp.dma_start(max_rows[a.slot], mrows[:, :]).then_inc(a_mw, 16)
                    sp.wait_ge(a_mw, 16 * (a.index + 1))
                    for par in range(2):
                        src = max_rows[a.slot].rearrange("(m h) n -> m h n", m=3)[:, par::2, :]
                        dst = QS[a.slot][64 * par + 56:64 * par + 59, :].rearrange("p (a n) -> p a n", n=512)
                        sp.dma_start(dst, src).then_inc(a_mr[a.slot], 16)
                if "P" in what:
                    sp.wait_ge(a_mbt, c.index + 1)
                    sp.dma_start(mask_rows[c.slot], mbt[:, :]).then_inc(a_dw, 16)
                    sp.wait_ge(a_dw, 7 * 16 * (c.index + 1))
                    if "B" in what:
                        sp.wait_ge(a_pv, NH * (b.index + 1))
                    for n, (stack, terms) in enumerate(((QS, (0, 0, 0, 1, 1, 2)), (KS, (0, 1, 2, 0, 1, 0)))):
                        for par in range(2):
                            for row, m in enumerate(terms):
                                src = qk_parts[c.slot][3 * n + m].rearrange("(h d) n -> d h n", d=HD)[:, par::2, :]
                                p0 = 64 * par + HD * row
                                dst = stack[c.slot][p0:p0 + HD, :].rearrange("p (a n) -> p a n", n=512)
                                sp.dma_start(dst, src).then_inc(a_stk[c.slot], 16)
                    for par in range(2):
                        src = mask_rows[c.slot].rearrange("(h j) n -> j h n", j=8)[:, par::2, :]
                        dst = QS[c.slot][64 * par + 48:64 * par + 56, :].rearrange("p (a n) -> p a n", n=512)
                        sp.dma_start(dst, src).then_inc(a_stk[c.slot], 16)

            for rounds, _, part in steps():
                if rounds is None:
                    for k, what in part:
                        step(Batch(k), what)
                else:
                    with sp.Fori(0, rounds) as i:
                        for k, what in part:
                            step(Batch(k, i), what)

            sp.wait_ge(a_pv, NH * NB)
            sp.dma_start(wgu_s[:, :], wgu).then_inc(s_we, 16)
            sp.dma_start(wd_s[:, :], wd).then_inc(s_we, 16)
            ffn(1)
            for t in range(0, T, 4):
                sp.wait_ge(e_comb, CH * CT + t + 4)
                sp.dma_start(out[t:t + 4].rearrange("t p d -> p t d"), X[:, t:t + 4, :]).then_inc(s_out, 16)
            sp.wait_ge(s_out, 16 * (T // 4))

        @block.gpsimd
        def _(pool):
            ch = Chain(pool, pch)
            g = nc.gpsimd
            g.memset(zero_t, 0.0).then_inc(s_zt, 1)
            g.memset(eps_c[:, :], EPS)
            g.memset(ones_b[:, :], 1.0)
            g.memset(ones_f[:, :], 1.0)
            g.memset(identf[:, :], 0.0)
            g.memset(identb[:, :], 0.0)
            g.memset(block_diag[:, :, :], 0.0)
            g.memset(diag_sel[:, :, :], 0.0)
            g.memset(reset_e[:, :], 1.0)
            g.memset(pack[:, :], 0.0)
            ch.link(g.iota(iota_e[:, :], pattern=[[1, E]], base=0, channel_multiplier=0,
                           allow_small_or_imprecise_dtypes=True))
            g.iota(iota_p[:, :], pattern=[[0, 1]], base=0, channel_multiplier=1, allow_small_or_imprecise_dtypes=True)
            for r in range(4):
                ch.link(g.affine_select(out=pack[:, :], in_=pack[:, :], compare_op=ALU.not_equal, fill=float(32 ** r),
                                        base=-r, pattern=[[-4, GR]], channel_multiplier=1))
            for half, op in enumerate((ALU.is_gt, ALU.is_ge)):
                sign = 1 if half else -1
                g.affine_select(out=half_sel[:, half:half + 1], in_=ones_f[:, 0:1], compare_op=op, fill=0.0,
                                base=-64 * sign, pattern=[[0, 1]], channel_multiplier=sign)
            for m in (identf, identb):
                g.affine_select(out=m[:, :], in_=m[:, :], compare_op=ALU.not_equal, fill=1.0, base=0,
                                pattern=[[-1, P]], channel_multiplier=1)
            g.affine_select(out=tri[:, :], in_=ones_b[:, 0:P], compare_op=ALU.is_gt, fill=0.0, base=0,
                            pattern=[[1, P]], channel_multiplier=-1)
            v = reset_e[:, :].rearrange("p (e t) -> p e t", e=E)
            g.affine_select(out=v, in_=v, compare_op=ALU.not_equal, fill=0.0, base=0,
                            pattern=[[0, E], [1, 16]], channel_multiplier=0)
            ch.link(g.affine_select(out=key_block[:, :], in_=ones_b[0:8, :], compare_op=ALU.is_ge, fill=0.0,
                                    base=0, pattern=[[1, 512]], channel_multiplier=-BS))
            g.memset(block_diag[:, :, :], 1.0).then_inc(pch, 1)
            ch.n += 1
            pool.wait_ge(pch, ch.n)
            ch.link(g.affine_select(out=block_diag[:, :, :], in_=block_diag[:, :, :], compare_op=ALU.is_ge,
                                    fill=0.0, base=0, pattern=[[-HD, NH], [0, 8]], channel_multiplier=1))
            ch.link(g.affine_select(out=block_diag[:, :, :], in_=block_diag[:, :, :], compare_op=ALU.is_ge,
                                    fill=0.0, base=HD - 1, pattern=[[HD, NH], [0, 8]], channel_multiplier=-1))
            ch.link(g.affine_select(out=key_block[:, :], in_=key_block[:, :], compare_op=ALU.is_ge, fill=0.0,
                                    base=BS - 1, pattern=[[-1, 512]], channel_multiplier=BS))
            for half in range(2):
                part = diag_sel[64 * half:64 * half + 64, :, :]
                ch.link(g.affine_select(out=part, in_=part, compare_op=ALU.not_equal, fill=1.0, base=-half,
                                        pattern=[[-2, 4], [1, 8]], channel_multiplier=0))
            g.tensor_scalar(diag_bias[:, :, :], diag_sel[:, :, :], -1.0, BIG, ALU.add, ALU.mult).then_inc(s_cst, 1)

            def scatter(f, c):
                q = CH * f + c
                pool.wait_ge(f_pos, q + 1)
                if f == 0 and c == 0:
                    pool.wait_ge(s_zero, 16 * CH * (BLK // 16))
                if f:
                    pool.wait_ge(e_tx, CH * GR)
                for t in range(CT):
                    for k in range(K):
                        pool.indirect_dma_start(
                            XS[c], bass.IndirectOffsetOnAxis(ap=pos[c][:, k, t:t + 1], axis=0),
                            XN[:, c * CT + t, :], None).then_inc(e_scat[c], 16)

            def gather(f, c, tiles=range(CT)):
                q = CH * f + c
                if 0 in tiles:
                    for s in range(2):
                        pool.wait_ge(e_st[s], 16 * (q + 1) * (GR // 2))
                for t in tiles:
                    for k in range(K):
                        pool.indirect_dma_start(
                            G[c][t][:, k, :], None, YS[c],
                            bass.IndirectOffsetOnAxis(ap=pos[c][:, k, t:t + 1], axis=0)).then_inc(e_gat[c][t // 4], 16)

            scatter(0, 0)
            scatter(0, 1)
            gather(0, 0)
            gather(0, 1, range(0, 4))

            pool.wait_ge(e_comb, CT)
            for s in range(2):
                last = g.memset(VA[s], 0.0)
            ch.link(last)
            for s in range(2):
                for half in range(2):
                    o = VA[s][:, :, :, 9 * half + 8:9 * half + 9].rearrange("p i h c -> p (i h) c")
                    last = g.tensor_scalar(o, ones_f[:, 0:4 * NH].unsqueeze(2), half_sel[:, half:half + 1], None, ALU.mult)
            ch.link(last)

            def values(b):
                pool.wait_ge(a_natc, 4 * (b.index + 1))
                pool.nop(nofuse=True)
                for i in range(4):
                    for half in range(2):
                        last = g.tensor_scalar(VA[b.slot][:, i, :, 9 * half:9 * half + 8], NAT[:, i, 2, :, :],
                                               half_sel[:, half:half + 1], None, ALU.mult)
                last.then_inc(a_va, 1)

            def parts(c):
                for n in range(2):
                    pool.wait_ge(a_rest, 2 * c.index + n + 1)
                    if n == 0 and (c.k >= 1):
                        pool.wait_ge(a_dw, 7 * 16 * c.index)
                    pool.nop(nofuse=True)
                    ch.link(g.tensor_copy(qk_mid[n][:, :], rest[n][:, :]))
                    g.tensor_tensor(qk_lo[n][:, :], rest[n][:, :], qk_mid[n][:, :], ALU.subtract).then_inc(a_parts, 1)

            def step(b, what):
                a, c, t = b.plus(1), b.plus(2), b.plus(-1)
                if "T" in what:
                    pool.wait_ge(t_kr, t.index + 1)
                    for i in range(4):
                        o = O[t.slot][:, :, i, :, 0:8]
                        kr = KR[:, i, :, :].unsqueeze(3).to_broadcast([P, NH, 8, HD])
                        g.tensor_tensor(o, o, kr, ALU.mult).then_inc(t_w, 1)
                if "A" in what:
                    if "T" in what:
                        pool.wait_ge(t_ao, t.index + 1)
                    values(a)
                if b.k == -1:
                    gather(0, 1, range(8, CT))
                if "P" in what:
                    parts(c)
                if b.k == -2:
                    gather(0, 1, range(4, 8))

            per = 2 * 2
            for rounds, _, part in steps():
                if rounds is None:
                    for k, what in part:
                        step(Batch(k), what)
                else:
                    with pool.Fori(0, rounds) as i:
                        ch.enter(i, per)
                        for k, what in part:
                            step(Batch(k, i), what)
                        ch.leave(rounds)

            for c in range(CH):
                scatter(1, c)
            for c in range(CH):
                gather(1, c)

        @block.scalar
        def _(act):
            ch = Chain(act, ach)

            def copy(dst, src):
                return nc.scalar.activation(dst, src, ACT.Copy)

            def normalise(f, c):
                q = CH * f + c
                act.wait_ge(f_stat, q + 1)
                if q == 0:
                    act.wait_ge(s_cst, 1)
                nc.scalar.activation(rstd[:, :], mv[:, :, 1], ACT.Sqrt, bias=eps_c[:, :]).then_inc(f_sqrt, 1)
                for n in range(TG):
                    act.wait_ge(f_tx, q * TG + n + 1)
                    copy(XNT[:, (c * TG + n) * 512:(c * TG + n + 1) * 512], bank(4 + n % 2)).then_inc(f_xnt, 1)

            def shared(f, groups):
                for g in groups:
                    for j in range(4):
                        n = 4 * (CH * TG * f + g) + j
                        act.wait_ge(h_g, n + 1)
                        if n >= 2:
                            act.wait_ge(h_m, n - 1)
                        nc.scalar.activation(SG[j % 2][:, :], bank(j % 2), ACT.Silu).then_inc(h_s, 1)
                        for c in range(CH):
                            if groups == EARLY[f] and 4 * g + j == piece_slot(f, c, 3):
                                act.wait_ge(f_lm, CH * f + c + 1)
                                nc.scalar.activation(EX, L, ACT.Exp).then_inc(f_ex, 1)

            def experts(f, c):
                q = CH * f + c

                def xt(g, s):
                    act.wait_ge(e_tx, q * GR + g + 1)
                    copy(XT[s][:, :], bank(4)).then_inc(e_xt, 1)

                def silu(g, s):
                    act.wait_ge(e_gu, q * GR + g + 1)
                    v = banks[:, 2 * s:2 * s + 2, :].rearrange("p a (b c) -> p (a b) c", c=256)
                    o = SG[s][:, :].rearrange("p (b c) -> p b c", b=4)
                    nc.scalar.activation(o, v[:, :, 0:128], ACT.Silu).then_inc(e_s, 1)

                def y(g, s):
                    act.wait_ge(e_y, q * GR + g + 1)
                    yg = YG[s][:, :, :].rearrange("p b d -> p (b d)")
                    copy(yg, bank(6 + s)).then_inc(e_yc, 1)

                def store_buffer(i, s):
                    if q or not isinstance(i, int) or i >= 1:
                        act.wait_ge(e_st[s], 16 * (q * (GR // 2) + i))

                def pair(i, first_pair=False, last_pair=False):
                    for s in range(2):
                        silu(2 * i + s, s)
                        if not last_pair:
                            xt(2 * i + 2 + s, s)
                        if not first_pair:
                            store_buffer(i - 1, s)
                            y(2 * i - 2 + s, s)

                xt(0, 0)
                xt(1, 1)
                pair(0, first_pair=True)
                pair(1)
                with act.Fori(2, GR // 2 - 1) as i:
                    pair(i)
                pair(GR // 2 - 1, last_pair=True)
                for s in range(2):
                    store_buffer(GR // 2 - 1, s)
                    y(GR - 2 + s, s)

            def tail_copy(t):
                act.wait_ge(t_at, t.index + 1)
                copy(AOT[:, :], bank(6)).then_inc(t_atc, 1)

            def probs(b, h, n):
                for j in range(AH):
                    act.wait_ge(a_s, AH * (n + h) + j + 1)
                    if j == 0 and (h >= 2 or b.k >= 1):
                        act.wait_ge(a_pv, n + h - 1)
                    nc.scalar.activation(PT[h % 2][:, 512 * j:512 * (j + 1)], bank(2 + j % 2),
                                         ACT.Exp, scale=SCALE).then_inc(a_e, 1)

            def take_ot(b, h, n):
                act.wait_ge(a_pv, n + h + 1)
                if b.k >= 1 or h >= 1:
                    act.wait_ge(a_ot, n + h)
                copy(OT, bank(5)).then_inc(a_otc, 1)

            def take_o(b, h, n):
                act.wait_ge(a_ot, n + h + 1)
                o = O[b.slot][:, h, :, :, :].rearrange("p i (j a) c -> p (i j) (a c)", a=2)
                copy(o, bank(4).rearrange("p (m c) -> p m c", c=32)[:, :, 0:18]).then_inc(a_oc, 1)

            def step(b, what):
                a, c, t = b.plus(1), b.plus(2), b.plus(-1)
                n = NH * b.index
                if b.k == 0:
                    act.wait_ge(e_comb, CH * CT)
                for h in range(NH + 2):
                    if "B" in what:
                        if h >= 2:
                            take_ot(b, h - 2, n)
                        if h < NH:
                            probs(b, h, n)
                        if h >= 2:
                            take_o(b, h - 2, n)
                    if h == 0 and "P" in what:
                        act.wait_ge(a_stat, c.index + 1)
                        nc.scalar.activation(rstd[:, 0:4], mv[:, 0:4, 1], ACT.Sqrt, bias=eps_c[:, :]).then_inc(a_sqrt, 1)
                    if h == 8 and "P" in what:
                        act.wait_ge(a_tx, c.index + 1)
                        copy(xaT[:, :], bank(7)).then_inc(a_xt, 1)
                    if h == 10 and "T" in what:
                        tail_copy(t)
                    if h == 13 and "P" in what:
                        for m in range(2):
                            act.wait_ge(a_qk, 2 * c.index + m + 1)
                            if m == 0 and c.k >= 1:
                                act.wait_ge(a_dw, 7 * 16 * c.index)
                            copy(qk_hi[m][:, :], bank(m)).then_inc(a_hi, 1)
                    if h == 14 and "A" in what:
                        act.wait_ge(a_mt, a.index + 1)
                        nc.scalar.activation(mrows[:, :], bank(6).bitcast(BF16)[0:3 * NH, 0:512], ACT.Copy).then_inc(a_mtc, 1)
                        act.wait_ge(a_pd, a.index + 1)
                        mx = MX[a.slot].rearrange("p i h j -> p (i h j)")
                        nc.scalar.activation(mx, mx, ACT.Exp, scale=SCALE)
                        e = ediag[a.slot][:, :, :]
                        nc.scalar.activation(e, e, ACT.Exp, scale=SCALE).then_inc(a_pe, 1)
                    if h in (15, 16) and "P" in what:
                        for i in (2 * h - 30, 2 * h - 29):
                            act.wait_ge(a_nat, 4 * c.index + i + 1)
                            if i == 0 and c.k >= 1:
                                act.wait_ge(a_va, c.index)
                            nat = NAT[:, i, :, :, :].rearrange("p a h d -> p (a h d)")
                            copy(nat, bank(i % 2)[:, 0:384]).then_inc(a_natc, 1)
                    if h == 17 and "P" in what:
                        act.wait_ge(a_mn, c.index + 1)
                        mn = MN[c.slot].rearrange("p i h j -> p (i h j)")
                        copy(mn, bank(1)).then_inc(a_mnc, 1)

            normalise(0, 0)
            normalise(0, 1)
            shared(0, EARLY[0])
            experts(0, 0)
            experts(0, 1)
            for rounds, _, part in steps():
                if rounds is None:
                    for k, what in part:
                        step(Batch(k), what)
                else:
                    with act.Fori(0, rounds) as i:
                        for k, what in part:
                            step(Batch(k, i), what)
            normalise(1, 0)
            normalise(1, 1)
            shared(1, EARLY[1])
            experts(1, 0)
            experts(1, 1)
            shared(1, LATE)

        @block.vector
        def _(dve):
            v = nc.vector
            ch = Chain(dve, dch)

            def normalise(f, c):
                q = CH * f + c
                if f == 0:
                    dve.wait_ge(s_x[c], 16)
                    if c == 0:
                        dve.wait_ge(s_cst, 1)
                        dve.wait_ge(s_w, 7 * 16)
                for t in range(CT):
                    last = v.bn_stats(stats[:, t, :], X[:, c * CT + t, :])
                ch.link(last)
                for t in range(CT):
                    last = v.bn_aggr(mv[:, t, :], stats[:, t, :])
                last.then_inc(f_stat, 1)
                dve.wait_ge(f_sqrt, q + 1)
                ch.link(v.reciprocal(rstd[:, :], rstd[:, :]))
                for n in range(TG):
                    for t in range(4 * n, 4 * n + 4):
                        last = v.tensor_scalar(XN[:, c * CT + t, :], X[:, c * CT + t, :], mv[:, t, 0:1],
                                               rstd[:, t:t + 1], ALU.subtract, ALU.mult)
                    last.then_inc(f_xn, 1)

            def route(f, c):
                q = CH * f + c
                dve.wait_ge(f_log, q + 1)
                ch.link(v.tensor_tensor(L, bank(6 + c).rearrange("p (t e) -> p t e", t=CT),
                                        rb_s[:, :].unsqueeze(1).to_broadcast([P, CT, E]), ALU.add))
                for t in range(CT):
                    last = v.max(top8[:, t, :], L[:, t, :])
                ch.link(last)
                yield
                for t in range(CT):
                    last = v.max_index(idx8[:, t, :], top8[:, t, :], L[:, t, :])
                ch.link(last)
                ch.link(v.tensor_copy(idxf[:, :, :], idx8[:, :, :]))
                yield
                v.tensor_tensor(L, L, top8[:, :, 0:1].to_broadcast([P, CT, E]), ALU.subtract).then_inc(f_lm, 1)
                v.tensor_tensor(OH[:, :, :, :],
                                iota_e[:, :].unsqueeze(1).unsqueeze(3).to_broadcast([P, K, E, CT]),
                                idxf[:, :, 0:K].rearrange("p t k -> p k t").unsqueeze(2).to_broadcast([P, K, E, CT]),
                                ALU.is_equal).then_inc(f_oh, 1)
                yield
                dve.wait_ge(f_ex, q + 1)
                ch.link(v.tensor_reduce(zsum[:, :], EX, AX, ALU.add))
                dve.wait_ge(f_oh, q + 1)
                ch.link(v.reciprocal(zsum[:, :], zsum[:, :]))
                ch.link(v.tensor_tensor(EX, EX, zsum[:, :].unsqueeze(2).to_broadcast([P, CT, E]), ALU.mult))
                yield
                for k in range(K):
                    last = v.tensor_tensor(OHP[:, k, :, :], OH[:, k, :, :], EX.rearrange("p t e -> p e t"), ALU.mult)
                ch.link(last)
                yield
                ch.link(v.tensor_reduce(topw[:, :, :].rearrange("p t k -> p k t"),
                                        OHP[:, :, :, :].rearrange("p k e t -> p k t e"), AX, ALU.add))
                ch.link(v.tensor_reduce(wsum[:, :], topw[:, :, :], AX, ALU.add))
                ch.link(v.tensor_scalar_max(wsum[:, :], wsum[:, :], 1e-12))
                ch.link(v.reciprocal(wsum[:, :], wsum[:, :]))
                ch.link(v.tensor_tensor(topw[:, :, :], topw[:, :, :],
                                        wsum[:, :].unsqueeze(2).to_broadcast([P, CT, K]), ALU.mult))
                ch.link(v.tensor_scalar(GW[c][:, :, :], topw[:, :, :], 0.5, None, ALU.mult))
                yield
                dve.wait_ge(f_cnt, q + 1)
                ch.link(v.tensor_copy(tot, bank(4)))
                ch.link(v.tensor_tensor_scan(scan, reset_e[:, :], tot, 0.0, ALU.mult, ALU.add))
                sc3 = scan.rearrange("p (e t) -> p e t", e=E)
                ch.link(v.tensor_scalar(nblk[:, :], sc3[:, :, CT - 1], 1.0 / P, 0.5 - 1.0 / (2 * P), ALU.mult, ALU.add))
                ch.link(v.tensor_scalar(nblk[:, :], nblk[:, :], ROUND, -ROUND, ALU.add, ALU.add))
                ch.link(v.tensor_tensor_scan(cumb[:, :], ones_b[:, 0:E], nblk[:, :], 0.0, ALU.mult, ALU.add))
                v.tensor_scalar(cmpb[:, :], cumb[:, :], iota_p[:, :], None, ALU.is_le)
                ch.link(v.tensor_tensor(begin[:, :], cumb[:, :], nblk[:, :], ALU.subtract))
                ch.link(v.tensor_reduce(eblk[:, :], cmpb[:, :], AX, ALU.add))
                v.tensor_scalar(eblk[:, :], eblk[:, :], float(E - 1), None, ALU.min).then_inc(f_eb, 1)
                ch.link(v.tensor_scalar(begin[:, :], begin[:, :], float(P), None, ALU.mult))
                yield
                v.tensor_tensor(place, bank(5), scan, ALU.add).then_inc(dch, 1)
                ch.n += 1
                dve.wait_ge(dch, ch.n)
                ch.link(v.tensor_tensor(place, place, tot, ALU.subtract))
                pl3 = place.rearrange("p (e t) -> p e t", e=E)
                ch.link(v.tensor_tensor(pl3, pl3, begin[:, :].unsqueeze(2).to_broadcast([P, E, CT]), ALU.add))
                for k in range(K):
                    last = v.tensor_tensor(OHP[:, k, :, :], OH[:, k, :, :], pl3, ALU.mult)
                ch.link(last)
                yield
                ch.link(v.tensor_reduce(posf[:, :, :], OHP[:, :, :, :].rearrange("p k e t -> p k t e"), AX, ALU.add))
                v.tensor_copy(pos[c][:, :, :], posf[:, :, :]).then_inc(f_pos, 1)
                yield
                dve.wait_ge(f_ebt, q + 1)
                v.tensor_copy(ids[c][:, :], bank(4)[0:1, 0:GR]).then_inc(f_ids, 1)
                yield

            def shared(f, groups):
                base = CH * TG * f
                pieces = [route(f, c) for c in range(CH)]

                def finish(g):
                    dve.wait_ge(h_y, base + g + 1)
                    xg = X[:, 4 * g:4 * g + 4, :].rearrange("p t d -> p (t d)")
                    v.scalar_tensor_tensor(xg, bank(6), 0.5, xg, ALU.mult, ALU.add).then_inc(h_x, 1)

                for g in groups:
                    for j in range(4):
                        n = 4 * (base + g) + j
                        dve.wait_ge(h_s, n + 1)
                        if j == 0 and g >= 2:
                            dve.wait_ge(h_y, base + g - 1)
                        v.tensor_tensor(SHT[g % 2][:, j, :], SG[j % 2][:, :], bank(2 + j % 2), ALU.mult).then_inc(h_m, 1)
                        for c in range(CH):
                            for k in range(PIECES):
                                if groups == EARLY[f] and 4 * g + j == piece_slot(f, c, k):
                                    next(pieces[c])
                    if g > groups[0]:
                        finish(g - 1)
                finish(groups[-1])

            def experts(f, c):
                q = CH * f + c

                def mul(g, s):
                    dve.wait_ge(e_s, q * GR + g + 1)
                    u = banks[:, 2 * s:2 * s + 2, :].rearrange("p a (b c) -> p (a b) c", c=256)
                    v.tensor_tensor(HG[s][:, :, :], SG[s][:, :].rearrange("p (b c) -> p b c", b=4), u[:, :, 128:256],
                                    ALU.mult).then_inc(e_h, 1)

                def ht(g, s):
                    dve.wait_ge(e_th, q * GR + g + 1)
                    v.tensor_copy(HT[s][:, :], bank(5)).then_inc(e_ht, 1)

                mul(0, 0)
                mul(1, 1)
                ht(0, 0)
                with dve.Fori(1, GR // 2) as i:
                    ht(2 * i - 1, 1)
                    mul(2 * i, 0)
                    ht(2 * i, 0)
                    mul(2 * i + 1, 1)
                ht(GR - 1, 1)

            def combine(f, c):
                q = CH * f + c
                for t0 in range(0, CT, 4):
                    dve.wait_ge(e_gat[c][t0 // 4], (f + 1) * 4 * K * 16)
                    for k in range(K):
                        for t in range(t0, t0 + 4):
                            xt = X[:, c * CT + t, :]
                            last = v.scalar_tensor_tensor(xt, G[c][t][:, k, :], GW[c][:, t, k:k + 1], xt, ALU.mult, ALU.add)
                            if k == K - 1:
                                last.then_inc(e_comb, 1)
                        if k < K - 1:
                            ch.link(last)

            BJ = [P, 4, NH, 8]

            def tail1(t):
                o, s = O[t.slot], t.slot
                dve.wait_ge(a_oc, NH * (t.index + 1))
                dve.wait_ge(a_pe, t.index + 1)
                v.tensor_reduce(lsum[:, :, :], o[:, :, :, :, 8].rearrange("p h i j -> p i h j"), AX, ALU.add)
                ch.link(v.scalar_tensor_tensor(dcor[:, :, :], adiag[s][:, :, :], 1.0, ediag[s][:, :, :],
                                               ALU.subtract, ALU.mult))
                ch.link(v.tensor_tensor(lsum[:, :, :], lsum[:, :, :], dcor[:, :, :], ALU.subtract))
                ch.link(v.reciprocal(rinv[:, :, :], lsum[:, :, :]))
                v.tensor_tensor(MX[s], MX[s], rinv[:, :, :].unsqueeze(3).to_broadcast(BJ), ALU.mult).then_inc(t_pm, 1)

            def tail2(t):
                dve.wait_ge(t_pt, t.index + 1)
                ch.link(v.tensor_reduce(bmax[:, :], bank(6).rearrange("p (b n) -> p b n", n=BS), AX, ALU.max))
                v.tensor_scalar(keepx[:, :].rearrange("p (b n) -> p b n", n=BS),
                                bmax[:, :].unsqueeze(2).to_broadcast([P, 8, BS]), THRESH, None, ALU.is_gt).then_inc(t_kx, 1)

            def tail3(t):
                s = t.slot
                dve.wait_ge(t_kn, t.index + 1)
                v.tensor_tensor(KR, bank(7).rearrange("p (i h j) -> p i h j", i=4, h=NH),
                                rinv[:, :, :].unsqueeze(3).to_broadcast(BJ), ALU.mult).then_inc(t_kr, 1)
                dve.wait_ge(t_kr, t.index + 1)
                ch.link(v.tensor_tensor(tmp, KR, AL[s], ALU.mult))
                ch.link(v.tensor_tensor(tmp, tmp, diag_sel[:, :, :].unsqueeze(2).to_broadcast(BJ), ALU.mult))
                ch.link(v.tensor_reduce(dcor[:, :, :], tmp, AX, ALU.add))
                ch.link(v.tensor_tensor(dcor[:, :, :], rinv[:, :, :], dcor[:, :, :], ALU.subtract))
                ch.link(v.tensor_tensor(dcor[:, :, :], dcor[:, :, :], ediag[s][:, :, :], ALU.mult))
                for half in range(2):
                    ps = slice(64 * half, 64 * half + 64)
                    last = v.tensor_tensor(tmp[ps, :, :, :], VA[s][ps, :, :, 9 * half:9 * half + 8],
                                           dcor[ps, :, :].unsqueeze(3).to_broadcast([64, 4, NH, HD]), ALU.mult)
                ch.mark(last)

            def tail4(t, i):
                dve.wait_ge(t_w, 4 * t.index + i + 1)
                last = v.tensor_reduce(AO[:, i, :, :], O[t.slot][:, :, i, :, 0:8].rearrange("p h j d -> p h d j"),
                                       AX, ALU.add)
                if i == 3:
                    ch.link(last)
                    v.tensor_tensor(AO, AO, tmp, ALU.add).then_inc(t_ao, 1)

            def tail5(t):
                dve.wait_ge(t_op, t.index + 1)
                xg = X[:, bass.ds(4 * t.index, 4), :].rearrange("p t d -> p (t d)")
                v.tensor_tensor(xg, xg, bank(7), ALU.add).then_inc(t_x, 1)

            def maxima(a, h):
                for i in range(4):
                    n = 4 * h + i
                    dve.wait_ge(a_a, 4 * NH * a.index + n + 1)
                    v.tensor_reduce(MX[a.slot][:, i, h, :], bank(n % 2).rearrange("p (b n) -> p b n", n=BS), AX,
                                    ALU.max).then_inc(a_ar, 1)

            def rows(a):
                s = a.slot
                dve.wait_ge(a_mnc, a.index + 1)
                dve.wait_ge(a_ar, 4 * NH * (a.index + 1))
                v.tensor_tensor(tmp, diag_bias[:, :, :].unsqueeze(2).to_broadcast(BJ),
                                sdiag[s][:, :, :].unsqueeze(3).to_broadcast(BJ), ALU.add)
                v.tensor_scalar(AL[s], MN[s], -1.0, None, ALU.is_ge)
                ch.link(v.tensor_tensor(MX[s], MX[s], MN[s], ALU.add))
                ch.link(v.tensor_tensor(MX[s], MX[s], tmp, ALU.max))
                ch.link(v.tensor_reduce(mrow[:, :, :], MX[s], AX, ALU.max))
                v.tensor_scalar(mparts[:, :, 0, :], mrow[:, :, :], -1.0, None, ALU.mult)
                v.tensor_tensor(ediag[s][:, :, :], sdiag[s][:, :, :], mrow[:, :, :], ALU.subtract)
                ch.link(v.tensor_tensor(MX[s], MX[s], mrow[:, :, :].unsqueeze(3).to_broadcast(BJ), ALU.subtract))
                ch.link(v.scalar_tensor_tensor(mres[:, :, :], mrow[:, :, :], -1.0, mparts[:, :, 0, :],
                                               ALU.mult, ALU.subtract))
                ch.link(v.tensor_copy(mparts[:, :, 1, :], mres[:, :, :]))
                v.tensor_tensor(mparts[:, :, 2, :], mres[:, :, :], mparts[:, :, 1, :], ALU.subtract).then_inc(a_mp, 1)
                ch.link(v.tensor_tensor(tmp, AL[s], diag_sel[:, :, :].unsqueeze(2).to_broadcast(BJ), ALU.mult))
                v.tensor_reduce(adiag[s][:, :, :], tmp, AX, ALU.add).then_inc(a_pd, 1)

            def normalise_rows(c):
                for j in range(4):
                    last = v.bn_stats(stats[:, j, :], X[:, bass.ds(4 * c.index + j, 1), :].rearrange("p a d -> p (a d)"))
                ch.link(last)
                dve.nop(nofuse=True)
                for j in range(4):
                    last = v.bn_aggr(mv[:, j, :], stats[:, j, :])
                last.then_inc(a_stat, 1)
                dve.wait_ge(a_sqrt, c.index + 1)
                ch.link(v.reciprocal(rstd[:, 0:4], rstd[:, 0:4]))
                for j in range(4):
                    last = v.tensor_scalar(xa[:, j, :], X[:, bass.ds(4 * c.index + j, 1), :].rearrange("p a d -> p (a d)"),
                                           mv[:, j, 0:1], rstd[:, j:j + 1], ALU.subtract, ALU.mult)
                last.then_inc(a_xa, 1)

            def prepare(c):
                s = c.slot
                for m in range(2):
                    dve.wait_ge(a_hi, 2 * c.index + m + 1)
                    if c.k >= 1 and m == 0:
                        dve.wait_ge(a_parts, 2 * c.index)
                    v.tensor_tensor(rest[m][:, :], bank(m), qk_hi[m][:, :], ALU.subtract).then_inc(a_rest, 1)
                    v.tensor_reduce(bsum[:, m, :], bank(m).rearrange("p (b n) -> p b n", n=BS), AX,
                                    ALU.add).then_inc(a_sum, 1)
                dve.wait_ge(a_sum, 2 * (c.index + 1))
                ch.link(v.tensor_scalar(bsum[:, :, :], bsum[:, :, :], 1.0 / BS, None, ALU.mult))
                v.tensor_tensor(kmd[:, :, :], block_diag[:, :, :], bsum[:, 1:2, :].to_broadcast([P, NH, 8]),
                                ALU.mult).then_inc(a_kmd, 1)
                dve.wait_ge(a_natc, 4 * (c.index + 1))
                for i in range(4):
                    last = v.tensor_tensor(prod[:, i, :, :], NAT[:, i, 0, :, :], NAT[:, i, 1, :, :], ALU.mult)
                ch.link(last)
                v.tensor_reduce(sdiag[s][:, :, :], prod, AX, ALU.add).then_inc(a_sd, 1)
                dve.wait_ge(a_mb, c.index + 1)
                if c.k >= 1:
                    dve.wait_ge(a_dw, 7 * 16 * c.index)
                v.tensor_scalar(mbt[:, :].rearrange("p (b n) -> p b n", n=BS),
                                bank(0)[:, 0:8].unsqueeze(2).to_broadcast([P, 8, BS]),
                                THRESH * float(HD) ** 0.5, -BIG, ALU.is_le, ALU.mult).then_inc(a_mbt, 1)
                dve.wait_ge(a_sd, c.index + 1)

            def step(b, what):
                a, c, t = b.plus(1), b.plus(2), b.plus(-1)
                if "T" in what:
                    tail1(t)
                if "P" in what:
                    normalise_rows(c)
                if "T" in what:
                    tail2(t)
                    tail3(t)
                for h in range(NH):
                    if "A" in what:
                        maxima(a, h)
                    if "T" in what:
                        if h in (3, 5, 7, 9):
                            tail4(t, (h - 3) // 2)
                if "T" in what:
                    tail5(t)
                if "A" in what:
                    rows(a)
                if "P" in what:
                    prepare(c)

            normalise(0, 0)
            normalise(0, 1)
            shared(0, EARLY[0])
            experts(0, 0)
            experts(0, 1)
            combine(0, 0)
            dve.wait_ge(e_comb, CT)
            per = 2 * PER_DVE
            for rounds, _, part in steps():
                if rounds is None:
                    for k, what in part:
                        if k == 0:
                            combine(0, 1)
                            dve.wait_ge(e_comb, CH * CT)
                        step(Batch(k), what)
                else:
                    with dve.Fori(0, rounds) as i:
                        ch.enter(i, per)
                        for k, what in part:
                            step(Batch(k, i), what)
                        ch.leave(rounds)
            dve.wait_ge(t_x, NB)
            normalise(1, 0)
            normalise(1, 1)
            shared(1, EARLY[1])
            experts(1, 0)
            experts(1, 1)
            combine(1, 0)
            shared(1, LATE)
            combine(1, 1)

        @block.tensor
        def _(pe):
            mm, tr = nc.tensor.matmul, nc.tensor.transpose
            packed = [pe.alloc_register(f"packed{s}") for s in range(2)]
            packed_before = [pe.alloc_register(f"packed_before{s}") for s in range(2)]

            def normalise(f, c):
                q = CH * f + c
                if q == 0:
                    pe.wait_ge(s_cst, 1)
                    pe.wait_ge(s_w, 7 * 16)
                if f == 1 and c == 0:
                    pe.wait_ge(t_x, NB)
                for n in range(TG):
                    pe.wait_ge(f_xn, q * TG + n + 1)
                    if n >= 2 or c:
                        pe.wait_ge(f_xnt, q * TG + n - 1)
                    for j in range(4):
                        last = tr(bank(4 + n % 2)[:, j * P:(j + 1) * P], XN[:, c * CT + 4 * n + j, :], identf[:, :])
                    last.then_inc(f_tx, 1)
                    if n >= 1:
                        logits(q, c, n - 1)
                logits(q, c, TG - 1).then_inc(f_log, 1)

            def logits(q, c, n):
                pe.wait_ge(f_xnt, q * TG + n + 1)
                for j in range(4):
                    t = 4 * n + j
                    last = mm(bank(6 + c)[:, t * E:(t + 1) * E], XNT[:, (c * CT + t) * P:(c * CT + t + 1) * P],
                              rw_s[:, :], start=True, stop=True)
                return last

            def counts(f, c):
                q = CH * f + c
                pe.wait_ge(f_oh, q + 1)
                if c:
                    pe.wait_ge(f_pos, q)
                    pe.wait_ge(f_ids, q)
                for k in range(K):
                    mm(bank(5), tri[:, :], OH[:, k, :, :].rearrange("p e t -> p (e t)"), start=k == 0, stop=k == K - 1)
                for k in range(K):
                    last = mm(bank(4), ones_b[:, 0:P], OH[:, k, :, :].rearrange("p e t -> p (e t)"),
                              start=k == 0, stop=k == K - 1)
                last.then_inc(f_cnt, 1)

            def block_experts(f, c):
                pe.wait_ge(f_eb, CH * f + c + 1)
                mm(bank(4)[0:1, 0:GR], eblk[:, :], pack[:, :], start=True, stop=True).then_inc(f_ebt, 1)

            def shared(f, groups):
                base = CH * TG * f

                def gate_up(g, j):
                    n = 4 * (base + g) + j
                    xn = XNT[:, g * 512:(g + 1) * 512]
                    if n >= 2:
                        pe.wait_ge(h_m, n - 1)
                    mm(bank(j % 2), sg_s[:, j * P:(j + 1) * P], xn, start=True, stop=True)
                    mm(bank(2 + j % 2), su_s[:, j * P:(j + 1) * P], xn, start=True, stop=True).then_inc(h_g, 1)
                    for c in range(CH):
                        if groups == EARLY[f] and 4 * g + j == piece_slot(f, c, 4):
                            counts(f, c)
                        if groups == EARLY[f] and 4 * g + j == piece_slot(f, c, 8):
                            block_experts(f, c)

                def down(g):
                    pe.wait_ge(h_m, 4 * (base + g + 1))
                    if base + g:
                        pe.wait_ge(h_x, base + g)
                    for t in range(4):
                        for j in range(4):
                            last = mm(bank(6)[:, t * P:(t + 1) * P], SHT[g % 2][:, j, t * P:(t + 1) * P],
                                      sd_s[:, j, :], start=j == 0, stop=j == 3)
                    last.then_inc(h_y, 1)

                for g in groups:
                    gate_up(g, 0)
                    gate_up(g, 1)
                    if g > groups[0]:
                        down(g - 1)
                    gate_up(g, 2)
                    gate_up(g, 3)
                down(groups[-1])

            def experts(f, c):
                q = CH * f + c
                if c == 0:
                    pe.wait_ge(s_we, 32 * (f + 1))
                    pe.wait_ge(f_ids, CH * (f + 1))
                if c == 0:
                    pe.wait_ge(h_x, CH * TG * f + len(EARLY[f]))

                def first(g):
                    return q == 0 and isinstance(g, int) and g == 0

                def rows(g, i, s):
                    pe.wait_ge(e_xg[s], 16 * (q * (GR // 2) + i + 1))
                    if not first(g):
                        pe.wait_ge(e_xt, q * GR + g)
                    for j in range(4):
                        last = tr(bank(4)[:, j * P:(j + 1) * P], XG[s][:, j, :], identf[:, :])
                    last.then_inc(e_tx, 1)

                def gate_up(g, s, four):
                    pe.wait_ge(e_xt, q * GR + g + 1)
                    for j in range(4):
                        o = bank(2 * s + j // 2)[:, 256 * (j % 2):256 * (j % 2) + 256]
                        which = (four >> (5 * j)) & (E - 1)
                        last = mm(o, XT[s][:, j * P:(j + 1) * P], wgu_s[:, bass.ds(which * (2 * H), 2 * H)],
                                  start=True, stop=True)
                    last.then_inc(e_gu, 1)

                def turn(g, s):
                    pe.wait_ge(e_h, q * GR + g + 1)
                    if not first(g):
                        pe.wait_ge(e_ht, q * GR + g)
                    for j in range(4):
                        last = tr(bank(5)[:, j * P:(j + 1) * P], HG[s][:, j, :], identf[:, :])
                    last.then_inc(e_th, 1)

                def down(g, s, four):
                    pe.wait_ge(e_ht, q * GR + g + 1)
                    if q or not isinstance(g, int) or g >= 2:
                        pe.wait_ge(e_yc, q * GR + g - 1)
                    for j in range(4):
                        which = (four >> (5 * j)) & (E - 1)
                        last = mm(bank(6 + s)[:, j * P:(j + 1) * P], HT[s][:, j * P:(j + 1) * P],
                                  wd_s[:, bass.ds(which * D, D)], start=True, stop=True)
                    last.then_inc(e_y, 1)

                def fetch(i):
                    for s in range(2):
                        if not isinstance(i, int) or i >= 1:
                            pe.reg_mov(packed_before[s], packed[s])
                        pe.reg_load(packed[s], ids[c][0:1, bass.ds(2 * i + s, 1)])

                def pair(i, first_pair=False, last_pair=False):
                    four = [pe.snap(r, min_val=0, max_val=E ** 4 - 1) for r in packed]
                    if not first_pair:
                        before = [pe.snap(r, min_val=0, max_val=E ** 4 - 1) for r in packed_before]
                    gate_up(2 * i, 0, four[0])
                    if not last_pair:
                        fetch(i + 1)
                    if not first_pair:
                        turn(2 * i - 1, 1)
                    if not last_pair:
                        rows(2 * i + 2, i + 1, 0)
                    if not first_pair:
                        down(2 * i - 2, 0, before[0])
                    gate_up(2 * i + 1, 1, four[1])
                    turn(2 * i, 0)
                    if not last_pair:
                        rows(2 * i + 3, i + 1, 1)
                    if not first_pair:
                        down(2 * i - 1, 1, before[1])
                    return four

                fetch(0)
                rows(0, 0, 0)
                rows(1, 0, 1)
                pair(0, first_pair=True)
                pair(1)
                with pe.Fori(2, GR // 2 - 1) as i:
                    pair(i)
                four = pair(GR // 2 - 1, last_pair=True)
                turn(GR - 1, 1)
                down(GR - 2, 0, four[0])
                down(GR - 1, 1, four[1])

            def tail_p(t):
                pe.wait_ge(t_pm, t.index + 1)
                for i in range(4):
                    m = MX[t.slot][:, i, :, :].rearrange("p h j -> p (h j)")
                    last = tr(bank(6)[:, i * P:(i + 1) * P], m, identf[:, :])
                last.then_inc(t_pt, 1)

            def tail_k(t):
                pe.wait_ge(t_kx, t.index + 1)
                for i in range(4):
                    last = mm(bank(7)[:, i * P:(i + 1) * P], keepx[:, i * P:(i + 1) * P], identb[:, :], start=True, stop=True)
                last.then_inc(t_kn, 1)

            def tail_a(t):
                pe.wait_ge(t_ao, t.index + 1)
                for i in range(4):
                    o = AO[:, i, :, :].rearrange("p h d -> p (h d)")
                    last = tr(bank(6)[:, i * P:(i + 1) * P], o, identf[:, :])
                last.then_inc(t_at, 1)

            def tail_o(t):
                pe.wait_ge(t_atc, t.index + 1)
                for i in range(4):
                    last = mm(bank(7)[:, i * P:(i + 1) * P], AOT[:, i * P:(i + 1) * P], wo_s[:, :], start=True, stop=True)
                last.then_inc(t_op, 1)

            def max_scores(a, n):
                h, i = n // 4, n % 4
                p0 = 64 * (h % 2)
                o = (h // 2) * 512
                if a.k >= 1 or n >= 2:
                    pe.wait_ge(a_ar, 4 * NH * a.index + n - 1)
                mm(bank(n % 2), QS[a.slot][p0:p0 + 48, o + i * P:o + (i + 1) * P], KS[a.slot][p0:p0 + 48, o:o + 512],
                   start=True, stop=True).then_inc(a_a, 1)

            def scores(b, h, j):
                p0 = 64 * (h % 2)
                o = (h // 2) * 512
                n = AH * h + j
                if b.k >= 1 or n >= 2:
                    pe.wait_ge(a_e, AH * NH * b.index + n - 1)
                mm(bank(2 + n % 2), KS[b.slot][p0:p0 + 59, o + j * P:o + (j + 1) * P], QS[b.slot][p0:p0 + 59, o:o + 512],
                   start=True, stop=True).then_inc(a_s, 1)

            def sums(b, h, j):
                pe.wait_ge(a_e, AH * (NH * b.index + h) + j + 1)
                if j == 0 and (b.k >= 1 or h >= 1):
                    pe.wait_ge(a_otc, NH * b.index + h)
                last = mm(bank(5)[32 * j:32 * j + 32, :], VA[b.slot][:, j, h, :], PT[h % 2][:, 512 * j:512 * (j + 1)],
                          start=True, stop=True)
                if j == AH - 1:
                    last.then_inc(a_pv, 1)

            def turn_sums(b, h):
                pe.wait_ge(a_otc, NH * b.index + h + 1)
                if b.k >= 1 or h >= 1:
                    pe.wait_ge(a_oc, NH * b.index + h)
                for i in range(4):
                    last = tr(bank(4)[:, i * P:(i + 1) * P], OT[:, i * P:(i + 1) * P], identf[:, :])
                last.then_inc(a_ot, 1)

            def max_turn(a):
                pe.wait_ge(a_mp, a.index + 1)
                pe.nop(nofuse=True)
                for i in range(4):
                    m = mparts[:, i, :, :].rearrange("p m h -> p (m h)")
                    last = tr(bank(6).bitcast(BF16)[0:3 * NH, i * P:(i + 1) * P], m, identb[:, :])
                last.then_inc(a_mt, 1)

            def turn_rows(c, t):
                pe.wait_ge(a_xa, c.index + 1)
                if t is not None:
                    pe.wait_ge(t_kr, t.index + 1)
                for j in range(4):
                    last = tr(bank(7)[:, j * P:(j + 1) * P], xa[:, j, :], identf[:, :])
                last.then_inc(a_tx, 1)

            def project(c, a):
                pe.wait_ge(a_xt, c.index + 1)
                for m in range(2):
                    if a is not None:
                        pe.wait_ge(a_ar, 4 * NH * (a.index + 1) - 1 + m)
                    mm(bank(m), wqkv_s[:, m * D:(m + 1) * D], xaT[:, :], start=True, stop=True).then_inc(a_qk, 1)

            def project_rows(c, i):
                if i < 2:
                    pe.wait_ge(a_sum, 2 * c.index + i + 1)
                else:
                    pe.wait_ge(a_natc, 4 * c.index + i - 1)
                mm(bank(i % 2)[:, 0:384], xaT[:, i * P:(i + 1) * P], wqkv_s[:, :], start=True, stop=True).then_inc(a_nat, 1)

            def block_scores(c):
                pe.wait_ge(a_natc, 4 * (c.index + 1))
                pe.wait_ge(a_kmd, c.index + 1)
                mm(bank(0)[:, 0:8], kmd[:, :, :].rearrange("p h j -> p (h j)"), bsum[:, 0, :], start=True,
                   stop=True).then_inc(a_mb, 1)

            def turn_mask(c):
                pe.wait_ge(a_mbt, c.index + 1)
                for i in range(4):
                    last = mm(bank(1)[:, i * P:(i + 1) * P], mbt[:, i * P:(i + 1) * P], identb[:, :], start=True, stop=True)
                last.then_inc(a_mn, 1)

            def step(b, what):
                a, c, t = b.plus(1), b.plus(2), b.plus(-1)
                if "B" in what:
                    pe.wait_ge(a_mr[b.slot], 32 * (b.round + 1))
                    pe.wait_ge(a_va, b.index + 1)
                for h in range(NH + 2):
                    B, A = "B" in what, "A" in what and 4 <= h < 12
                    if A and h == 4:
                        pe.wait_ge(a_stk[a.slot], STK * (a.round + 1))
                        pe.wait_ge(a_mnc, a.index + 1)
                        if a.k == 0:
                            pe.wait_ge(a_cdma, 8 * 16)
                    for m in range(AH + 1):
                        if B and h < NH and m < AH:
                            scores(b, h, m)
                        if A and m < AH:
                            max_scores(a, 8 * (h - 4) + 2 * m)
                        if B and 1 <= h <= NH and m >= 1:
                            sums(b, h - 1, m - 1)
                        if B and h >= 2 and m == AH - 1:
                            turn_sums(b, h - 2)
                        if A and m < AH:
                            max_scores(a, 8 * (h - 4) + 2 * m + 1)
                    if "T" in what:
                        {1: tail_p, 2: tail_k, 10: tail_a, 11: tail_o}.get(h, lambda t: None)(t)
                    if "P" in what:
                        if h == 8:
                            turn_rows(c, t if "T" in what else None)
                        if h == 13:
                            project(c, a if "A" in what else None)
                        if h in (15, 16):
                            project_rows(c, 2 * h - 30)
                            project_rows(c, 2 * h - 29)
                        if h == 16:
                            block_scores(c)
                        if h == 17:
                            turn_mask(c)
                    if h == 14 and "A" in what:
                        max_turn(a)

            normalise(0, 0)
            normalise(0, 1)
            shared(0, EARLY[0])
            experts(0, 0)
            experts(0, 1)
            pe.wait_ge(e_yc, CH * GR)
            for rounds, _, part in steps():
                if rounds is None:
                    for k, what in part:
                        step(Batch(k), what)
                else:
                    with pe.Fori(0, rounds) as i:
                        for k, what in part:
                            step(Batch(k, i), what)
            normalise(1, 0)
            normalise(1, 1)
            shared(1, EARLY[1])
            experts(1, 0)
            experts(1, 1)
            pe.wait_ge(e_yc, 2 * CH * GR)
            shared(1, LATE)


PER_DVE = 22


def kernel(**inputs):
    import numpy as np
    import concourse.bacc as bacc
    from concourse.bass_utils import run_bass_kernel_spmd

    def lay(a):
        return np.ascontiguousarray(a)

    g = {k.replace("L0_", ""): np.asarray(v) for k, v in inputs.items()}
    arrays = {
        "x": lay(g["attn_x"].reshape(-1, P, D)),
        "wqkv": lay(np.concatenate([g["attn_wq"].T, g["attn_wk"].T, g["attn_wv"].T], axis=1)),
        "wo": lay(g["attn_wo"].T),
        "rw": lay(g["ffn_router_w"].T),
        "rb": lay(g["ffn_router_bias"]),
        "wgu": lay(np.concatenate([g["ffn_gate_w"].transpose(2, 0, 1), g["ffn_up_w"].transpose(2, 0, 1)],
                                  axis=2).reshape(D, E * 2 * H)),
        "wd": lay(g["ffn_down_w"].transpose(2, 0, 1).reshape(H, E * D)),
        "sg": lay(g["ffn_sgate_w"].T),
        "su": lay(g["ffn_sup_w"].T),
        "sd": lay(g["ffn_sdown_w"].T.reshape(4, P, D).transpose(1, 0, 2)),
    }
    nc = bacc.Bacc("TRN2", target_bir_lowering=False, num_devices=1)
    aps = [nc.dram_tensor(n, a.shape, FP32, kind="ExternalInput").ap() for n, a in arrays.items()]
    out = nc.dram_tensor("out", arrays["x"].shape, FP32, kind="ExternalOutput").ap()
    nc.disable_value_cache = True
    build(nc, *aps, out)
    r = run_bass_kernel_spmd(nc, [arrays], core_ids=[0])
    return r.results[0]["out"].reshape(g["attn_x"].shape)
```
